# Optimizing a Trainium2 kernel written in Bass

```python
import numpy as np
import jax
import jax.numpy as jnp

def _softmax(x, axis=-1):
    return jax.nn.softmax(x, axis=axis)

def _gelu(x):
    return jax.nn.gelu(x, approximate=True)

def _silu(x):
    return jax.nn.silu(x)

def _sigmoid(x):
    return jax.nn.sigmoid(x)

def _layernorm(x, axis=-1, eps=1e-05):
    m = jnp.mean(x, axis=axis, keepdims=True)
    v = jnp.var(x, axis=axis, keepdims=True)
    return (x - m) / jnp.sqrt(v + eps)

def _scatter_add(tgt, idx, src, axis=0):
    return tgt.at[idx].add(src)

def _segment_sum(src, seg, n):
    return jax.ops.segment_sum(src, seg, n)
kernel_name = 'mk_lm_tower_d1_tok_ids1024_r4_e0b660'

def setup_inputs(seed: int=0):
    np.random.seed(seed)
    _w = jnp.asarray

    def _rec_inputs():
        import jax
        import jax.numpy as jnp
        _rk = jax.random.key(seed)
        x = jax.random.randint(jax.random.fold_in(_rk, 1), (16, 256), 0, 31993, jnp.int32)
        return x
    x = _rec_inputs()

    def _L0_tok_setup():
        import jax, jax.numpy as jnp
        import numpy as np
        EPS = 1e-05

        def layernorm(x, s, b):
            m = jnp.mean(x, axis=-1, keepdims=True)
            v = jnp.mean(jnp.square(x - m), axis=-1, keepdims=True)
            return (x - m) * jax.lax.rsqrt(v + EPS) * s + b

        def ssm(x, a_diag, Bm, Cm, Dm):
            a = jax.nn.sigmoid(a_diag)
            u = jnp.einsum('btd,ds->bts', x, Bm)

            def step(h, u_t):
                h = a * h + u_t
                return (h, h)
            h0 = jnp.zeros((x.shape[0], a.shape[0]), x.dtype)
            _, H = jax.lax.scan(step, h0, jnp.swapaxes(u, 0, 1))
            H = jnp.swapaxes(H, 0, 1)
            return jnp.einsum('bts,sd->btd', H, Cm) + jnp.einsum('btd,de->bte', x, Dm)
        key = jax.random.key(seed)
        ks = jax.random.split(key, 12)
        Bn, T = (4, 512)
        V, Dm, S, L, F = (8000, 256, 64, 4, 1024)

        def xavier(k, shape):
            fan_in, fan_out = (shape[-2], shape[-1])
            lim = float(np.sqrt(6.0 / (fan_in + fan_out)))
            return jax.random.uniform(k, shape, jnp.float32, -lim, lim)
        return {'tokens': jax.random.randint(ks[0], (Bn, T), 0, V), 'emb': jax.random.normal(ks[1], (V, Dm), jnp.float32), 'pos_emb': jax.random.normal(ks[2], (1024, Dm), jnp.float32), 'A_diag': jax.random.uniform(ks[3], (L, S), jnp.float32, -0.5, 0.5), 'B': xavier(ks[4], (L, Dm, S)), 'C': xavier(ks[5], (L, S, Dm)), 'D': xavier(ks[6], (L, Dm, Dm)) * 0.1, 'w1': xavier(ks[7], (L, Dm, F)), 'b1': jnp.zeros((L, F), jnp.float32), 'w2': xavier(ks[8], (L, F, Dm)), 'b2': jnp.zeros((L, Dm), jnp.float32), 'ln1_s': jnp.ones((L, Dm), jnp.float32), 'ln1_b': jnp.zeros((L, Dm), jnp.float32), 'ln2_s': jnp.ones((L, Dm), jnp.float32), 'ln2_b': jnp.zeros((L, Dm), jnp.float32), 'lnf_s': jnp.ones((Dm,), jnp.float32), 'lnf_b': jnp.zeros((Dm,), jnp.float32)}
    _L0_tok_all = _L0_tok_setup()
    _L0_tok_in = {k: v for k, v in _L0_tok_all.items() if k in ('emb', 'pos_emb', 'A_diag', 'B', 'C', 'D', 'w1', 'b1', 'w2', 'b2', 'ln1_s', 'ln1_b', 'ln2_s', 'ln2_b', 'lnf_s', 'lnf_b')}
    del _L0_tok_all

    def _L0_attn_setup():
        import jax, jax.numpy as jnp
        import numpy as np
        DIM_EMB = 256
        NUM_HEADS = 16
        DIM_HEAD = DIM_EMB // NUM_HEADS
        key = jax.random.key(seed)
        k1, k2, k3 = jax.random.split(key, 3)
        x = jax.random.normal(k1, (4, 512, DIM_EMB), dtype=jnp.float32)
        w_qkv = jax.random.normal(k2, (3 * NUM_HEADS * DIM_HEAD, DIM_EMB), dtype=jnp.float32) * DIM_EMB ** (-0.5)
        w_out = jax.random.normal(k3, (DIM_EMB, NUM_HEADS * DIM_HEAD), dtype=jnp.float32) * (NUM_HEADS * DIM_HEAD) ** (-0.5)
        return {'x': x, 'w_qkv': w_qkv, 'w_out': w_out}
    _L0_attn_all = _L0_attn_setup()
    _L0_attn_in = {k: v for k, v in _L0_attn_all.items() if k in ('w_qkv', 'w_out')}
    del _L0_attn_all

    def _L0_ffn_setup():
        import jax, jax.numpy as jnp
        import numpy as np
        NUM_EXPERTS = 8
        NUM_LANGS = 4
        TOP_K = 2
        D_MODEL = 256
        EXPERT_SIZE = 1024
        B, S = (2, 512)
        key = jax.random.key(seed)
        ks = jax.random.split(key, 6)

        def xavier(k, shape, fan_in, fan_out):
            a = float(np.sqrt(6.0 / (fan_in + fan_out)))
            return jax.random.uniform(k, shape, jnp.float32, -a, a)
        return {'x': jax.random.normal(ks[0], (B, S, D_MODEL), jnp.float32), 'router_w': xavier(ks[1], (NUM_EXPERTS, D_MODEL), D_MODEL, NUM_EXPERTS), 'router_b': jnp.zeros((NUM_EXPERTS,), jnp.float32), 'lang_w': xavier(ks[2], (NUM_LANGS, D_MODEL), D_MODEL, NUM_LANGS), 'lang_b': jnp.zeros((NUM_LANGS,), jnp.float32), 'w1': xavier(ks[3], (NUM_EXPERTS, D_MODEL, EXPERT_SIZE), D_MODEL, EXPERT_SIZE), 'b1': jnp.zeros((NUM_EXPERTS, EXPERT_SIZE), jnp.float32), 'w2': xavier(ks[4], (NUM_EXPERTS, EXPERT_SIZE, D_MODEL), EXPERT_SIZE, D_MODEL), 'b2': jnp.zeros((NUM_EXPERTS, D_MODEL), jnp.float32)}
    _L0_ffn_all = _L0_ffn_setup()
    _L0_ffn_in = {k: v for k, v in _L0_ffn_all.items() if k in ('router_w', 'router_b', 'lang_w', 'lang_b', 'w1', 'b1', 'w2', 'b2')}
    del _L0_ffn_all
    return {'x': x, 'L0_tok_emb': _L0_tok_in['emb'], 'L0_tok_pos_emb': _L0_tok_in['pos_emb'], 'L0_tok_A_diag': _L0_tok_in['A_diag'], 'L0_tok_B': _L0_tok_in['B'], 'L0_tok_C': _L0_tok_in['C'], 'L0_tok_D': _L0_tok_in['D'], 'L0_tok_w1': _L0_tok_in['w1'], 'L0_tok_b1': _L0_tok_in['b1'], 'L0_tok_w2': _L0_tok_in['w2'], 'L0_tok_b2': _L0_tok_in['b2'], 'L0_tok_ln1_s': _L0_tok_in['ln1_s'], 'L0_tok_ln1_b': _L0_tok_in['ln1_b'], 'L0_tok_ln2_s': _L0_tok_in['ln2_s'], 'L0_tok_ln2_b': _L0_tok_in['ln2_b'], 'L0_tok_lnf_s': _L0_tok_in['lnf_s'], 'L0_tok_lnf_b': _L0_tok_in['lnf_b'], 'L0_attn_w_qkv': _L0_attn_in['w_qkv'], 'L0_attn_w_out': _L0_attn_in['w_out'], 'L0_ffn_router_w': _L0_ffn_in['router_w'], 'L0_ffn_router_b': _L0_ffn_in['router_b'], 'L0_ffn_lang_w': _L0_ffn_in['lang_w'], 'L0_ffn_lang_b': _L0_ffn_in['lang_b'], 'L0_ffn_w1': _L0_ffn_in['w1'], 'L0_ffn_b1': _L0_ffn_in['b1'], 'L0_ffn_w2': _L0_ffn_in['w2'], 'L0_ffn_b2': _L0_ffn_in['b2']}

def reference(x, L0_tok_emb, L0_tok_pos_emb, L0_tok_A_diag, L0_tok_B, L0_tok_C, L0_tok_D, L0_tok_w1, L0_tok_b1, L0_tok_w2, L0_tok_b2, L0_tok_ln1_s, L0_tok_ln1_b, L0_tok_ln2_s, L0_tok_ln2_b, L0_tok_lnf_s, L0_tok_lnf_b, L0_attn_w_qkv, L0_attn_w_out, L0_ffn_router_w, L0_ffn_router_b, L0_ffn_lang_w, L0_ffn_lang_b, L0_ffn_w1, L0_ffn_b1, L0_ffn_w2, L0_ffn_b2):
    import jax
    import jax.numpy as jnp

    def _L0_tok_ref(tokens, emb, pos_emb, A_diag, B, C, D, w1, b1, w2, b2, ln1_s, ln1_b, ln2_s, ln2_b, lnf_s, lnf_b):
        import jax, jax.numpy as jnp
        import numpy as np
        EPS = 1e-05

        def layernorm(x, s, b):
            m = jnp.mean(x, axis=-1, keepdims=True)
            v = jnp.mean(jnp.square(x - m), axis=-1, keepdims=True)
            return (x - m) * jax.lax.rsqrt(v + EPS) * s + b

        def ssm(x, a_diag, Bm, Cm, Dm):
            a = jax.nn.sigmoid(a_diag)
            u = jnp.einsum('btd,ds->bts', x, Bm)

            def step(h, u_t):
                h = a * h + u_t
                return (h, h)
            h0 = jnp.zeros((x.shape[0], a.shape[0]), x.dtype)
            _, H = jax.lax.scan(step, h0, jnp.swapaxes(u, 0, 1))
            H = jnp.swapaxes(H, 0, 1)
            return jnp.einsum('bts,sd->btd', H, Cm) + jnp.einsum('btd,de->bte', x, Dm)
        T = tokens.shape[1]
        x = emb[tokens] + pos_emb[:T][None]
        L = A_diag.shape[0]
        for l in range(L):
            x = x + ssm(layernorm(x, ln1_s[l], ln1_b[l]), A_diag[l], B[l], C[l], D[l])
            h = layernorm(x, ln2_s[l], ln2_b[l])
            h = jax.nn.gelu(jnp.einsum('btd,df->btf', h, w1[l]) + b1[l], approximate=False)
            x = x + jnp.einsum('btf,fd->btd', h, w2[l]) + b2[l]
        return layernorm(x, lnf_s, lnf_b)

    def _L0_attn_ref(x, w_qkv, w_out):
        import jax, jax.numpy as jnp
        import numpy as np
        DIM_EMB = 256
        NUM_HEADS = 16
        DIM_HEAD = DIM_EMB // NUM_HEADS
        b, t, _ = x.shape
        scale = DIM_HEAD ** (-0.5)
        qkv = jnp.einsum('bte,fe->btf', x, w_qkv)
        qkv = qkv.reshape(b, t, 3, NUM_HEADS, DIM_HEAD)
        q, k, v = (qkv[:, :, 0], qkv[:, :, 1], qkv[:, :, 2])
        scores = jnp.einsum('bihd,bjhd->bhij', q, k) * scale
        weights = jax.nn.softmax(scores, axis=-1)
        attn = jnp.einsum('bhij,bjhd->bhid', weights, v)
        concat = attn.transpose(0, 2, 1, 3).reshape(b, t, NUM_HEADS * DIM_HEAD)
        return jnp.einsum('btf,ef->bte', concat, w_out)

    def _L0_ffn_ref(x, router_w, router_b, lang_w, lang_b, w1, b1, w2, b2):
        import jax, jax.numpy as jnp
        import numpy as np
        NUM_EXPERTS = 8
        NUM_LANGS = 4
        TOP_K = 2
        D_MODEL = 256
        EXPERT_SIZE = 1024
        B, S = (2, 512)
        lang_logits = x @ lang_w.T + lang_b
        lang_probs = jax.nn.softmax(lang_logits, axis=-1)
        lp_pad = jnp.pad(lang_probs, ((0, 0), (0, 0), (0, 1)))
        idx = jnp.arange(NUM_EXPERTS) % NUM_LANGS
        expert_weights = lp_pad[..., idx] + lp_pad[..., idx + 1]
        router_logits = x @ router_w.T + router_b + 0.1 * expert_weights
        router_probs = jax.nn.softmax(router_logits, axis=-1)
        top_p, top_i = jax.lax.top_k(router_probs, TOP_K)
        top_p = top_p / top_p.sum(axis=-1, keepdims=True)
        h = jax.nn.gelu(jnp.einsum('bsd,edh->bseh', x, w1) + b1, approximate=False)
        expert_out = jnp.einsum('bseh,ehd->bsed', h, w2) + b2
        sel = jnp.take_along_axis(expert_out, top_i[..., None], axis=2)
        return (top_p[..., None] * sel).sum(axis=2)
    h = _L0_tok_ref(x, L0_tok_emb, L0_tok_pos_emb, L0_tok_A_diag, L0_tok_B, L0_tok_C, L0_tok_D, L0_tok_w1, L0_tok_b1, L0_tok_w2, L0_tok_b2, L0_tok_ln1_s, L0_tok_ln1_b, L0_tok_ln2_s, L0_tok_ln2_b, L0_tok_lnf_s, L0_tok_lnf_b)
    h = h + _L0_attn_ref(_layernorm(h, axis=-1), L0_attn_w_qkv, L0_attn_w_out)
    h = h + _L0_ffn_ref(_layernorm(h, axis=-1), L0_ffn_router_w, L0_ffn_router_b, L0_ffn_lang_w, L0_ffn_lang_b, L0_ffn_w1, L0_ffn_b1, L0_ffn_w2, L0_ffn_b2)
    return h

_drawn_inputs = setup_inputs


def setup_inputs(seed=0):
    import zlib

    import numpy as np

    out = dict(_drawn_inputs(seed))
    spreads = {'L0_tok_b1': (0.0, 0.1),
     'L0_tok_b2': (0.0, 0.1),
     'L0_tok_ln1_s': (1.0, 0.2),
     'L0_tok_ln1_b': (0.0, 0.1),
     'L0_tok_ln2_s': (1.0, 0.2),
     'L0_tok_ln2_b': (0.0, 0.1),
     'L0_tok_lnf_s': (1.0, 0.2),
     'L0_tok_lnf_b': (0.0, 0.1),
     'L0_ffn_router_b': (0.0, 0.1),
     'L0_ffn_lang_b': (0.0, 0.1),
     'L0_ffn_b1': (0.0, 0.1),
     'L0_ffn_b2': (0.0, 0.1)}
    factors = {}
    for name, (base, spread) in spreads.items():
        noise = np.random.default_rng([zlib.crc32(name.encode()), seed]).standard_normal(out[name].shape)
        drawn = base * np.exp(spread * noise) if base else spread * noise
        out[name] = jnp.asarray(drawn.astype(out[name].dtype))
    for name, factor in factors.items():
        out[name] = (out[name] * factor).astype(out[name].dtype)
    return out
```

```python
from contextlib import ExitStack

import concourse.bass as bass
from concourse import mybir

P = 128
ALU = mybir.AluOpType
ACT = mybir.ActivationFunctionType
AX = mybir.AxisListType
F32 = mybir.dt.float32
F32R = mybir.dt.float32r
I32 = mybir.dt.int32
U32 = mybir.dt.uint32

SEQS, T = 16, 256
N = SEQS * T
TILES = N // P
D = 256
KD = D // P
LAYERS, S, F = 4, 64, 1024
FC = F // P
G = 4
GROUPS = TILES // G
GT = G * P
HEADS, DH = 16, 16
EXPERTS, LANGS = 8, 4
EPS = 1e-5
BLOCKS = 2 * N // P + EXPERTS
ds = bass.ds


ONE = 1


def start_at_one(nc, sems):
    with nc.Block() as block:
        @block.sync
        def _(sp):
            for s in sems:
                sp.sem_inc(s, ONE)


def wait_apart(eng, started, sem, value):
    value = value if isinstance(value, int) else eng.compute_val(value)
    eng.wait_ge(started, 1)
    eng.wait_ge(sem, value)


def embed(nc, started, x_res, emb, pos, tokens):
    vocab = emb.shape[0]
    with ExitStack() as ctx:
        def sb(name, shape, dt):
            return ctx.enter_context(nc.sbuf_tensor(name, shape, dt))

        def sem(name):
            return ctx.enter_context(nc.semaphore(name))

        tok_i = sb("tok_i", [P, TILES], I32)
        tok_f = sb("tok_f", [P, TILES], F32)
        wrap = sb("wrap", [P, TILES], F32)
        wrapped = sb("wrapped", [P, TILES], F32)
        row = sb("row", [P, TILES], U32)
        pos_sb = sb("pos_sb", [P, T // P, D], F32)
        tokens_in, pos_in, idx_step, gathered, added = map(
            sem, ("tokens_in", "pos_in", "idx_step", "gathered", "pos_added"))

        block = ctx.enter_context(nc.Block())

        @block.sync
        def _(sp):
            sp.dma_start(tok_i[:], tokens).then_inc(tokens_in, 16)
            sp.dma_start(pos_sb[:], pos[0:T, :].rearrange("(j p) d -> p j d", p=P)).then_inc(pos_in, 16)

        @block.gpsimd
        def _(pool):
            pool.wait_ge(idx_step, 4)
            for t in range(TILES):
                pool.indirect_dma_start(
                    out=x_res[:, t, :], out_offset=None, in_=emb,
                    in_offset=bass.IndirectOffsetOnAxis(ap=row[:, t:t + 1], axis=0),
                ).then_inc(gathered, 16)

        @block.vector
        def _(dve):
            dve.wait_ge(tokens_in, 16)
            dve.tensor_copy(tok_f[:], tok_i[:]).then_inc(idx_step, 1)
            dve.wait_ge(idx_step, 1)
            dve.tensor_scalar(wrap[:], tok_f[:], 0.0, float(vocab), ALU.is_lt, ALU.mult).then_inc(idx_step, 1)
            dve.wait_ge(idx_step, 2)
            dve.tensor_tensor(wrapped[:], tok_f[:], wrap[:], ALU.add).then_inc(idx_step, 1)
            dve.wait_ge(idx_step, 3)
            dve.tensor_scalar(row[:], wrapped[:], 0.0, float(vocab - 1), ALU.max, ALU.min).then_inc(idx_step, 1)
            dve.wait_ge(pos_in, 16)
            dve.wait_ge(gathered, 16 * TILES)
            for t in range(0, TILES, T // P):
                dve.tensor_tensor(x_res[:, t:t + T // P, :], x_res[:, t:t + T // P, :], pos_sb[:],
                                  ALU.add).then_inc(added, 1)
            dve.wait_ge(added, TILES * P // T)


def tower(nc, started, x_res, ident, neg_half, w):
    with ExitStack() as ctx:
        def sb(name, shape, dt=F32):
            return ctx.enter_context(nc.sbuf_tensor(name, shape, dt))

        def psum(name):
            return ctx.enter_context(nc.psum_tensor(name, [P, 512], F32))

        sems = []

        def sem(name):
            sems.append(ctx.enter_context(nc.semaphore(name)))
            return sems[-1]

        b_all = sb("b_all", [P, LAYERS, KD, S])
        b_now = sb("b_now", [P, KD, S])
        c_now = sb("c_now", [P, D])
        d_now = sb("d_now", [P, KD, D])
        c_all = sb("c_all", [P, LAYERS, D])
        d_all = sb("d_all", [P, LAYERS, KD, D])
        a_raw = sb("a_raw", [P, LAYERS])
        decay = sb("decay", [P, LAYERS])
        decay_row = sb("decay_row", [P, LAYERS, T])
        b1_all = sb("b1_all", [P, LAYERS, FC])
        b2_all = sb("b2_all", [P, LAYERS, D])
        ln_par = sb("ln_par", [P, 4, LAYERS, KD])
        w1_raw = sb("w1_raw", [P, KD, F])
        w2_raw = sb("w2_raw", [P, FC, D])
        w1_hi, w1_lo = sb("w1_hi", [P, KD, F], F32R), sb("w1_lo", [P, KD, F], F32R)
        w2_hi, w2_lo = sb("w2_hi", [P, FC, D], F32R), sb("w2_lo", [P, FC, D], F32R)
        lnf_s, lnf_b = sb("lnf_s", [P, D]), sb("lnf_b", [P, D])
        stats = [sb(f"stats{i}", [P, G, 6]) for i in range(2)]
        mv = [sb(f"mean_var{i}", [P, G, 2]) for i in range(2)]
        vare = [sb(f"var_eps{i}", [P, G]) for i in range(2)]
        rstd = [sb(f"rstd{i}", [P, G]) for i in range(2)]
        xn = [sb(f"xn{i}", [P, G, D]) for i in range(2)]
        x1T = sb("x1T", [P, KD, GT])
        states = sb("states", [P, T])
        x2T = sb("x2T", [P, KD, GT])
        x2T_hi, x2T_lo = sb("x2T_hi", [P, KD, GT], F32R), sb("x2T_lo", [P, KD, GT], F32R)
        HB = 4
        hT = sb("hT", [P, HB, GT])
        hT_hi, hT_lo = sb("hT_hi", [P, HB, GT], F32R), sb("hT_lo", [P, HB, GT], F32R)
        ps_t = [psum(f"ps_t{i}") for i in range(2)]
        ps_y = [psum(f"ps_y{i}") for i in range(2)]
        ps_h = [psum(f"ps_h{i}") for i in range(HB)]

        small_in, a_in, w1_in, w2_in = map(sem, ("small_in", "a_in", "w1_in", "w2_in"))
        decay_done, decay_ready = sem("decay_done"), sem("decay_ready")
        w1_hi_done, w1_split, w2_hi_done, w2_split, ssm_w_ready = map(
            sem, ("w1_hi_done", "w1_split", "w2_hi_done", "w2_split", "ssm_w_ready"))
        stat_done = [sem(f"stat_done{i}") for i in range(2)]
        aggr_done = [sem(f"aggr_done{i}") for i in range(2)]
        vare_done = [sem(f"vare_done{i}") for i in range(2)]
        rstd_done = [sem(f"rstd_done{i}") for i in range(2)]
        xn_done = [sem(f"xn_done{i}") for i in range(2)]
        t_done = [sem(f"t_done{i}") for i in range(2)]
        x1_ready, u_done, scan_done, y_done, res1_done = map(
            sem, ("x1_ready", "u_done", "scan_done", "y_done", "res1_done"))
        b2_added, x2_evac, x2_lo_done = map(sem, ("b2_added", "x2_evac", "x2_lo_done"))
        h_done, gelu_done, h_lo_done, f_done, res2_done = map(
            sem, ("h_done", "gelu_done", "h_lo_done", "f_done", "res2_done"))
        lnf_in, fin = sem("lnf_in"), sem("final_ln")

        start_at_one(nc, sems)
        block = ctx.enter_context(nc.Block())

        @block.sync
        def _(sp):
            sp.dma_start(a_raw[:], w["A_diag"]).then_inc(a_in, 16)
            small = [(b_all[:, l], w["B"][l].rearrange("(k p) s -> p k s", p=P)) for l in range(LAYERS)]
            small += [(c_all[64 * h:64 * h + 64, :, :], w["C"].rearrange("l s d -> s l d")) for h in range(2)]
            small += [(d_all[:, l], w["D"][l].rearrange("(k p) e -> p k e", p=P)) for l in range(LAYERS)]
            small += [(b1_all[:], w["b1"]), (ln_par[:], w["ln_par"]),
                      (b2_all[:], w["b2"].rearrange("(o l) d -> o l d", o=1).to_broadcast([P, LAYERS, D]))]
            for dst, src in small:
                sp.dma_start(dst, src).then_inc(small_in, 16)
            with sp.Fori(0, LAYERS) as l:
                sp.wait_ge(w1_split, ONE + l)
                sp.dma_start(w1_raw[:], w["w1"][ds(l, 1)].rearrange("o (k p) f -> p (o k) f", p=P)).then_inc(w1_in, 16)
                sp.wait_ge(w2_split, ONE + l)
                sp.dma_start(w2_raw[:], w["w2"][ds(l, 1)].rearrange("o (c p) d -> p (o c) d", p=P)).then_inc(w2_in, 16)
            for dst, name in ((lnf_s, "lnf_s"), (lnf_b, "lnf_b")):
                sp.dma_start(dst[:], w[name].rearrange("(o d) -> o d", o=1).to_broadcast([P, D])).then_inc(lnf_in, 16)

        SMALL = 16 * (LAYERS * 2 + 2 + 3)

        @block.tensor
        def _(pe):
            def turn(i, n):
                pe.wait_ge(xn_done[i], ONE + G * (n + 1))
                for k in range(KD):
                    for j in range(G):
                        last = pe.transpose(ps_t[k][:, P * j:P * j + P], xn[i][:, j, P * k:P * k + P], ident)
                last.then_inc(t_done[i], 1)

            def turn1(n):
                pe.wait_ge(x2_evac, ONE + 4 * n)
                turn(0, n)

            def drive(n):
                pe.wait_ge(x1_ready, ONE + 2 * (n + 1))
                for q in range(2):
                    for k in range(KD):
                        last = pe.matmul(ps_t[0][S * q:S * q + S, 0:T], b_now[:, k, :],
                                         x1T[:, k, T * q:T * q + T], start=(k == 0), stop=(k == KD - 1))
                last.then_inc(u_done, 1)

            def ssm_out(n):
                pe.wait_ge(scan_done, ONE + n + 1)
                for j in range(G):
                    out = ps_t[j // 2][:, D * (j % 2):D * (j % 2) + D]
                    q, i0 = j // 2, P * (j % 2)
                    for k in range(KD):
                        pe.matmul(out, x1T[:, k, P * j:P * j + P], d_now[:, k, :], start=(k == 0), stop=False)
                    last = pe.matmul(out, states[S * q:S * q + S, i0:i0 + P],
                                     c_now[S * q:S * q + S, :], start=False, stop=True)
                last.then_inc(y_done, 1)

            def turn2(n):
                pe.wait_ge(res1_done, ONE + 2 * (n + 1))
                turn(1, n)

            def up(n, c):
                if c == 0:
                    pe.wait_ge(x2_lo_done, ONE + KD * (n + 1))
                passes = [(w1_hi, x2T_hi), (w1_hi, x2T_lo), (w1_lo, x2T_hi)]
                for k in range(KD):
                    for i, (a, b) in enumerate(passes):
                        last = pe.matmul(ps_h[c % HB][:], a[:, k, P * c:P * c + P], b[:, k, :],
                                         start=(k == 0 and i == 0), stop=(k == KD - 1 and i == 2))
                last.then_inc(h_done, 1)

            def down(n, c):
                if c == 0:
                    pe.wait_ge(res2_done, ONE + 2 * n)
                pe.wait_ge(h_lo_done, ONE + FC * n + c + 1)
                for j in range(G):
                    out = ps_y[j // 2][:, D * (j % 2):D * (j % 2) + D]
                    tok = slice(P * j, P * j + P)
                    for i, (a, b) in enumerate([(hT_hi, w2_hi), (hT_hi, w2_lo), (hT_lo, w2_hi)]):
                        last = pe.matmul(out, a[:, c % HB, tok], b[:, c, :],
                                         start=(c == 0 and i == 0 and j % 2 == 0), stop=(c == FC - 1 and i == 2),
                                         skip_group_check=True)
                if c == FC - 1:
                    last.then_inc(f_done, 1)

            def step(n, ssm_next):
                up(n, 0)
                up(n, 1)
                if ssm_next:
                    turn1(n + 1)
                down(n, 0)
                up(n, 2)
                if ssm_next:
                    drive(n + 1)
                down(n, 1)
                up(n, 3)
                down(n, 2)
                if ssm_next:
                    ssm_out(n + 1)
                up(n, 4)
                down(n, 3)
                up(n, 5)
                down(n, 4)
                up(n, 6)
                if ssm_next:
                    turn2(n + 1)
                down(n, 5)
                up(n, 7)
                down(n, 6)
                down(n, 7)

            pe.wait_ge(small_in, ONE + SMALL)
            with pe.Fori(0, LAYERS) as l:
                first = GROUPS * l
                turn1(first)
                pe.wait_ge(ssm_w_ready, ONE + 3 * (l + 1))
                drive(first)
                ssm_out(first)
                turn2(first)
                wait_apart(pe, started, w1_split, ONE + l + 1)
                wait_apart(pe, started, w2_split, ONE + l + 1)
                with pe.Fori(0, GROUPS - 1) as g:
                    step(GROUPS * l + g, True)
                step(GROUPS * l + GROUPS - 1, False)

        @block.vector
        def _(dve):
            def group(n0, j=0, count=G):
                return x_res[:, ds(G * n0 + j, count), :]

            def statistics(i, n, g):
                for j in range(G):
                    dve.bn_stats(stats[i][:, j, :], x_res[:, ds(G * g + j, 1), :]).then_inc(stat_done[i], 1)
                wait_apart(dve, started, stat_done[i], ONE + G * (n + 1))
                for j in range(G):
                    dve.bn_aggr(mv[i][:, j, :], stats[i][:, j, :]).then_inc(aggr_done[i], 1)
                dve.wait_ge(aggr_done[i], ONE + G * (n + 1))
                dve.wait_ge(rstd_done[i], ONE + n)
                dve.tensor_scalar(vare[i][:], mv[i][:, :, 1], EPS, None, ALU.add).then_inc(vare_done[i], 1)

            def normalise(i, n, g):
                dve.wait_ge(rstd_done[i], ONE + n + 1)
                dve.wait_ge(t_done[i], ONE + n)
                for j in range(G):
                    dve.tensor_scalar(xn[i][:, j, :], x_res[:, ds(G * g + j, 1), :].rearrange("p o d -> p (o d)"),
                                      mv[i][:, j, 0:1], rstd[i][:, j:j + 1], ALU.subtract, ALU.mult)\
                       .then_inc(xn_done[i], 1)

            def scan(n, l):
                dve.wait_ge(u_done, ONE + n + 1)
                dve.wait_ge(y_done, ONE + n)
                dve.tensor_tensor_scan(states[:], decay_row[:, ds(l, 1), :].rearrange("p o t -> p (o t)"),
                                       ps_t[0][:, 0:T], 0.0, ALU.mult, ALU.add).then_inc(scan_done, 1)

            def add_pair(ps, done, g):
                for h in range(2):
                    pair = x_res[:, ds(G * g + 2 * h, 2), :]
                    dve.tensor_tensor(pair, ps[h][:].rearrange("p (j d) -> p j d", j=2), pair, ALU.add)\
                       .then_inc(done, 1)

            def residual1(n, g):
                dve.wait_ge(y_done, ONE + n + 1)
                add_pair(ps_t, res1_done, g)
                wait_apart(dve, started, res1_done, ONE + 2 * (n + 1))
                statistics(1, n, g)

            def x2_rest(n):
                dve.wait_ge(h_done, ONE + FC * n)
                for k in range(KD):
                    dve.wait_ge(x2_evac, ONE + 4 * n + 2 * (k + 1))
                    dve.tensor_tensor(x2T_lo[:, k, :], x2T[:, k, :], x2T_hi[:, k, :].bitcast(F32), ALU.subtract)\
                       .then_inc(x2_lo_done, 1)

            def h_rest(n, c):
                b = c % HB
                dve.wait_ge(gelu_done, ONE + 2 * (FC * n + c + 1))
                dve.tensor_tensor(hT_lo[:, b, :], hT[:, b, :], hT_hi[:, b, :].bitcast(F32), ALU.subtract)\
                   .then_inc(h_lo_done, 1)

            def residual2(n, g):
                dve.wait_ge(f_done, ONE + n + 1)
                dve.wait_ge(b2_added, ONE + n + 1)
                add_pair(ps_y, res2_done, g)

            def step(n, l, g, ssm_next):
                if ssm_next:
                    wait_apart(dve, started, res2_done, ONE + 2 * n)
                    statistics(0, n + 1, g + 1)
                h_rest(n, 0)
                if ssm_next:
                    normalise(0, n + 1, g + 1)
                h_rest(n, 1)
                if ssm_next:
                    scan(n + 1, l)
                h_rest(n, 2)
                h_rest(n, 3)
                if ssm_next:
                    residual1(n + 1, g + 1)
                h_rest(n, 4)
                if ssm_next:
                    normalise(1, n + 1, g + 1)
                h_rest(n, 5)
                h_rest(n, 6)
                h_rest(n, 7)
                if ssm_next:
                    x2_rest(n + 1)
                residual2(n, g)

            dve.memset(decay_row[:], 1.0).then_inc(decay_ready, 1)
            dve.wait_ge(decay_done, ONE + 1)
            dve.wait_ge(decay_ready, ONE + 1)
            for l in range(LAYERS):
                dve.tensor_scalar(decay_row[:, l, :], decay_row[:, l, :], decay[:, l:l + 1], None, ALU.mult)\
                   .then_inc(decay_ready, 1)
            dve.wait_ge(decay_ready, ONE + 1 + LAYERS)
            with dve.Fori(0, LAYERS) as l:
                first = GROUPS * l
                dve.wait_ge(res2_done, ONE + 2 * first)
                statistics(0, first, 0)
                dve.wait_ge(w1_in, ONE + 16 * (l + 1))
                dve.wait_ge(f_done, ONE + first)
                dve.tensor_copy(w1_hi[:], w1_raw[:]).then_inc(w1_hi_done, 1)
                normalise(0, first, 0)
                dve.wait_ge(w1_hi_done, ONE + l + 1)
                dve.tensor_tensor(w1_lo[:], w1_raw[:], w1_hi[:].bitcast(F32), ALU.subtract).then_inc(w1_split, 1)
                scan(first, l)
                residual1(first, 0)
                normalise(1, first, 0)
                x2_rest(first)
                with dve.Fori(0, GROUPS - 1) as g:
                    step(first + g, l, g, True)
                step(first + GROUPS - 1, l, GROUPS - 1, False)

            steps = LAYERS * GROUPS
            dve.wait_ge(lnf_in, ONE + 32)
            dve.wait_ge(res2_done, ONE + 2 * steps)
            with dve.Fori(0, GROUPS) as g:
                statistics(0, steps + g, g)
                dve.wait_ge(rstd_done[0], ONE + steps + g + 1)
                for j in range(G):
                    dve.tensor_scalar(xn[0][:, j, :], x_res[:, ds(G * g + j, 1), :].rearrange("p o d -> p (o d)"),
                                      mv[0][:, j, 0:1], rstd[0][:, j:j + 1], ALU.subtract, ALU.mult)\
                       .then_inc(xn_done[0], 1)
                dve.wait_ge(xn_done[0], ONE + G * (steps + g + 1))
                dve.tensor_tensor(xn[0][:], xn[0][:], lnf_s[:].unsqueeze(1).to_broadcast([P, G, D]), ALU.mult)\
                   .then_inc(fin, 1)
                dve.wait_ge(fin, ONE + 2 * g + 1)
                dve.tensor_tensor(x_res[:, ds(G * g, G), :], xn[0][:], lnf_b[:].unsqueeze(1).to_broadcast([P, G, D]),
                                  ALU.add).then_inc(fin, 1)
                dve.wait_ge(fin, ONE + 2 * g + 2)

        @block.scalar
        def _(act):
            def turned1(n, l):
                wait_apart(act, started, t_done[0], ONE + n + 1)
                wait_apart(act, started, y_done, ONE + n)
                for k in range(KD):
                    act.activation(x1T[:, k, :], ps_t[k][:], ACT.Identity, scale=ln_par[:, 0, ds(l, 1), k],
                                   bias=ln_par[:, 1, ds(l, 1), k]).then_inc(x1_ready, 1)

            def turned2(n, l):
                wait_apart(act, started, t_done[1], ONE + n + 1)
                wait_apart(act, started, x2_lo_done, ONE + KD * n)
                wait_apart(act, started, h_done, ONE + FC * n)
                for k in range(KD):
                    for dst in (x2T, x2T_hi):
                        act.activation(dst[:, k, :], ps_t[k][:], ACT.Identity, scale=ln_par[:, 2, ds(l, 1), k],
                                       bias=ln_par[:, 3, ds(l, 1), k]).then_inc(x2_evac, 1)

            def gelu(n, l, c):
                wait_apart(act, started, h_done, ONE + FC * n + c + 1)
                for dst in (hT, hT_hi):
                    act.activation(dst[:, c % HB, :], ps_h[c % HB][:], ACT.Gelu, bias=b1_all[:, ds(l, 1), c])\
                       .then_inc(gelu_done, 1)

            def step(n, l, ssm_next):
                gelu(n, l, 0)
                if ssm_next:
                    turned1(n + 1, l)
                for c in range(1, FC):
                    gelu(n, l, c)
                if ssm_next:
                    turned2(n + 1, l)

            act.wait_ge(a_in, ONE + 16)
            act.activation(decay[:], a_raw[:], ACT.Sigmoid).then_inc(decay_done, 1)
            act.wait_ge(small_in, ONE + SMALL)
            with act.Fori(0, LAYERS) as l:
                first = GROUPS * l
                turned1(first, l)
                act.wait_ge(w2_in, ONE + 16 * (l + 1))
                act.wait_ge(f_done, ONE + first)
                act.activation(w2_hi[:], w2_raw[:], ACT.Copy).then_inc(w2_hi_done, 1)
                turned2(first, l)
                with act.Fori(0, GROUPS - 1) as g:
                    step(first + g, l, True)
                step(first + GROUPS - 1, l, False)

        @block.gpsimd
        def _(pool):
            def root(i, n):
                pool.wait_ge(vare_done[i], ONE + n + 1)
                pool.wait_ge(xn_done[i], ONE + G * n)
                pool.tensor_tensor(rstd[i][:], vare[i][:], neg_half[:, 0:G], ALU.pow).then_inc(rstd_done[i], 1)

            def add_b2(n, l, g):
                pool.wait_ge(xn_done[1], ONE + G * (n + 1))
                part = x_res[:, ds(G * g, G), :]
                pool.tensor_tensor(part, part, b2_all[:, ds(l, 1), :].to_broadcast([P, G, D]), ALU.add)\
                    .then_inc(b2_added, 1)

            pool.wait_ge(small_in, ONE + SMALL)
            with pool.Fori(0, LAYERS) as l:
                first = GROUPS * l
                pool.wait_ge(y_done, ONE + first)
                pool.tensor_copy(b_now[:].unsqueeze(1), b_all[:, ds(l, 1)]).then_inc(ssm_w_ready, 1)
                pool.tensor_copy(c_now[:].unsqueeze(1), c_all[:, ds(l, 1)]).then_inc(ssm_w_ready, 1)
                pool.tensor_copy(d_now[:].unsqueeze(1), d_all[:, ds(l, 1)]).then_inc(ssm_w_ready, 1)
                root(0, first)
                root(1, first)
                add_b2(first, l, 0)
                pool.wait_ge(w2_hi_done, ONE + l + 1)
                pool.tensor_tensor(w2_lo[:], w2_raw[:], w2_hi[:].bitcast(F32), ALU.subtract).then_inc(w2_split, 1)
                with pool.Fori(0, GROUPS - 1) as g:
                    root(0, first + g + 1)
                    root(1, first + g + 1)
                    add_b2(first + g + 1, l, g + 1)
            with pool.Fori(0, GROUPS) as g:
                root(0, LAYERS * GROUPS + g)


def attention(nc, started, x_res, ident, neg_half, w):
    ST = T // P
    QUAD = 4
    DV = 32
    QUADS = HEADS // QUAD
    HC = HEADS * DH // P
    PER = P // DH
    with ExitStack() as ctx:
        def sb(name, shape, dt=F32):
            return ctx.enter_context(nc.sbuf_tensor(name, shape, dt))

        def psum(name):
            return ctx.enter_context(nc.psum_tensor(name, [P, 512], F32))

        sems = []

        def sem(name):
            sems.append(ctx.enter_context(nc.semaphore(name)))
            return sems[-1]

        w_qkv = sb("w_qkv", [P, KD, 3 * D])
        w_out = sb("w_out", [P, KD, D])
        blocks = sb("blocks", [P, PER])
        q_mask = sb("q_mask", [P, 2])
        stats, mv = sb("a_stats", [P, ST, 6]), sb("a_mv", [P, ST, 2])
        vare, rstd = sb("a_vare", [P, ST]), sb("a_rstd", [P, ST])
        xn = sb("a_xn", [P, ST, D])
        xT = sb("a_xT", [P, KD, T])
        q = [[sb(f"q{p}{i}", [P, HC, T]) for i in range(2)] for p in range(2)]
        kT = [sb(f"kT{p}", [P, HC, T]) for p in range(2)]
        v = [sb(f"v{p}", [P, ST, HEADS, DV]) for p in range(2)]
        nmax = [sb(f"nmax{i}", [P, ST]) for i in range(2)]
        prob = [sb(f"prob{i}", [P, ST, T]) for i in range(2)]
        probT = [sb(f"probT{i}", [P, ST, T]) for i in range(2)]
        oT = sb("oT", [P, T])
        rsum = sb("rsum", [P, ST, QUAD])
        o_norm = sb("o_norm", [P, ST, D])
        onT = sb("onT", [P, KD, T])
        ps_s = [psum(f"ps_s{i}") for i in range(2)]
        ps_pt = [psum(f"ps_pt{i}") for i in range(2)]
        ps_p = [psum(f"ps_p{i}") for i in range(2)]
        ps_o, ps_f = psum("ps_o"), psum("ps_f")

        w_in, mask_step, v_init = sem("aw_in"), sem("mask_step"), sem("v_init")
        stat_done, aggr_done, vare_done, rstd_done, xn_done = map(
            sem, ("a_stat_done", "a_aggr_done", "a_vare_done", "a_rstd_done", "a_xn_done"))
        xt_done, xt_evac, q_done, q_evac, k_done, k_evac, v_done, v_evac = map(
            sem, ("xt_done", "xt_evac", "q_done", "q_evac", "k_done", "k_evac", "v_done", "v_evac"))
        s_done, nmax_done, exp_done, pt_done, pt_evac, pv_done = map(
            sem, ("s_done", "nmax_done", "exp_done", "pt_done", "pt_evac", "pv_done"))
        ot_evac, to_done, rsum_done, norm_done = map(sem, ("ot_evac", "to_done", "rsum_done", "norm_done"))
        on_done, on_evac, out_done, res_done = map(sem, ("on_done", "on_evac", "out_done", "a_res_done"))

        start_at_one(nc, sems)
        block = ctx.enter_context(nc.Block())

        def over_sequences(eng, run):
            run(0, 0, True, False)
            with eng.Fori(0, SEQS // 2 - 1) as i:
                run(2 * i + 1, 1, False, False)
                run(2 * i + 2, 0, False, False)
            run(SEQS - 1, 1, False, True)

        @block.sync
        def _(sp):
            sp.dma_start(w_qkv[:], w["w_qkvT"].rearrange("(k p) f -> p k f", p=P)).then_inc(w_in, 16)
            sp.dma_start(w_out[:], w["w_outT"].rearrange("(k p) f -> p k f", p=P)).then_inc(w_in, 16)

        @block.gpsimd
        def _(pool):
            pool.memset(blocks[:], 1.0 / DH ** 0.5).then_inc(mask_step, 1)
            pool.wait_ge(mask_step, ONE + 1)
            pool.affine_select(out=blocks[:], in_=blocks[:], compare_op=ALU.is_ge, fill=0.0, base=0,
                               pattern=[[-DH, PER]], channel_multiplier=1).then_inc(mask_step, 1)
            pool.wait_ge(mask_step, ONE + 2)
            pool.affine_select(out=blocks[:], in_=blocks[:], compare_op=ALU.is_ge, fill=0.0, base=DH - 1,
                               pattern=[[DH, PER]], channel_multiplier=-1).then_inc(mask_step, 1)
            for p in range(2):
                pool.memset(v[p][:], 0.0).then_inc(v_init, 1)
            pool.wait_ge(v_init, ONE + 2)
            for p in range(2):
                pool.memset(v[p][:, :, :, DH:DH + 1], 1.0).then_inc(v_init, 1)

            def root(b):
                pool.wait_ge(vare_done, ONE + b + 1)
                pool.wait_ge(xn_done, ONE + ST * b)
                pool.tensor_tensor(rstd[:], vare[:], neg_half[:, 0:ST], ALU.pow).then_inc(rstd_done, 1)

            root(0)
            with pool.Fori(0, SEQS - 1) as b:
                root(b + 1)

        @block.tensor
        def _(pe):
            def turn_x(b):
                pe.wait_ge(xn_done, ONE + ST * (b + 1))
                pe.wait_ge(k_evac, ONE + b)
                for k in range(KD):
                    for j in range(ST):
                        last = pe.transpose(ps_p[0][:, T * k + P * j:T * k + P * j + P],
                                            xn[:, j, P * k:P * k + P], ident)
                last.then_inc(xt_done, 1)

            def project(bank, f0, done):
                for c in range(HC):
                    for k in range(KD):
                        last = pe.matmul(ps_p[bank][:, T * c:T * c + T], w_qkv[:, k, f0 + P * c:f0 + P * c + P],
                                         xT[:, k, :], start=(k == 0), stop=(k == KD - 1))
                last.then_inc(done, 1)

            def project_q(b):
                pe.wait_ge(xt_evac, ONE + b + 1)
                pe.wait_ge(v_evac, ONE + b)
                project(1, 0, q_done)

            def project_k(b):
                project(0, D, k_done)

            def project_v(b):
                pe.wait_ge(q_evac, ONE + 2 * (b + 1))
                for j in range(ST):
                    for k in range(KD):
                        last = pe.matmul(ps_p[1][:, D * j:D * j + D], xT[:, k, P * j:P * j + P],
                                         w_qkv[:, k, 2 * D:3 * D], start=(k == 0), stop=(k == KD - 1))
                last.then_inc(v_done, 1)

            def scores(b, p, h):
                m = HEADS * b + h
                if h == 0:
                    pe.wait_ge(q_evac, ONE + 2 * (b + 1))
                    pe.wait_ge(k_evac, ONE + b + 1)
                c, rows = h // PER, slice(DV * (h % PER // 2), DV * (h % PER // 2) + DV)
                for i in range(ST):
                    last = pe.matmul(ps_s[h % 2][:, T * i:T * i + T], q[p][h % 2][rows, c, P * i:P * i + P],
                                     kT[p][rows, c, :], start=True, stop=True)
                last.then_inc(s_done, 1)

            def turn_probs(b, h):
                pe.wait_ge(exp_done, ONE + ST * (HEADS * b + h + 1))
                for j in range(ST):
                    for i in range(ST):
                        last = pe.transpose(ps_pt[h % 2][:, T * j + P * i:T * j + P * i + P],
                                            prob[h % 2][:, i, P * j:P * j + P], ident)
                last.then_inc(pt_done, 1)

            def weigh(b, p, h):
                pe.wait_ge(pt_evac, ONE + HEADS * b + h + 1)
                if h == 0:
                    pe.wait_ge(v_evac, ONE + b + 1)
                if h % QUAD == 0:
                    pe.wait_ge(ot_evac, ONE + QUADS * b + h // QUAD)
                rows = slice(DV * (h % QUAD), DV * (h % QUAD) + DV)
                for j in range(ST):
                    last = pe.matmul(ps_o[rows, 0:T], v[p][:, j, h, :], probT[h % 2][:, j, :],
                                     start=(j == 0), stop=(j == ST - 1))
                if h % QUAD == QUAD - 1:
                    last.then_inc(pv_done, 1)

            def turn_quad(b, u):
                pe.wait_ge(ot_evac, ONE + QUADS * b + u + 1)
                if u == 0:
                    pe.wait_ge(res_done, ONE + b)
                else:
                    pe.wait_ge(norm_done, ONE + QUADS * b + u)
                for i in range(ST):
                    last = pe.transpose(ps_f[:, P * i:P * i + P], oT[:, P * i:P * i + P], ident)
                last.then_inc(to_done, 1)

            def turn_out(b):
                pe.wait_ge(norm_done, ONE + QUADS * (b + 1))
                for k in range(KD):
                    for i in range(ST):
                        last = pe.transpose(ps_f[:, T * k + P * i:T * k + P * i + P],
                                            o_norm[:, i, P * k:P * k + P], ident)
                last.then_inc(on_done, 1)

            def project_out(b):
                pe.wait_ge(on_evac, ONE + b + 1)
                for i in range(ST):
                    for k in range(KD):
                        last = pe.matmul(ps_f[:, D * i:D * i + D], onT[:, k, P * i:P * i + P], w_out[:, k, :],
                                         start=(k == 0), stop=(k == KD - 1))
                last.then_inc(out_done, 1)

            def sequence(b, p, first, last):
                for h in range(HEADS):
                    turn_probs(b, h)
                    if h + 2 < HEADS:
                        scores(b, p, h + 2)
                    elif not last:
                        scores(b + 1, 1 - p, h + 2 - HEADS)
                    if h:
                        weigh(b, p, h - 1)
                    elif not first:
                        weigh(b - 1, 1 - p, HEADS - 1)
                    if h % QUAD == 1 and h > QUAD:
                        turn_quad(b, h // QUAD - 1)
                    if not first:
                        if h == 1:
                            turn_quad(b - 1, QUADS - 1)
                        if h == 3:
                            turn_out(b - 1)
                        if h == 4:
                            project_out(b - 1)
                    if not last:
                        if h == 2:
                            turn_x(b + 1)
                        if h == 5:
                            project_q(b + 1)
                        if h == 7:
                            project_k(b + 1)
                        if h == 9:
                            project_v(b + 1)

            pe.wait_ge(w_in, ONE + 32)
            turn_x(0)
            project_q(0)
            project_k(0)
            project_v(0)
            scores(0, 0, 0)
            scores(0, 0, 1)
            pe.wait_ge(v_init, ONE + 4)
            over_sequences(pe, sequence)
            weigh(SEQS - 1, 1, HEADS - 1)
            turn_quad(SEQS - 1, QUADS - 1)
            turn_out(SEQS - 1)
            project_out(SEQS - 1)

        @block.vector
        def _(dve):
            def statistics(b):
                for j in range(ST):
                    dve.bn_stats(stats[:, j, :], x_res[:, ds(ST * b + j, 1), :]).then_inc(stat_done, 1)
                wait_apart(dve, started, stat_done, ONE + ST * (b + 1))
                for j in range(ST):
                    dve.bn_aggr(mv[:, j, :], stats[:, j, :]).then_inc(aggr_done, 1)
                dve.wait_ge(aggr_done, ONE + ST * (b + 1))
                dve.wait_ge(rstd_done, ONE + b)
                dve.tensor_scalar(vare[:], mv[:, :, 1], EPS, None, ALU.add).then_inc(vare_done, 1)

            def normalise(b):
                dve.wait_ge(rstd_done, ONE + b + 1)
                dve.wait_ge(xt_done, ONE + b)
                for j in range(ST):
                    dve.tensor_scalar(xn[:, j, :], x_res[:, ds(ST * b + j, 1), :].rearrange("p o d -> p (o d)"),
                                      mv[:, j, 0:1], rstd[:, j:j + 1], ALU.subtract, ALU.mult).then_inc(xn_done, 1)

            def row_max(b, h):
                m = HEADS * b + h
                dve.wait_ge(s_done, ONE + m + 1)
                dve.tensor_reduce(nmax[h % 2][:], ps_s[h % 2][:].rearrange("p (i j) -> p i j", i=ST), AX.X, ALU.max,
                                  negate=True).then_inc(nmax_done, 1)

            def probs_out(b, h):
                dve.wait_ge(pt_done, ONE + HEADS * b + h + 1)
                dve.tensor_copy(probT[h % 2][:].rearrange("p j i -> p (j i)"), ps_pt[h % 2][:]).then_inc(pt_evac, 1)

            def divide(b, u):
                n = QUADS * b + u
                quad = ps_f[:, 0:T].rearrange("p (i h e) -> p i h e", i=ST, h=QUAD)
                dve.wait_ge(to_done, ONE + n + 1)
                dve.reciprocal(rsum[:].unsqueeze(3), quad[:, :, :, DH:DH + 1]).then_inc(rsum_done, 1)
                dve.wait_ge(rsum_done, ONE + n + 1)
                if u == 0:
                    dve.wait_ge(on_done, ONE + b)
                dve.tensor_tensor(o_norm[:, :, QUAD * DH * u:QUAD * DH * (u + 1)].rearrange("p i (h e) -> p i h e", h=QUAD),
                                  quad[:, :, :, 0:DH], rsum[:].unsqueeze(3).to_broadcast([P, ST, QUAD, DH]),
                                  ALU.mult).then_inc(norm_done, 1)

            def residual(b):
                dve.wait_ge(out_done, ONE + b + 1)
                pair = x_res[:, ds(ST * b, ST), :]
                dve.tensor_tensor(pair, ps_f[:].rearrange("p (j d) -> p j d", j=ST), pair, ALU.add)\
                   .then_inc(res_done, 1)

            def sequence(b, p, first, last):
                for h in range(HEADS):
                    probs_out(b, h)
                    if h + 2 < HEADS:
                        row_max(b, h + 2)
                    elif not last:
                        row_max(b + 1, h + 2 - HEADS)
                    if h % QUAD == 1 and h > QUAD:
                        divide(b, h // QUAD - 1)
                    if not first:
                        if h == 1:
                            divide(b - 1, QUADS - 1)
                        if h == 4:
                            residual(b - 1)
                    if not last:
                        if h == 0:
                            statistics(b + 1)
                        if h == 1:
                            normalise(b + 1)

            dve.wait_ge(mask_step, ONE + 3)
            for i in range(2):
                dve.tensor_reduce(q_mask[:, i:i + 1], blocks[:, i::2], AX.X, ALU.add).then_inc(mask_step, 1)
            statistics(0)
            normalise(0)
            row_max(0, 0)
            row_max(0, 1)
            over_sequences(dve, sequence)
            divide(SEQS - 1, QUADS - 1)
            residual(SEQS - 1)
            dve.wait_ge(res_done, ONE + SEQS)

        @block.scalar
        def _(act):
            def x_out(b):
                act.wait_ge(xt_done, ONE + b + 1)
                act.wait_ge(v_done, ONE + b)
                act.activation(xT[:].rearrange("p k t -> p (k t)"), ps_p[0][:], ACT.Copy).then_inc(xt_evac, 1)

            def q_out(b, p):
                act.wait_ge(q_done, ONE + b + 1)
                for i in range(2):
                    act.activation(q[p][i][:].rearrange("p c t -> p (c t)"), ps_p[1][:], ACT.Copy,
                                   scale=q_mask[:, i:i + 1]).then_inc(q_evac, 1)

            def k_out(b, p):
                act.wait_ge(k_done, ONE + b + 1)
                act.activation(kT[p][:].rearrange("p c t -> p (c t)"), ps_p[0][:], ACT.Copy).then_inc(k_evac, 1)

            def v_out(b, p):
                act.wait_ge(v_done, ONE + b + 1)
                act.activation(v[p][:, :, :, 0:DH], ps_p[1][:].rearrange("p (j h e) -> p j h e", j=ST, h=HEADS),
                               ACT.Copy).then_inc(v_evac, 1)

            def exponentials(b, h):
                act.wait_ge(nmax_done, ONE + HEADS * b + h + 1)
                for i in range(ST):
                    act.activation(prob[h % 2][:, i, :], ps_s[h % 2][:, T * i:T * i + T], ACT.Exp,
                                   bias=nmax[h % 2][:, i:i + 1]).then_inc(exp_done, 1)

            def quad_out(b, u):
                n = QUADS * b + u
                act.wait_ge(pv_done, ONE + n + 1)
                act.wait_ge(to_done, ONE + n)
                act.activation(oT[:], ps_o[:, 0:T], ACT.Copy).then_inc(ot_evac, 1)

            def out_out(b):
                act.wait_ge(on_done, ONE + b + 1)
                act.wait_ge(out_done, ONE + b)
                act.activation(onT[:].rearrange("p k t -> p (k t)"), ps_f[:], ACT.Copy).then_inc(on_evac, 1)

            def sequence(b, p, first, last):
                for h in range(HEADS):
                    if h + 2 < HEADS:
                        exponentials(b, h + 2)
                    elif not last:
                        exponentials(b + 1, h + 2 - HEADS)
                    if h % QUAD == 0 and h:
                        quad_out(b, h // QUAD - 1)
                    if not first:
                        if h == 0:
                            quad_out(b - 1, QUADS - 1)
                        if h == 3:
                            out_out(b - 1)
                    if not last:
                        if h == 2:
                            x_out(b + 1)
                        if h == 5:
                            q_out(b + 1, 1 - p)
                        if h == 7:
                            k_out(b + 1, 1 - p)
                        if h == 9:
                            v_out(b + 1, 1 - p)

            act.wait_ge(mask_step, ONE + 5)
            act.wait_ge(v_init, ONE + 4)
            x_out(0)
            q_out(0, 0)
            k_out(0, 0)
            v_out(0, 0)
            exponentials(0, 0)
            exponentials(0, 1)
            over_sequences(act, sequence)
            quad_out(SEQS - 1, QUADS - 1)
            out_out(SEQS - 1)


def route(nc, started, x_res, xn_dram, ident, neg_half, w, r):
    E, L = EXPERTS, LANGS
    with ExitStack() as ctx:
        def sb(name, shape, dt=F32):
            return ctx.enter_context(nc.sbuf_tensor(name, shape, dt))

        def psum(name, cols=512):
            return ctx.enter_context(nc.psum_tensor(name, [P, cols], F32))

        sems = []

        def sem(name):
            sems.append(ctx.enter_context(nc.semaphore(name)))
            return sems[-1]

        w_r = sb("w_r", [P, KD, E + L])
        bias = sb("r_bias", [P, E + L])
        stats, mv = sb("r_stats", [P, G, 6]), sb("r_mv", [P, G, 2])
        vare, rstd = sb("r_vare", [P, G]), sb("r_rstd", [P, G])
        xn = sb("r_xn", [P, G, D])
        xT = sb("r_xT", [P, KD, GT])
        logits = sb("logits", [P, TILES, E + L])
        col = [sb(f"r_col{i}", [P, TILES, 1]) for i in range(6)]
        lang = sb("lang", [P, TILES, L + 1])
        ew = sb("ew", [P, TILES, L])
        pr = [sb(f"r_pr{i}", [P, TILES, E]) for i in range(3)]
        hot = [sb(f"hot{i}", [P, TILES, E]) for i in range(2)]
        both = sb("both", [P, TILES, E])
        rev = sb("rev", [P, E])
        lane_i, lane_f = sb("lane_i", [P, P], I32), sb("lane_f", [P, P])
        token_i, token_f = sb("token_i", [P, TILES], I32), sb("token_f", [P, TILES])
        thresholds = sb("thresholds", [P, TILES])
        before = sb("before", [P, P])
        ones = sb("r_ones", [P, P])
        totals = sb("totals", [P, E, TILES])
        keep = sb("keep", [P, E, TILES])
        running = sb("running", [P, E, TILES])
        place = sb("place", [P, E, TILES])
        over = sb("over", [P, E, TILES])
        blocks_of, ends, starts = sb("blocks_of", [P, E]), sb("ends", [P, E]), sb("starts", [P, E])
        past = sb("past", [P, BLOCKS, E])
        block_f = sb("block_f", [P, BLOCKS, 1])
        slot_f = [sb(f"slot_f{i}", [P, TILES, 1]) for i in range(2)]
        slot_i = [sb(f"slot_i{i}", [P, TILES], I32) for i in range(2)]
        part_i = [sb(f"part_i{i}", [P, TILES], I32) for i in range(4)]
        part_f = [sb(f"part_f{i}", [P, TILES]) for i in range(4)]
        lane_hot = [sb(f"lane_hot{i}", [P, P]) for i in range(4)]
        block_hot = [sb(f"block_hot{i}", [P, BLOCKS]) for i in range(4)]
        ps_t = [psum(f"r_ps_t{i}") for i in range(2)]
        ps_l, ps_rank, ps_tot, ps_tab = psum("ps_l"), psum("ps_rank"), psum("ps_tot"), psum("ps_tab")

        w_in, const = sem("rw_in"), sem("r_const")
        stat_done, aggr_done, vare_done, rstd_done, xn_done, xn_stored = map(
            sem, ("r_stat", "r_aggr", "r_vare_done", "r_rstd_done", "r_xn_done", "xn_stored"))
        t_done, t_evac, l_done, l_evac = map(sem, ("r_t_done", "r_t_evac", "l_done", "l_evac"))
        chain, exp_go, exp_back, both_ready, rank_done, hot_ready, table_used = map(
            sem, ("r_chain", "exp_go", "exp_back", "both_ready", "rank_done", "hot_ready", "table_used"))
        CONSTS = 10

        start_at_one(nc, sems)
        block = ctx.enter_context(nc.Block())

        @block.sync
        def _(sp):
            sp.dma_start(w_r[:], w["routerT"].rearrange("(k p) e -> p k e", p=P)).then_inc(w_in, 16)
            sp.dma_start(bias[:, 0:E], w["router_b"].rearrange("(o e) -> o e", o=1).to_broadcast([P, E])).then_inc(w_in, 16)
            sp.dma_start(bias[:, E:E + L], w["lang_b"].rearrange("(o e) -> o e", o=1).to_broadcast([P, L])).then_inc(w_in, 16)
            with sp.Fori(0, GROUPS) as g:
                sp.wait_ge(xn_done, ONE + G * (g + 1))
                sp.dma_start(xn_dram[ds(GT * g, GT), :].rearrange("(j p) d -> p j d", p=P), xn[:]).then_inc(xn_stored, 16)
            sp.wait_ge(xn_stored, ONE + 16 * GROUPS)

        @block.gpsimd
        def _(pool):
            pool.iota(lane_i[:], pattern=[[1, P]], base=0, channel_multiplier=0).then_inc(const, 1)
            pool.iota(token_i[:], pattern=[[P, TILES]], base=0, channel_multiplier=1).then_inc(const, 1)
            pool.memset(ones[:], 1.0).then_inc(const, 1)
            pool.memset(keep[:], 1.0).then_inc(const, 1)
            pool.memset(lang[:], 0.0).then_inc(const, 1)
            pool.wait_ge(const, ONE + 5)
            pool.tensor_copy(lane_f[:], lane_i[:]).then_inc(const, 1)
            pool.tensor_copy(token_f[:], token_i[:]).then_inc(const, 1)
            pool.affine_select(out=before[:], in_=ones[:], compare_op=ALU.is_ge, fill=0.0, base=-1,
                               pattern=[[1, P]], channel_multiplier=-1).then_inc(const, 1)
            pool.memset(keep[:, :, 0:1], 0.0).then_inc(const, 1)
            pool.wait_ge(const, ONE + 9)
            pool.tensor_scalar(rev[:], lane_f[:, 0:E], -1.0, float(E), ALU.mult, ALU.add).then_inc(const, 1)
            with pool.Fori(0, GROUPS) as g:
                pool.wait_ge(vare_done, ONE + g + 1)
                pool.wait_ge(xn_done, ONE + G * g)
                pool.tensor_tensor(rstd[:], vare[:], neg_half[:, 0:G], ALU.pow).then_inc(rstd_done, 1)

        @block.tensor
        def _(pe):
            with pe.Fori(0, GROUPS) as g:
                pe.wait_ge(xn_done, ONE + G * (g + 1))
                pe.wait_ge(t_evac, ONE + KD * g)
                for k in range(KD):
                    for j in range(G):
                        last = pe.transpose(ps_t[k][:, P * j:P * j + P], xn[:, j, P * k:P * k + P], ident)
                last.then_inc(t_done, 1)
                pe.wait_ge(w_in, ONE + 48)
                pe.wait_ge(t_evac, ONE + KD * (g + 1))
                pe.wait_ge(l_evac, ONE + g)
                for j in range(G):
                    for k in range(KD):
                        last = pe.matmul(ps_l[:, (E + L) * j:(E + L) * (j + 1)], xT[:, k, P * j:P * j + P], w_r[:, k, :],
                                         start=(k == 0), stop=(k == KD - 1))
                last.then_inc(l_done, 1)
            pe.wait_ge(both_ready, ONE + 1)
            pe.wait_ge(const, ONE + CONSTS)
            flat = both[:].rearrange("p t e -> p (t e)")
            pe.matmul(ps_rank[:, 0:TILES * E], before[:], flat, start=True, stop=True)
            pe.matmul(ps_tot[:, 0:TILES * E], ones[:], flat, start=True, stop=True).then_inc(rank_done, 1)
            def table(n, i, first=False, last=False):
                pe.wait_ge(hot_ready, ONE + 2 * (n + 1))
                pe.matmul(ps_tab[:, 0:BLOCKS], lane_hot[i][:], block_hot[i][:], start=first, stop=last,
                          skip_group_check=True).then_inc(table_used, 1)

            for i in range(4):
                table(i, i, first=(i == 0))
            with pe.Fori(1, 2 * TILES // 4 - 1) as n:
                for i in range(4):
                    table(4 * n + i, i)
            for i in range(4):
                table(2 * TILES - 4 + i, i, last=(i == 3))

        @block.scalar
        def _(act):
            with act.Fori(0, GROUPS) as g:
                act.wait_ge(t_done, ONE + g + 1)
                act.wait_ge(l_done, ONE + g)
                for k in range(KD):
                    act.activation(xT[:, k, :], ps_t[k][:], ACT.Copy).then_inc(t_evac, 1)
            act.wait_ge(exp_go, ONE + 1)
            act.activation(lang[:, :, 0:L], logits[:, :, E:E + L], ACT.Exp).then_inc(exp_back, 1)
            act.wait_ge(exp_go, ONE + 2)
            act.activation(pr[1][:], pr[0][:], ACT.Exp).then_inc(exp_back, 1)

        @block.vector
        def _(dve):
            links = [0]

            def link(ins):
                links[0] += 1
                ins.then_inc(chain, 1)
                dve.wait_ge(chain, ONE + links[0])

            with dve.Fori(0, GROUPS) as g:
                for j in range(G):
                    dve.bn_stats(stats[:, j, :], x_res[:, ds(G * g + j, 1), :]).then_inc(stat_done, 1)
                wait_apart(dve, started, stat_done, ONE + G * (g + 1))
                for j in range(G):
                    dve.bn_aggr(mv[:, j, :], stats[:, j, :]).then_inc(aggr_done, 1)
                dve.wait_ge(aggr_done, ONE + G * (g + 1))
                dve.wait_ge(rstd_done, ONE + g)
                dve.tensor_scalar(vare[:], mv[:, :, 1], EPS, None, ALU.add).then_inc(vare_done, 1)
                dve.wait_ge(rstd_done, ONE + g + 1)
                dve.wait_ge(t_done, ONE + g)
                dve.wait_ge(xn_stored, ONE + 16 * g)
                for j in range(G):
                    dve.tensor_scalar(xn[:, j, :], x_res[:, ds(G * g + j, 1), :].rearrange("p o d -> p (o d)"),
                                      mv[:, j, 0:1], rstd[:, j:j + 1], ALU.subtract, ALU.mult).then_inc(xn_done, 1)
                dve.wait_ge(l_done, ONE + g + 1)
                dve.wait_ge(w_in, ONE + 48)
                dve.tensor_tensor(logits[:, ds(G * g, G), :], ps_l[:, 0:G * (E + L)].rearrange("p (j e) -> p j e", j=G),
                                  bias[:].unsqueeze(1).to_broadcast([P, G, E + L]), ALU.add).then_inc(l_evac, 1)
            dve.wait_ge(l_evac, ONE + GROUPS)
            dve.wait_ge(const, ONE + CONSTS)

            def wide(c, n):
                return c[:].to_broadcast([P, TILES, n])

            link(dve.tensor_reduce(col[0][:, :, 0], logits[:, :, E:E + L], AX.X, ALU.max))
            dve.tensor_tensor(logits[:, :, E:E + L], logits[:, :, E:E + L], wide(col[0], L), ALU.subtract)\
               .then_inc(exp_go, 1)
            dve.wait_ge(exp_back, ONE + 1)
            link(dve.tensor_reduce(col[1][:, :, 0], lang[:, :, 0:L], AX.X, ALU.add))
            link(dve.reciprocal(col[2][:], col[1][:]))
            link(dve.tensor_tensor(lang[:, :, 0:L], lang[:, :, 0:L], wide(col[2], L), ALU.mult))
            link(dve.tensor_tensor(ew[:], lang[:, :, 0:L], lang[:, :, 1:L + 1], ALU.add))
            for i in range(E // L):
                link(dve.scalar_tensor_tensor(out=pr[2][:, :, L * i:L * i + L], in0=ew[:], scalar=0.1,
                                              in1=logits[:, :, L * i:L * i + L], op0=ALU.mult, op1=ALU.add))
            link(dve.tensor_reduce(col[0][:, :, 0], pr[2][:], AX.X, ALU.max))
            dve.tensor_tensor(pr[0][:], pr[2][:], wide(col[0], E), ALU.subtract).then_inc(exp_go, 1)
            dve.wait_ge(exp_back, ONE + 2)
            link(dve.tensor_reduce(col[1][:, :, 0], pr[1][:], AX.X, ALU.add))
            link(dve.reciprocal(col[2][:], col[1][:]))
            link(dve.tensor_tensor(pr[0][:], pr[1][:], wide(col[2], E), ALU.mult))
            best = [col[3], col[4]]
            for i in range(2):
                link(dve.tensor_reduce(best[i][:, :, 0], pr[0][:], AX.X, ALU.max))
                link(dve.tensor_tensor(pr[1][:], pr[0][:], wide(best[i], E), ALU.is_equal))
                link(dve.tensor_tensor(pr[2][:], pr[1][:], rev[:].unsqueeze(1).to_broadcast([P, TILES, E]), ALU.mult))
                link(dve.tensor_reduce(col[5][:, :, 0], pr[2][:], AX.X, ALU.max))
                link(dve.tensor_tensor(hot[i][:], rev[:].unsqueeze(1).to_broadcast([P, TILES, E]), wide(col[5], E),
                                       ALU.is_equal))
                if i == 0:
                    link(dve.scalar_tensor_tensor(out=pr[0][:], in0=hot[0][:], scalar=-2.0, in1=pr[0][:],
                                                  op0=ALU.mult, op1=ALU.add))
            link(dve.tensor_tensor(col[0][:], best[0][:], best[1][:], ALU.add))
            link(dve.reciprocal(col[1][:], col[0][:]))
            for i in range(2):
                link(dve.tensor_tensor(r["weight"][i][:].unsqueeze(2), best[i][:], col[1][:], ALU.mult))
            dve.tensor_tensor(both[:], hot[0][:], hot[1][:], ALU.add).then_inc(both_ready, 1)
            dve.wait_ge(rank_done, ONE + 1)
            link(dve.tensor_copy(totals[:], ps_tot[:, 0:TILES * E].rearrange("p (t e) -> p e t", e=E)))
            link(dve.tensor_tensor_scan(running[:].rearrange("p e t -> p (e t)"), keep[:].rearrange("p e t -> p (e t)"),
                                        totals[:].rearrange("p e t -> p (e t)"), 0.0, ALU.mult, ALU.add))
            link(dve.tensor_scalar(thresholds[:], lane_f[:, 0:TILES], float(P), None, ALU.mult))
            link(dve.tensor_tensor(over[:], running[:, :, TILES - 1:TILES].to_broadcast([P, E, TILES]),
                                   thresholds[:].unsqueeze(1).to_broadcast([P, E, TILES]), ALU.is_gt))
            link(dve.tensor_reduce(blocks_of[:], over[:], AX.X, ALU.add))
            link(dve.tensor_tensor_scan(ends[:], ones[:, 0:E], blocks_of[:], 0.0, ALU.mult, ALU.add))
            link(dve.tensor_tensor(starts[:], ends[:], blocks_of[:], ALU.subtract))
            link(dve.tensor_tensor(past[:], lane_f[:, 0:BLOCKS].unsqueeze(2).to_broadcast([P, BLOCKS, E]),
                                   ends[:].unsqueeze(1).to_broadcast([P, BLOCKS, E]), ALU.is_ge))
            link(dve.tensor_reduce(block_f[:, :, 0], past[:], AX.X, ALU.add))
            link(dve.tensor_scalar(r["expert"][:], block_f[:, :, 0], float(E - 1), None, ALU.min))
            link(dve.tensor_tensor(place[:], running[:], totals[:], ALU.subtract))
            link(dve.tensor_tensor(running[:], place[:], ps_rank[:, 0:TILES * E].rearrange("p (t e) -> p e t", e=E), ALU.add))
            link(dve.scalar_tensor_tensor(out=place[:], in0=starts[:].unsqueeze(2).to_broadcast([P, E, TILES]),
                                          scalar=float(P), in1=running[:], op0=ALU.mult, op1=ALU.add))
            for i in range(2):
                link(dve.tensor_tensor(pr[i][:], hot[i][:], place[:].rearrange("p e t -> p t e"), ALU.mult))
                link(dve.tensor_reduce(slot_f[i][:, :, 0], pr[i][:], AX.X, ALU.add))
                link(dve.tensor_copy(r["slot"][i][:], slot_f[i][:, :, 0]))
                link(dve.tensor_copy(slot_i[i][:], slot_f[i][:, :, 0]))
                link(dve.tensor_scalar(part_i[2 * i][:], slot_i[i][:], P - 1, None, ALU.bitwise_and))
                link(dve.tensor_scalar(part_i[2 * i + 1][:], slot_i[i][:], P.bit_length() - 1, None,
                                       ALU.logical_shift_right))
                for j in (2 * i, 2 * i + 1):
                    link(dve.tensor_copy(part_f[j][:], part_i[j][:]))

            def one_hots(t, u, i):
                b = 2 * u + i
                dve.tensor_scalar(lane_hot[b][:], lane_f[:], part_f[2 * i][:, ds(t, 1)], None,
                                  ALU.is_equal).then_inc(hot_ready, 1)
                dve.tensor_scalar(block_hot[b][:], lane_f[:, 0:BLOCKS], part_f[2 * i + 1][:, ds(t, 1)],
                                  token_f[:, ds(t, 1)], ALU.is_equal, ALU.mult).then_inc(hot_ready, 1)

            for u in range(2):
                for i in range(2):
                    one_hots(u, u, i)
            with dve.Fori(1, TILES // 2) as n:
                for u in range(2):
                    for i in range(2):
                        dve.wait_ge(table_used, ONE + 4 * n + 2 * u + i - 3)
                        one_hots(2 * n + u, u, i)
            dve.wait_ge(table_used, ONE + 2 * TILES)
            link(dve.tensor_copy(r["token"][:], ps_tab[:, 0:BLOCKS]))


def experts(nc, started, xn_dram, y_dram, ident, w1, w2, w_in, r, w):
    with ExitStack() as ctx:
        def sb(name, shape, dt=F32):
            return ctx.enter_context(nc.sbuf_tensor(name, shape, dt))

        def psum(name):
            return ctx.enter_context(nc.psum_tensor(name, [P, 512], F32))

        sems = []

        def sem(name):
            sems.append(ctx.enter_context(nc.semaphore(name)))
            return sems[-1]

        b1 = sb("e_b1", [P, EXPERTS, FC])
        b2 = sb("e_b2", [P, EXPERTS, D])
        index = [sb(f"index{i}", [P, 1], U32) for i in range(2)]
        index_ready = sem("index_ready")
        xg = [sb(f"xg{i}", [P, D]) for i in range(2)]
        xgT = [sb(f"xgT{i}", [P, KD, P]) for i in range(2)]
        pre = sb("pre", [P, F])
        hT = [sb(f"e_hT{i}", [P, FC, P]) for i in range(2)]
        y = [sb(f"e_y{i}", [P, D]) for i in range(2)]
        ps_x = psum("e_ps_x")
        ps_h = [psum(f"e_ps_h{i}") for i in range(2)]
        ps_t = [psum(f"e_ps_t{i}") for i in range(2)]
        ps_y = psum("e_ps_y")
        gathered = [ctx.enter_context(nc.semaphore(f"e_gathered{i}")) for i in range(2)]
        y_stored = [sem(f"e_y_stored{i}") for i in range(2)]
        b_in, xt_done, xt_evac, h_done, h_evac, ht_done, gelu_done, y_done, y_evac = map(
            sem, ("eb_in", "e_xt_done", "e_xt_evac", "e_h_done", "e_h_evac", "e_ht_done",
                  "e_gelu_done", "e_y_done", "e_y_evac"))

        start_at_one(nc, sems)
        block = ctx.enter_context(nc.Block())

        def expert_of(eng, b):
            return eng.value_load(r["expert"][0:1, ds(b, 1)], min_val=0, max_val=EXPERTS - 1)

        @block.gpsimd
        def _(pool):
            def gather(b, i):
                pool.tensor_copy(index[i][:], r["token"][:, ds(b, 1)]).then_inc(index_ready, 1)
                wait_apart(pool, started, index_ready, ONE + b + 1)
                pool.indirect_dma_start(
                    out=xg[i][:], out_offset=None, in_=xn_dram,
                    in_offset=bass.IndirectOffsetOnAxis(ap=index[i][:], axis=0),
                ).then_inc(gathered[i], 16)

            gather(0, 0)
            gather(1, 1)
            with pool.Fori(0, BLOCKS // 2 - 1) as n:
                for i in range(2):
                    pool.wait_ge(xt_done, ONE + 2 * n + i + 1)
                    gather(2 * n + i + 2, i)

        @block.sync
        def _(sp):
            sp.dma_start(b1[:], w["e_b1"]).then_inc(b_in, 16)
            sp.dma_start(b2[:], w["e_b2"].rearrange("(o e) d -> o e d", o=1).to_broadcast([P, EXPERTS, D])).then_inc(b_in, 16)
            with sp.Fori(0, BLOCKS // 2) as n:
                for i in range(2):
                    b = 2 * n + i
                    sp.wait_ge(y_evac, ONE + b + 1)
                    sp.dma_start(y_dram[ds(P * b, P), :], y[i][:]).then_inc(y_stored[i], 16)
            for i in range(2):
                sp.wait_ge(y_stored[i], ONE + 16 * BLOCKS // 2)

        @block.tensor
        def _(pe):
            def turn_x(b, i, pair):
                pe.wait_ge(gathered[i], 16 * (pair + 1))
                pe.wait_ge(xt_evac, ONE + b)
                for k in range(KD):
                    last = pe.transpose(ps_x[:, P * k:P * k + P], xg[i][:, P * k:P * k + P], ident)
                last.then_inc(xt_done, 1)

            def hidden(b, i):
                e = expert_of(pe, b)
                pe.wait_ge(xt_evac, ONE + b + 1)
                pe.wait_ge(h_evac, ONE + 2 * b)
                for f in range(2):
                    for k in range(KD):
                        last = pe.matmul(ps_h[f][:], xgT[i][:, k, :],
                                         w1[:, ds(e, 1), k, 512 * f:512 * f + 512].rearrange("p o f -> p (o f)"),
                                         start=(k == 0), stop=(k == KD - 1))
                last.then_inc(h_done, 1)

            def turn_h(b):
                pe.wait_ge(h_evac, ONE + 2 * (b + 1))
                pe.wait_ge(gelu_done, ONE + FC * b)
                for c in range(FC):
                    last = pe.transpose(ps_t[c // 4][:, P * (c % 4):P * (c % 4) + P], pre[:, P * c:P * c + P], ident)
                last.then_inc(ht_done, 1)

            def output(b, i):
                e = expert_of(pe, b)
                pe.wait_ge(gelu_done, ONE + FC * (b + 1))
                pe.wait_ge(y_evac, ONE + b)
                for c in range(FC):
                    last = pe.matmul(ps_y[:, 0:D], hT[i][:, c, :], w2[:, ds(e, 1), c, :].rearrange("p o d -> p (o d)"),
                                     start=(c == 0), stop=(c == FC - 1))
                last.then_inc(y_done, 1)

            pe.wait_ge(w_in, 16 * 2 * EXPERTS)
            turn_x(0, 0, 0)
            hidden(0, 0)
            turn_x(1, 1, 0)
            hidden(1, 1)
            turn_h(0)
            turn_x(2, 0, 1)
            with pe.Fori(0, BLOCKS // 2 - 2) as n:
                for i in (1, 2):
                    b = 2 * n + i
                    hidden(b + 1, (i + 1) % 2)
                    turn_h(b)
                    turn_x(b + 2, i % 2, n + 1 + i // 2)
                    output(b - 1, (i + 1) % 2)
            b = BLOCKS - 3
            hidden(b + 1, 0)
            turn_h(b)
            turn_x(b + 2, 1, BLOCKS // 2 - 1)
            output(b - 1, 0)
            hidden(b + 2, 1)
            turn_h(b + 1)
            output(b, 1)
            turn_h(b + 2)
            output(b + 1, 0)
            output(b + 2, 1)

        @block.vector
        def _(dve):
            def hidden_out(b):
                dve.wait_ge(h_done, ONE + b + 1)
                dve.wait_ge(ht_done, ONE + b)
                for f in range(2):
                    dve.tensor_copy(pre[:, 512 * f:512 * f + 512], ps_h[f][:]).then_inc(h_evac, 1)

            def output_out(b, i):
                e = expert_of(dve, b)
                dve.wait_ge(y_done, ONE + b + 1)
                dve.tensor_tensor(y[i][:], ps_y[:, 0:D], b2[:, ds(e, 1), :].rearrange("p o d -> p (o d)"), ALU.add)\
                   .then_inc(y_evac, 1)

            dve.wait_ge(b_in, ONE + 32)
            hidden_out(0)
            hidden_out(1)
            hidden_out(2)
            output_out(0, 0)
            hidden_out(3)
            output_out(1, 1)
            with dve.Fori(1, BLOCKS // 2 - 1) as n:
                for i in range(2):
                    b = 2 * n + i
                    hidden_out(b + 2)
                    dve.wait_ge(y_stored[i], ONE + 16 * n)
                    output_out(b, i)
            for i in range(2):
                b = BLOCKS - 2 + i
                dve.wait_ge(y_stored[i], ONE + 16 * (BLOCKS // 2 - 1))
                output_out(b, i)

        @block.scalar
        def _(act):
            def x_out(b, i):
                act.wait_ge(xt_done, ONE + b + 1)
                act.activation(xgT[i][:].rearrange("p k t -> p (k t)"), ps_x[:, 0:KD * P], ACT.Copy).then_inc(xt_evac, 1)

            def gelu(b, i):
                e = expert_of(act, b)
                wait_apart(act, started, ht_done, ONE + b + 1)
                for c in range(FC):
                    act.activation(hT[i][:, c, :], ps_t[c // 4][:, P * (c % 4):P * (c % 4) + P], ACT.Gelu,
                                   bias=b1[:, ds(e, 1), c]).then_inc(gelu_done, 1)

            act.wait_ge(b_in, ONE + 32)
            x_out(0, 0)
            x_out(1, 1)
            gelu(0, 0)
            with act.Fori(0, BLOCKS // 2 - 1) as n:
                for i in range(2):
                    act.wait_ge(h_done, ONE + 2 * n + i + 1)
                    x_out(2 * n + i + 2, i)
                    gelu(2 * n + i + 1, (i + 1) % 2)
            gelu(BLOCKS - 1, 1)


def combine(nc, started, x_res, y_dram, out, r):
    with ExitStack() as ctx:
        SLOTS = 4
        rows = [[ctx.enter_context(nc.sbuf_tensor(f"rows{i}_{s}", [P, D], F32)) for s in range(SLOTS)] for i in range(2)]
        result = [ctx.enter_context(nc.sbuf_tensor(f"result{s}", [P, D], F32)) for s in range(SLOTS)]
        half = [ctx.enter_context(nc.sbuf_tensor(f"half{s}", [P, D], F32)) for s in range(SLOTS)]
        index = [[ctx.enter_context(nc.sbuf_tensor(f"slot{i}_{s}", [P, 1], U32)) for s in range(SLOTS)] for i in range(2)]
        fetched = [ctx.enter_context(nc.semaphore(f"rows_in{s}")) for s in range(SLOTS)]
        stored = [ctx.enter_context(nc.semaphore(f"out_stored{s}")) for s in range(SLOTS)]
        index_ready, first_done, done = [ctx.enter_context(nc.semaphore(n)) for n in
                                         ("slots_ready", "first_added", "result_done")]
        sems = [*stored, index_ready, first_done, done]
        start_at_one(nc, sems)
        block = ctx.enter_context(nc.Block())

        @block.gpsimd
        def _(pool):
            def fetch(t, s):
                for i in range(2):
                    pool.tensor_copy(index[i][s][:], r["slot"][i][:, ds(t, 1)]).then_inc(index_ready, 1)
                wait_apart(pool, started, index_ready, ONE + 2 * (t + 1))
                for i in range(2):
                    pool.indirect_dma_start(
                        out=rows[i][s][:], out_offset=None, in_=y_dram,
                        in_offset=bass.IndirectOffsetOnAxis(ap=index[i][s][:], axis=0),
                    ).then_inc(fetched[s], 16)

            for s in range(SLOTS):
                fetch(s, s)
            with pool.Fori(1, TILES // SLOTS) as n:
                for s in range(SLOTS):
                    pool.wait_ge(done, ONE + SLOTS * n + s - SLOTS + 1)
                    fetch(SLOTS * n + s, s)

        @block.vector
        def _(dve):
            def add(t, s, turn):
                dve.wait_ge(fetched[s], 32 * (turn + 1))
                x = x_res[:, ds(t, 1), :].rearrange("p o d -> p (o d)")
                dve.scalar_tensor_tensor(out=half[s][:], in0=rows[0][s][:], scalar=r["weight"][0][:, ds(t, 1)],
                                         in1=x, op0=ALU.mult, op1=ALU.add).then_inc(first_done, 1)
                dve.wait_ge(first_done, ONE + t + 1)
                dve.scalar_tensor_tensor(out=result[s][:], in0=rows[1][s][:], scalar=r["weight"][1][:, ds(t, 1)],
                                         in1=half[s][:], op0=ALU.mult, op1=ALU.add).then_inc(done, 1)

            for s in range(SLOTS):
                add(s, s, 0)
            with dve.Fori(1, TILES // SLOTS) as n:
                for s in range(SLOTS):
                    dve.wait_ge(stored[s], ONE + 16 * n)
                    add(SLOTS * n + s, s, n)

        @block.sync
        def _(sp):
            with sp.Fori(0, TILES // SLOTS) as n:
                for s in range(SLOTS):
                    sp.wait_ge(done, ONE + SLOTS * n + s + 1)
                    sp.dma_start(out[ds(P * (SLOTS * n + s), P), :], result[s][:]).then_inc(stored[s], 16)
            for s in range(SLOTS):
                sp.wait_ge(stored[s], ONE + 16 * TILES // SLOTS)


def build(nc, w, out):
    with ExitStack() as ctx:
        def sb(name, shape, dt=F32):
            return ctx.enter_context(nc.sbuf_tensor(name, shape, dt))

        x_res = sb("x_res", [P, TILES, D])
        ident = sb("ident", [P, P])
        neg_half = sb("neg_half", [P, 8])
        r = {"token": sb("slot_token", [P, BLOCKS], U32), "expert": sb("block_expert", [P, BLOCKS], I32),
             "slot": [sb(f"token_slot{i}", [P, TILES], U32) for i in range(2)],
             "weight": [sb(f"token_weight{i}", [P, TILES]) for i in range(2)]}
        xn_dram = nc.dram_tensor("xn_dram", [N, D], F32, kind="Internal").ap()
        y_dram = nc.dram_tensor("y_dram", [P * BLOCKS, D], F32, kind="Internal").ap()
        const = ctx.enter_context(nc.semaphore("const"))
        started = ctx.enter_context(nc.semaphore("started"))
        experts_in = ctx.enter_context(nc.semaphore("experts_in"))
        with nc.Block() as block:
            @block.gpsimd
            def _(pool):
                pool.memset(neg_half[:], -0.5).then_inc(const, 1)
                pool.memset(ident[:], 0.0).then_inc(const, 1)
                pool.wait_ge(const, 2)
                pool.affine_select(out=ident[:], in_=ident[:], compare_op=ALU.not_equal, fill=1.0, base=0,
                                   pattern=[[-1, P]], channel_multiplier=1).then_inc(const, 1)
                pool.wait_ge(const, 3)
                pool.memset(neg_half[:], -0.5).then_inc(started, 1)
                pool.wait_ge(started, 1)
        embed(nc, started, x_res, w["emb"], w["pos_emb"], w["tokens"])
        tower(nc, started, x_res, ident[:], neg_half, w)
        e_w1 = sb("e_w1", [P, EXPERTS, KD, F])
        e_w2 = sb("e_w2", [P, EXPERTS, FC, D])
        with nc.Block() as block:
            @block.sync
            def _(sp):
                for e in range(EXPERTS):
                    sp.dma_start(e_w1[:, e], w["e_w1"][e].rearrange("(k p) f -> p k f", p=P)).then_inc(experts_in, 16)
                    sp.dma_start(e_w2[:, e], w["e_w2"][e].rearrange("(c p) d -> p c d", p=P)).then_inc(experts_in, 16)
        attention(nc, started, x_res, ident[:], neg_half, w)
        route(nc, started, x_res, xn_dram, ident[:], neg_half, w, r)
        experts(nc, started, xn_dram, y_dram, ident[:], e_w1, e_w2, experts_in, r, w)
        combine(nc, started, x_res, y_dram, out, r)


def lay_out(inputs):
    import numpy as np

    a = {k.removeprefix("L0_tok_"): v for k, v in inputs.items() if k.startswith("L0_tok_")}
    a["tokens"] = np.asarray(inputs["x"]).reshape(TILES, P).T
    f = {k.removeprefix("L0_ffn_"): np.asarray(v) for k, v in inputs.items() if k.startswith("L0_ffn_")}
    a["routerT"] = np.concatenate([f["router_w"], f["lang_w"]]).T
    a["router_b"], a["lang_b"] = f["router_b"], f["lang_b"]
    a["e_w1"], a["e_w2"], a["e_b2"] = f["w1"], f["w2"], f["b2"]
    a["e_b1"] = f["b1"].reshape(EXPERTS, FC, P).transpose(2, 0, 1)
    a["w_qkvT"] = np.asarray(inputs["L0_attn_w_qkv"]).T
    a["w_outT"] = np.asarray(inputs["L0_attn_w_out"]).T
    a["A_diag"] = np.concatenate([a["A_diag"].T] * 2)
    a["b1"] = np.asarray(a["b1"]).reshape(LAYERS, FC, P).transpose(2, 0, 1)
    a["ln_par"] = np.stack([np.asarray(a.pop(n)).reshape(LAYERS, KD, P).transpose(2, 0, 1)
                            for n in ("ln1_s", "ln1_b", "ln2_s", "ln2_b")], axis=1)
    return {k: np.ascontiguousarray(v) for k, v in a.items()}


def kernel(**inputs):
    import concourse.bacc as bacc
    from concourse.bass_utils import run_bass_kernel_spmd

    nc = bacc.Bacc("TRN2", target_bir_lowering=False, num_devices=1)
    arrays = {f"in_{k}": v for k, v in lay_out(inputs).items()}
    w = {k.removeprefix("in_"): nc.dram_tensor(k, v.shape, mybir.dt.from_np(v.dtype), kind="ExternalInput").ap()
         for k, v in arrays.items()}
    out = nc.dram_tensor("out", (N, D), F32, kind="ExternalOutput").ap()
    build(nc, w, out)
    r = run_bass_kernel_spmd(nc, [arrays], core_ids=[0])
    return r.results[0]["out"].reshape(SEQS, T, D)
```

```python
from contextlib import ExitStack

import concourse.bass as bass
from concourse import mybir

P = 128
ALU = mybir.AluOpType
ACT = mybir.ActivationFunctionType
AX = mybir.AxisListType
F32 = mybir.dt.float32
F32R = mybir.dt.float32r
I32 = mybir.dt.int32
U32 = mybir.dt.uint32

SEQS, T = 16, 256
N = SEQS * T
TILES = N // P
D = 256
KD = D // P
LAYERS, S, F = 4, 64, 1024
FC = F // P
G = 4
GROUPS = TILES // G
GT = G * P
HEADS, DH = 16, 16
EXPERTS, LANGS = 8, 4
EPS = 1e-5
BLOCKS = 2 * N // P + EXPERTS
ds = bass.ds


ONE = 1


def start_at_one(nc, sems):
    with nc.Block() as block:
        @block.sync
        def _(sp):
            for s in sems:
                sp.sem_inc(s, ONE)


def wait_apart(eng, started, sem, value):
    value = value if isinstance(value, int) else eng.compute_val(value)
    eng.wait_ge(started, 1)
    eng.wait_ge(sem, value)


def tower(nc, started, x_res, ident, neg_half, w_qkv, w_out, attn_w_in, w):
    vocab = w["emb"].shape[0]
    with ExitStack() as ctx:
        def sb(name, shape, dt=F32):
            return ctx.enter_context(nc.sbuf_tensor(name, shape, dt))

        def psum(name):
            return ctx.enter_context(nc.psum_tensor(name, [P, 512], F32))

        sems = []

        def sem(name):
            sems.append(ctx.enter_context(nc.semaphore(name)))
            return sems[-1]

        tok_i = sb("tok_i", [P, TILES], I32)
        tok_f = sb("tok_f", [P, TILES])
        wrap = sb("wrap", [P, TILES])
        wrapped = sb("wrapped", [P, TILES])
        row = sb("row", [P, TILES], U32)
        pos_sb = sb("pos_sb", [P, T // P, D])
        b_all = sb("b_all", [P, LAYERS, KD, S])
        b_now = sb("b_now", [P, KD, S])
        c_now = sb("c_now", [P, D])
        d_now = sb("d_now", [P, KD, D])
        c_all = sb("c_all", [P, LAYERS, D])
        d_all = sb("d_all", [P, LAYERS, KD, D])
        a_raw = sb("a_raw", [P, LAYERS])
        decay = sb("decay", [P, LAYERS])
        decay_row = sb("decay_row", [P, LAYERS, T])
        b1_all = sb("b1_all", [P, LAYERS, FC])
        b2_all = sb("b2_all", [P, LAYERS, D])
        ln_par = sb("ln_par", [P, 4, LAYERS, KD])
        w1_raw = sb("w1_raw", [P, KD, F])
        w2_raw = sb("w2_raw", [P, FC, D])
        w1_hi, w1_lo = sb("w1_hi", [P, KD, F], F32R), sb("w1_lo", [P, KD, F], F32R)
        w2_hi, w2_lo = sb("w2_hi", [P, FC, D], F32R), sb("w2_lo", [P, FC, D], F32R)
        lnf_s, lnf_b = sb("lnf_s", [P, D]), sb("lnf_b", [P, D])
        NORMS = 3
        stats = [sb(f"stats{i}", [P, G, 6]) for i in range(NORMS)]
        mv = [sb(f"mean_var{i}", [P, G, 2]) for i in range(NORMS)]
        vare = [sb(f"var_eps{i}", [P, G]) for i in range(NORMS)]
        rstd = [sb(f"rstd{i}", [P, G]) for i in range(NORMS)]
        xn = [sb(f"xn{i}", [P, G, D]) for i in range(NORMS)]
        x1T = sb("x1T", [P, KD, GT])
        states = sb("states", [P, T])
        x2T = sb("x2T", [P, KD, GT])
        x2T_hi = [sb(f"x2T_hi{i}", [P, KD, GT], F32R) for i in range(2)]
        x2T_lo = [sb(f"x2T_lo{i}", [P, KD, GT], F32R) for i in range(2)]
        HB = 4
        hT = sb("hT", [P, HB, GT])
        hT_hi, hT_lo = sb("hT_hi", [P, HB, GT], F32R), sb("hT_lo", [P, HB, GT], F32R)
        ps_t = [psum(f"ps_t{i}") for i in range(2)]
        ps_y = [psum(f"ps_y{i}") for i in range(2)]
        ps_h = [psum(f"ps_h{i}") for i in range(HB)]

        gathered = [ctx.enter_context(nc.semaphore(f"gathered{g}")) for g in range(GROUPS)]
        tokens_in, pos_in, idx_step, pos_added = map(sem, ("tokens_in", "pos_in", "idx_step", "pos_added"))
        small_in, a_in, w1_in, w2_in = map(sem, ("small_in", "a_in", "w1_in", "w2_in"))
        decay_done, decay_ready = sem("decay_done"), sem("decay_ready")
        hi_done, w1_split, w2_split, ssm_w_ready = map(sem, ("w_hi_done", "w1_split", "w2_split", "ssm_w_ready"))
        w2_hi_done = sem("w2_hi_done")
        stat_done = [sem(f"stat_done{i}") for i in range(NORMS)]
        aggr_done = [sem(f"aggr_done{i}") for i in range(NORMS)]
        vare_done = [sem(f"vare_done{i}") for i in range(NORMS)]
        rstd_done = [sem(f"rstd_done{i}") for i in range(NORMS)]
        xn_done = [sem(f"xn_done{i}") for i in range(NORMS)]
        t_done = [sem(f"t_done{i}") for i in range(2)]
        x1_ready, u_done, scan_done, y_done, res1_done = map(
            sem, ("x1_ready", "u_done", "scan_done", "y_done", "res1_done"))
        b2_added, x2_evac, x2_lo_done = map(sem, ("b2_added", "x2_evac", "x2_lo_done"))
        h_done, gelu_done, h_lo_done, f_done, res2_done = map(
            sem, ("h_done", "gelu_done", "h_lo_done", "f_done", "res2_done"))
        lnf_in, scaled, fin = sem("lnf_in"), sem("final_scaled"), sem("final_ln")

        start_at_one(nc, sems)
        block = ctx.enter_context(nc.Block())

        def layer_of_bodies(eng, l, last, body):
            with eng.Fori(0, GROUPS // 2 - 1) as i:
                for p in range(2):
                    body(GROUPS * l + 2 * i + p, 2 * i + p, p, l, last)
            for p in range(2):
                g = GROUPS - 2 + p
                body(GROUPS * l + g, g, p, l, last)

        def all_bodies(eng, body, first_layer=0):
            with eng.Fori(first_layer, LAYERS - 1) as l:
                layer_of_bodies(eng, l, False, body)
            layer_of_bodies(eng, LAYERS - 1, True, body)

        def after(g, steps, last):
            if isinstance(g, int) and g + steps >= GROUPS:
                return None if last else g + steps - GROUPS
            return g + steps

        def next_layer(g, l):
            return l + 1 if isinstance(g, int) and g == GROUPS - 1 else l

        @block.sync
        def _(sp):
            sp.dma_start(tok_i[:], w["tokens"]).then_inc(tokens_in, 16)
            sp.dma_start(pos_sb[:], w["pos_emb"][0:T, :].rearrange("(j p) d -> p j d", p=P)).then_inc(pos_in, 16)
            sp.dma_start(a_raw[:], w["A_diag"]).then_inc(a_in, 16)
            small = [(b_all[:, l], w["B"][l].rearrange("(k p) s -> p k s", p=P)) for l in range(LAYERS)]
            small += [(c_all[64 * h:64 * h + 64, :, :], w["C"].rearrange("l s d -> s l d")) for h in range(2)]
            small += [(d_all[:, l], w["D"][l].rearrange("(k p) e -> p k e", p=P)) for l in range(LAYERS)]
            small += [(b1_all[:], w["b1"]), (ln_par[:], w["ln_par"]),
                      (b2_all[:], w["b2"].rearrange("(o l) d -> o l d", o=1).to_broadcast([P, LAYERS, D]))]
            for dst, src in small:
                sp.dma_start(dst, src).then_inc(small_in, 16)
            with sp.Fori(0, LAYERS) as l:
                sp.wait_ge(w1_split, ONE + l)
                sp.dma_start(w1_raw[:], w["w1"][ds(l, 1)].rearrange("o (k p) f -> p (o k) f", p=P)).then_inc(w1_in, 16)
                sp.wait_ge(w2_split, ONE + l)
                sp.dma_start(w2_raw[:], w["w2"][ds(l, 1)].rearrange("o (c p) d -> p (o c) d", p=P)).then_inc(w2_in, 16)
            sp.dma_start(w_qkv[:], w["w_qkvT"].rearrange("(k p) f -> p k f", p=P)).then_inc(attn_w_in, 16)
            sp.dma_start(w_out[:], w["w_outT"].rearrange("(k p) f -> p k f", p=P)).then_inc(attn_w_in, 16)
            for dst, name in ((lnf_s, "lnf_s"), (lnf_b, "lnf_b")):
                sp.dma_start(dst[:], w[name].rearrange("(o d) -> o d", o=1).to_broadcast([P, D])).then_inc(lnf_in, 16)

        SMALL = 16 * (LAYERS * 2 + 2 + 3)

        @block.tensor
        def _(pe):
            def turn(i, n):
                pe.wait_ge(xn_done[i], ONE + G * (n + 1))
                for k in range(KD):
                    for j in range(G):
                        last = pe.transpose(ps_t[k][:, P * j:P * j + P], xn[i][:, j, P * k:P * k + P], ident)
                last.then_inc(t_done[i], 1)

            def turn1(n):
                pe.wait_ge(x2_evac, ONE + 2 * KD * n)
                turn(0, n)

            def drive(n):
                pe.wait_ge(x1_ready, ONE + KD * (n + 1))
                for q in range(2):
                    for k in range(KD):
                        last = pe.matmul(ps_t[0][S * q:S * q + S, 0:T], b_now[:, k, :],
                                         x1T[:, k, T * q:T * q + T], start=(k == 0), stop=(k == KD - 1))
                last.then_inc(u_done, 1)

            def ssm_out(n):
                pe.wait_ge(scan_done, ONE + n + 1)
                for j in range(G):
                    out = ps_t[j // 2][:, D * (j % 2):D * (j % 2) + D]
                    q, i0 = j // 2, P * (j % 2)
                    for k in range(KD):
                        pe.matmul(out, x1T[:, k, P * j:P * j + P], d_now[:, k, :], start=(k == 0), stop=False)
                    last = pe.matmul(out, states[S * q:S * q + S, i0:i0 + P],
                                     c_now[S * q:S * q + S, :], start=False, stop=True)
                last.then_inc(y_done, 1)

            def turn2(n):
                pe.wait_ge(res1_done, ONE + 2 * (n + 1))
                turn(1, n)

            def up(n, p, c):
                if c == 0:
                    pe.wait_ge(x2_lo_done, ONE + KD * (n + 1))
                passes = [(w1_hi, x2T_hi[p]), (w1_hi, x2T_lo[p]), (w1_lo, x2T_hi[p])]
                for k in range(KD):
                    for i, (a, b) in enumerate(passes):
                        last = pe.matmul(ps_h[c % HB][:], a[:, k, P * c:P * c + P], b[:, k, :],
                                         start=(k == 0 and i == 0), stop=(k == KD - 1 and i == 2))
                last.then_inc(h_done, 1)

            def down(n, l, c):
                if c == 0:
                    pe.wait_ge(res2_done, ONE + 2 * n)
                    wait_apart(pe, started, w2_split, ONE + l + 1)
                pe.wait_ge(h_lo_done, ONE + FC * n + c + 1)
                for j in range(G):
                    out = ps_y[j // 2][:, D * (j % 2):D * (j % 2) + D]
                    tok = slice(P * j, P * j + P)
                    for i, (a, b) in enumerate([(hT_hi, w2_hi), (hT_hi, w2_lo), (hT_lo, w2_hi)]):
                        last = pe.matmul(out, a[:, c % HB, tok], b[:, c, :],
                                         start=(c == 0 and i == 0 and j % 2 == 0), stop=(c == FC - 1 and i == 2),
                                         skip_group_check=True)
                if c == FC - 1:
                    last.then_inc(f_done, 1)

            def body(n, g, p, l, last):
                more = after(g, 1, last) is not None
                if more:
                    turn1(n + 1)
                up(n, p, 2)
                down(n, l, 0)
                if more:
                    if next_layer(g, l) is not l:
                        pe.wait_ge(ssm_w_ready, ONE + 3 * (l + 2))
                    drive(n + 1)
                up(n, p, 3)
                if more:
                    ssm_out(n + 1)
                down(n, l, 1)
                up(n, p, 4)
                down(n, l, 2)
                up(n, p, 5)
                down(n, l, 3)
                up(n, p, 6)
                if more:
                    turn2(n + 1)
                down(n, l, 4)
                up(n, p, 7)
                down(n, l, 5)
                if more:
                    if next_layer(g, l) is not l:
                        pe.wait_ge(w1_split, ONE + l + 2)
                    up(n + 1, 1 - p, 0)
                down(n, l, 6)
                if more:
                    up(n + 1, 1 - p, 1)
                down(n, l, 7)

            pe.wait_ge(small_in, ONE + SMALL)
            turn1(0)
            pe.wait_ge(ssm_w_ready, ONE + 3)
            drive(0)
            ssm_out(0)
            turn2(0)
            pe.wait_ge(w1_split, ONE + 1)
            up(0, 0, 0)
            up(0, 0, 1)
            all_bodies(pe, body)

        @block.vector
        def _(dve):
            def statistics(i, n, g):
                for j in range(G):
                    dve.bn_stats(stats[i][:, j, :], x_res[:, ds(G * g + j, 1), :]).then_inc(stat_done[i], 1)
                wait_apart(dve, started, stat_done[i], ONE + G * (n + 1))
                for j in range(G):
                    dve.bn_aggr(mv[i][:, j, :], stats[i][:, j, :]).then_inc(aggr_done[i], 1)
                dve.wait_ge(aggr_done[i], ONE + G * (n + 1))
                dve.wait_ge(rstd_done[i], ONE + n)
                dve.tensor_scalar(vare[i][:], mv[i][:, :, 1], EPS, None, ALU.add).then_inc(vare_done[i], 1)

            def normalise(i, n, g):
                dve.wait_ge(rstd_done[i], ONE + n + 1)
                if i < 2:
                    dve.wait_ge(t_done[i], ONE + n)
                else:
                    dve.wait_ge(fin, ONE + n)
                for j in range(G):
                    dve.tensor_scalar(xn[i][:, j, :], x_res[:, ds(G * g + j, 1), :].rearrange("p o d -> p (o d)"),
                                      mv[i][:, j, 0:1], rstd[i][:, j:j + 1], ALU.subtract, ALU.mult)\
                       .then_inc(xn_done[i], 1)

            def statistics1(n, g):
                wait_apart(dve, started, pos_added, ONE + g + 1)
                statistics(0, n, g)

            def scan(n, l):
                dve.wait_ge(u_done, ONE + n + 1)
                dve.wait_ge(y_done, ONE + n)
                dve.tensor_tensor_scan(states[:], decay_row[:, ds(l, 1), :].rearrange("p o t -> p (o t)"),
                                       ps_t[0][:, 0:T], 0.0, ALU.mult, ALU.add).then_inc(scan_done, 1)

            def add_pair(ps, done, g):
                for h in range(2):
                    pair = x_res[:, ds(G * g + 2 * h, 2), :]
                    dve.tensor_tensor(pair, ps[h][:].rearrange("p (j d) -> p j d", j=2), pair, ALU.add)\
                       .then_inc(done, 1)

            def residual1(n, g):
                dve.wait_ge(y_done, ONE + n + 1)
                add_pair(ps_t, res1_done, g)
                wait_apart(dve, started, res1_done, ONE + 2 * (n + 1))
                statistics(1, n, g)

            def x2_rest(n, p):
                for k in range(KD):
                    dve.wait_ge(x2_evac, ONE + 2 * KD * n + 2 * (k + 1))
                    dve.tensor_tensor(x2T_lo[p][:, k, :], x2T[:, k, :], x2T_hi[p][:, k, :].bitcast(F32), ALU.subtract)\
                       .then_inc(x2_lo_done, 1)

            def h_rest(n, c):
                b = c % HB
                dve.wait_ge(gelu_done, ONE + 2 * (FC * n + c + 1))
                dve.tensor_tensor(hT_lo[:, b, :], hT[:, b, :], hT_hi[:, b, :].bitcast(F32), ALU.subtract)\
                   .then_inc(h_lo_done, 1)

            def residual2(n, g):
                dve.wait_ge(f_done, ONE + n + 1)
                dve.wait_ge(b2_added, ONE + n + 1)
                add_pair(ps_y, res2_done, g)

            def body(n, g, p, l, last):
                g1, g2 = after(g, 1, last), after(g, 2, last)
                h_rest(n, 2)
                if g1 is not None:
                    scan(n + 1, next_layer(g, l))
                h_rest(n, 3)
                if g1 is not None:
                    residual1(n + 1, g1)
                h_rest(n, 4)
                if g1 is not None:
                    normalise(1, n + 1, g1)
                h_rest(n, 5)
                if g2 is not None:
                    wait_apart(dve, started, res2_done, ONE + 2 * n)
                    statistics1(n + 2, g2)
                h_rest(n, 6)
                if g1 is not None:
                    x2_rest(n + 1, 1 - p)
                h_rest(n, 7)
                if g2 is not None:
                    normalise(0, n + 2, g2)
                if g1 is not None:
                    h_rest(n + 1, 0)
                residual2(n, g)
                if last:
                    wait_apart(dve, started, res2_done, ONE + 2 * (n + 1))
                    statistics(2, g, g)
                if g1 is not None:
                    h_rest(n + 1, 1)
                if last:
                    normalise(2, g, g)

            dve.wait_ge(tokens_in, ONE + 16)
            dve.tensor_copy(tok_f[:], tok_i[:]).then_inc(idx_step, 1)
            dve.wait_ge(idx_step, ONE + 1)
            dve.tensor_scalar(wrap[:], tok_f[:], 0.0, float(vocab), ALU.is_lt, ALU.mult).then_inc(idx_step, 1)
            dve.wait_ge(idx_step, ONE + 2)
            dve.tensor_tensor(wrapped[:], tok_f[:], wrap[:], ALU.add).then_inc(idx_step, 1)
            dve.wait_ge(idx_step, ONE + 3)
            dve.tensor_scalar(row[:], wrapped[:], 0.0, float(vocab - 1), ALU.max, ALU.min).then_inc(idx_step, 1)
            dve.memset(decay_row[:], 1.0).then_inc(decay_ready, 1)
            dve.wait_ge(decay_done, ONE + 1)
            dve.wait_ge(decay_ready, ONE + 1)
            for l in range(LAYERS):
                dve.tensor_scalar(decay_row[:, l, :], decay_row[:, l, :], decay[:, l:l + 1], None, ALU.mult)\
                   .then_inc(decay_ready, 1)
            dve.wait_ge(decay_ready, ONE + 1 + LAYERS)
            statistics1(0, 0)
            normalise(0, 0, 0)
            dve.wait_ge(w1_in, ONE + 16)
            dve.tensor_copy(w1_hi[:], w1_raw[:]).then_inc(hi_done, 1)
            dve.wait_ge(hi_done, ONE + 1)
            dve.tensor_tensor(w1_lo[:], w1_raw[:], w1_hi[:].bitcast(F32), ALU.subtract).then_inc(w1_split, 1)
            scan(0, 0)
            residual1(0, 0)
            normalise(1, 0, 0)
            x2_rest(0, 0)
            statistics1(1, 1)
            normalise(0, 1, 1)
            dve.wait_ge(w2_hi_done, ONE + 1)
            dve.tensor_tensor(w2_lo[:], w2_raw[:], w2_hi[:].bitcast(F32), ALU.subtract).then_inc(w2_split, 1)
            h_rest(0, 0)
            h_rest(0, 1)
            all_bodies(dve, body)

        @block.scalar
        def _(act):
            def turned1(n, l):
                wait_apart(act, started, t_done[0], ONE + n + 1)
                wait_apart(act, started, y_done, ONE + n)
                for k in range(KD):
                    act.activation(x1T[:, k, :], ps_t[k][:], ACT.Identity, scale=ln_par[:, 0, ds(l, 1), k],
                                   bias=ln_par[:, 1, ds(l, 1), k]).then_inc(x1_ready, 1)

            def turned2(n, p, l):
                wait_apart(act, started, t_done[1], ONE + n + 1)
                wait_apart(act, started, x2_lo_done, ONE + KD * n)
                for k in range(KD):
                    for dst in (x2T, x2T_hi[p]):
                        act.activation(dst[:, k, :], ps_t[k][:], ACT.Identity, scale=ln_par[:, 2, ds(l, 1), k],
                                       bias=ln_par[:, 3, ds(l, 1), k]).then_inc(x2_evac, 1)

            def gelu(n, l, c):
                wait_apart(act, started, h_done, ONE + FC * n + c + 1)
                for dst in (hT, hT_hi):
                    act.activation(dst[:, c % HB, :], ps_h[c % HB][:], ACT.Gelu, bias=b1_all[:, ds(l, 1), c])\
                       .then_inc(gelu_done, 1)

            def body(n, g, p, l, last):
                more = after(g, 1, last) is not None
                if more:
                    turned1(n + 1, next_layer(g, l))
                for c in range(2, FC - 1):
                    gelu(n, l, c)
                if more:
                    turned2(n + 1, 1 - p, next_layer(g, l))
                gelu(n, l, FC - 1)
                if more:
                    for c in range(2):
                        gelu(n + 1, next_layer(g, l), c)

            act.wait_ge(a_in, ONE + 16)
            act.activation(decay[:], a_raw[:], ACT.Sigmoid).then_inc(decay_done, 1)
            act.wait_ge(small_in, ONE + SMALL)
            turned1(0, 0)
            act.wait_ge(w2_in, ONE + 16)
            act.activation(w2_hi[:], w2_raw[:], ACT.Copy).then_inc(w2_hi_done, 1)
            turned2(0, 0, 0)
            for c in range(2):
                gelu(0, 0, c)
            all_bodies(act, body)

        @block.gpsimd
        def _(pool):
            def gather(g):
                for t in range(G * g, G * g + G):
                    pool.indirect_dma_start(
                        out=x_res[:, t, :], out_offset=None, in_=w["emb"],
                        in_offset=bass.IndirectOffsetOnAxis(ap=row[:, t:t + 1], axis=0),
                    ).then_inc(gathered[g], 16)

            def add_pos(g):
                pool.wait_ge(gathered[g], 16 * G)
                group = x_res[:, G * g:G * g + G, :].rearrange("p (s j) d -> p s j d", j=T // P)
                pool.tensor_tensor(group, group, pos_sb[:].unsqueeze(1).to_broadcast([P, GT // T, T // P, D]), ALU.add)\
                    .then_inc(pos_added, 1)

            def root(i, n):
                pool.wait_ge(vare_done[i], ONE + n + 1)
                pool.wait_ge(xn_done[i], ONE + G * n)
                pool.tensor_tensor(rstd[i][:], vare[i][:], neg_half[:, 0:G], ALU.pow).then_inc(rstd_done[i], 1)

            def add_b2(n, l, g):
                pool.wait_ge(xn_done[1], ONE + G * (n + 1))
                part = x_res[:, ds(G * g, G), :]
                pool.tensor_tensor(part, part, b2_all[:, ds(l, 1), :].to_broadcast([P, G, D]), ALU.add)\
                    .then_inc(b2_added, 1)

            def ssm_weights(n, l):
                wait_apart(pool, started, y_done, ONE + n)
                pool.tensor_copy(b_now[:].unsqueeze(1), b_all[:, ds(l, 1)]).then_inc(ssm_w_ready, 1)
                pool.tensor_copy(c_now[:].unsqueeze(1), c_all[:, ds(l, 1)]).then_inc(ssm_w_ready, 1)
                pool.tensor_copy(d_now[:].unsqueeze(1), d_all[:, ds(l, 1)]).then_inc(ssm_w_ready, 1)

            LAG = 3

            def split(n, l, c):
                parts = []
                if c < FC:
                    chunk = slice(P * c, P * c + P)
                    parts.append((w1_raw[:, :, chunk], w1_hi[:, :, chunk], w1_lo[:, :, chunk], c == FC - 1, w1_split))
                if c >= LAG:
                    d = c - LAG
                    parts.append((w2_raw[:, d, :], w2_hi[:, d, :], w2_lo[:, d, :], d == FC - 1, w2_split))
                if c <= FC + 1:
                    wait_apart(pool, started, h_done, ONE + FC * n + c + 1)
                else:
                    wait_apart(pool, started, f_done, ONE + n + 1)
                for raw, hi, _, _, _ in parts:
                    pool.tensor_copy(hi, raw).then_inc(hi_done, 1)
                wait_apart(pool, started, hi_done, ONE + 1 + 2 * FC * (l - 1) + min(c + 1, FC) + max(0, c + 1 - LAG))
                for raw, hi, lo, final, done in parts:
                    ins = pool.tensor_tensor(lo, raw, hi.bitcast(F32), ALU.subtract)
                    if final:
                        ins.then_inc(done, 1)

            def body(n, g, p, l, last):
                g1, g2 = after(g, 1, last), after(g, 2, last)
                turning = g1 is not None and next_layer(g, l) is not l
                if isinstance(l, int) and l == 0:
                    if g + 2 < GROUPS:
                        add_pos(g + 2)
                    if g + 4 < GROUPS:
                        gather(g + 4)
                if turning:
                    ssm_weights(n + 1, l + 1)
                    pool.wait_ge(w1_in, ONE + 16 * (l + 2))
                    pool.wait_ge(w2_in, ONE + 16 * (l + 2))
                    for c in range(5):
                        split(n, l + 1, c)
                if g1 is not None:
                    root(1, n + 1)
                if turning:
                    split(n, l + 1, 5)
                elif g1 is not None:
                    add_b2(n + 1, l, g1)
                if g2 is not None:
                    root(0, n + 2)
                if turning:
                    for c in range(6, FC):
                        split(n, l + 1, c)
                    add_b2(n + 1, l + 1, g1)
                    for c in range(FC, FC + LAG):
                        split(n, l + 1, c)
                if last:
                    root(2, g)
                    pool.wait_ge(xn_done[2], ONE + G * (g + 1))
                    pool.tensor_tensor(xn[2][:], xn[2][:], lnf_s[:].unsqueeze(1).to_broadcast([P, G, D]), ALU.mult)\
                        .then_inc(scaled, 1)
                    wait_apart(pool, started, scaled, ONE + g + 1)
                    pool.tensor_tensor(x_res[:, ds(G * g, G), :], xn[2][:],
                                       lnf_b[:].unsqueeze(1).to_broadcast([P, G, D]), ALU.add).then_inc(fin, 1)

            pool.wait_ge(idx_step, ONE + 4)
            gather(0)
            gather(1)
            pool.wait_ge(pos_in, ONE + 16)
            add_pos(0)
            pool.wait_ge(small_in, ONE + SMALL)
            ssm_weights(0, 0)
            root(0, 0)
            add_pos(1)
            gather(2)
            root(1, 0)
            add_b2(0, 0, 0)
            root(0, 1)
            gather(3)
            for g in range(GROUPS):
                body(g, g, g % 2, 0, False)
            with pool.Fori(1, LAYERS - 1) as l:
                layer_of_bodies(pool, l, False, body)
            pool.wait_ge(lnf_in, ONE + 32)
            layer_of_bodies(pool, LAYERS - 1, True, body)
            pool.wait_ge(fin, ONE + GROUPS)


def attention(nc, started, x_res, ident, neg_half, w_qkv, w_out, w_in):
    ST = T // P
    QUAD = 4
    DV = 32
    QUADS = HEADS // QUAD
    HC = HEADS * DH // P
    PER = P // DH
    with ExitStack() as ctx:
        def sb(name, shape, dt=F32):
            return ctx.enter_context(nc.sbuf_tensor(name, shape, dt))

        def psum(name):
            return ctx.enter_context(nc.psum_tensor(name, [P, 512], F32))

        sems = []

        def sem(name):
            sems.append(ctx.enter_context(nc.semaphore(name)))
            return sems[-1]

        blocks = sb("blocks", [P, PER])
        q_mask = sb("q_mask", [P, 2])
        stats, mv = sb("a_stats", [P, ST, 6]), sb("a_mv", [P, ST, 2])
        vare, rstd = sb("a_vare", [P, ST]), sb("a_rstd", [P, ST])
        xn = sb("a_xn", [P, ST, D])
        xT = sb("a_xT", [P, KD, T])
        q = [[sb(f"q{p}{i}", [P, HC, T]) for i in range(2)] for p in range(2)]
        kT = [sb(f"kT{p}", [P, HC, T]) for p in range(2)]
        v = [sb(f"v{p}", [P, ST, HEADS, DV]) for p in range(2)]
        nmax = [sb(f"nmax{i}", [P, ST]) for i in range(2)]
        prob = [sb(f"prob{i}", [P, ST, T]) for i in range(2)]
        probT = [sb(f"probT{i}", [P, ST, T]) for i in range(2)]
        oT = sb("oT", [P, T])
        rsum = sb("rsum", [P, ST, QUAD])
        o_norm = sb("o_norm", [P, ST, D])
        onT = sb("onT", [P, KD, T])
        ps_s = [psum(f"ps_s{i}") for i in range(2)]
        ps_pt = [psum(f"ps_pt{i}") for i in range(2)]
        ps_p = [psum(f"ps_p{i}") for i in range(2)]
        ps_o, ps_f = psum("ps_o"), psum("ps_f")

        mask_step, v_init = sem("mask_step"), sem("v_init")
        stat_done, aggr_done, vare_done, rstd_done, xn_done = map(
            sem, ("a_stat_done", "a_aggr_done", "a_vare_done", "a_rstd_done", "a_xn_done"))
        xt_done, xt_evac, q_done, q_evac, k_done, k_evac, v_done, v_evac = map(
            sem, ("xt_done", "xt_evac", "q_done", "q_evac", "k_done", "k_evac", "v_done", "v_evac"))
        s_done, nmax_done, exp_done, pt_done, pt_evac, pv_done = map(
            sem, ("s_done", "nmax_done", "exp_done", "pt_done", "pt_evac", "pv_done"))
        ot_evac, to_done, rsum_done, norm_done = map(sem, ("ot_evac", "to_done", "rsum_done", "norm_done"))
        on_done, on_evac, out_done, res_done = map(sem, ("on_done", "on_evac", "out_done", "a_res_done"))

        start_at_one(nc, sems)
        block = ctx.enter_context(nc.Block())

        def over_sequences(eng, run):
            run(0, 0, True, False)
            with eng.Fori(0, SEQS // 2 - 1) as i:
                run(2 * i + 1, 1, False, False)
                run(2 * i + 2, 0, False, False)
            run(SEQS - 1, 1, False, True)

        @block.gpsimd
        def _(pool):
            pool.memset(blocks[:], 1.0 / DH ** 0.5).then_inc(mask_step, 1)
            pool.wait_ge(mask_step, ONE + 1)
            pool.affine_select(out=blocks[:], in_=blocks[:], compare_op=ALU.is_ge, fill=0.0, base=0,
                               pattern=[[-DH, PER]], channel_multiplier=1).then_inc(mask_step, 1)
            pool.wait_ge(mask_step, ONE + 2)
            pool.affine_select(out=blocks[:], in_=blocks[:], compare_op=ALU.is_ge, fill=0.0, base=DH - 1,
                               pattern=[[DH, PER]], channel_multiplier=-1).then_inc(mask_step, 1)
            for p in range(2):
                pool.memset(v[p][:], 0.0).then_inc(v_init, 1)
            pool.wait_ge(v_init, ONE + 2)
            for p in range(2):
                pool.memset(v[p][:, :, :, DH:DH + 1], 1.0).then_inc(v_init, 1)

            def root(b):
                pool.wait_ge(vare_done, ONE + b + 1)
                pool.wait_ge(xn_done, ONE + ST * b)
                pool.tensor_tensor(rstd[:], vare[:], neg_half[:, 0:ST], ALU.pow).then_inc(rstd_done, 1)

            root(0)
            with pool.Fori(0, SEQS - 1) as b:
                root(b + 1)

        @block.tensor
        def _(pe):
            def turn_x(b):
                pe.wait_ge(xn_done, ONE + ST * (b + 1))
                pe.wait_ge(k_evac, ONE + b)
                for k in range(KD):
                    for j in range(ST):
                        last = pe.transpose(ps_p[0][:, T * k + P * j:T * k + P * j + P],
                                            xn[:, j, P * k:P * k + P], ident)
                last.then_inc(xt_done, 1)

            def project(bank, f0, done):
                for c in range(HC):
                    for k in range(KD):
                        last = pe.matmul(ps_p[bank][:, T * c:T * c + T], w_qkv[:, k, f0 + P * c:f0 + P * c + P],
                                         xT[:, k, :], start=(k == 0), stop=(k == KD - 1))
                last.then_inc(done, 1)

            def project_q(b):
                pe.wait_ge(xt_evac, ONE + b + 1)
                pe.wait_ge(v_evac, ONE + b)
                project(1, 0, q_done)

            def project_k(b):
                project(0, D, k_done)

            def project_v(b):
                pe.wait_ge(q_evac, ONE + 2 * (b + 1))
                for j in range(ST):
                    for k in range(KD):
                        last = pe.matmul(ps_p[1][:, D * j:D * j + D], xT[:, k, P * j:P * j + P],
                                         w_qkv[:, k, 2 * D:3 * D], start=(k == 0), stop=(k == KD - 1))
                last.then_inc(v_done, 1)

            def scores(b, p, h):
                m = HEADS * b + h
                if h == 0:
                    pe.wait_ge(q_evac, ONE + 2 * (b + 1))
                    pe.wait_ge(k_evac, ONE + b + 1)
                c, rows = h // PER, slice(DV * (h % PER // 2), DV * (h % PER // 2) + DV)
                for i in range(ST):
                    last = pe.matmul(ps_s[h % 2][:, T * i:T * i + T], q[p][h % 2][rows, c, P * i:P * i + P],
                                     kT[p][rows, c, :], start=True, stop=True)
                last.then_inc(s_done, 1)

            def turn_probs(b, h):
                pe.wait_ge(exp_done, ONE + ST * (HEADS * b + h + 1))
                for j in range(ST):
                    for i in range(ST):
                        last = pe.transpose(ps_pt[h % 2][:, T * j + P * i:T * j + P * i + P],
                                            prob[h % 2][:, i, P * j:P * j + P], ident)
                last.then_inc(pt_done, 1)

            def weigh(b, p, h):
                pe.wait_ge(pt_evac, ONE + HEADS * b + h + 1)
                if h == 0:
                    pe.wait_ge(v_evac, ONE + b + 1)
                if h % QUAD == 0:
                    pe.wait_ge(ot_evac, ONE + QUADS * b + h // QUAD)
                rows = slice(DV * (h % QUAD), DV * (h % QUAD) + DV)
                for j in range(ST):
                    last = pe.matmul(ps_o[rows, 0:T], v[p][:, j, h, :], probT[h % 2][:, j, :],
                                     start=(j == 0), stop=(j == ST - 1))
                if h % QUAD == QUAD - 1:
                    last.then_inc(pv_done, 1)

            def turn_quad(b, u):
                pe.wait_ge(ot_evac, ONE + QUADS * b + u + 1)
                if u == 0:
                    pe.wait_ge(res_done, ONE + b)
                else:
                    pe.wait_ge(norm_done, ONE + QUADS * b + u)
                for i in range(ST):
                    last = pe.transpose(ps_f[:, P * i:P * i + P], oT[:, P * i:P * i + P], ident)
                last.then_inc(to_done, 1)

            def turn_out(b):
                pe.wait_ge(norm_done, ONE + QUADS * (b + 1))
                for k in range(KD):
                    for i in range(ST):
                        last = pe.transpose(ps_f[:, T * k + P * i:T * k + P * i + P],
                                            o_norm[:, i, P * k:P * k + P], ident)
                last.then_inc(on_done, 1)

            def project_out(b):
                pe.wait_ge(on_evac, ONE + b + 1)
                for i in range(ST):
                    for k in range(KD):
                        last = pe.matmul(ps_f[:, D * i:D * i + D], onT[:, k, P * i:P * i + P], w_out[:, k, :],
                                         start=(k == 0), stop=(k == KD - 1))
                last.then_inc(out_done, 1)

            def sequence(b, p, first, last):
                for h in range(HEADS):
                    turn_probs(b, h)
                    if h + 2 < HEADS:
                        scores(b, p, h + 2)
                    elif not last:
                        scores(b + 1, 1 - p, h + 2 - HEADS)
                    if h:
                        weigh(b, p, h - 1)
                    elif not first:
                        weigh(b - 1, 1 - p, HEADS - 1)
                    if h % QUAD == 1 and h > QUAD:
                        turn_quad(b, h // QUAD - 1)
                    if not first:
                        if h == 1:
                            turn_quad(b - 1, QUADS - 1)
                        if h == 3:
                            turn_out(b - 1)
                        if h == 4:
                            project_out(b - 1)
                    if not last:
                        if h == 2:
                            turn_x(b + 1)
                        if h == 5:
                            project_q(b + 1)
                        if h == 7:
                            project_k(b + 1)
                        if h == 9:
                            project_v(b + 1)

            pe.wait_ge(w_in, 32)
            turn_x(0)
            project_q(0)
            project_k(0)
            project_v(0)
            scores(0, 0, 0)
            scores(0, 0, 1)
            pe.wait_ge(v_init, ONE + 4)
            over_sequences(pe, sequence)
            weigh(SEQS - 1, 1, HEADS - 1)
            turn_quad(SEQS - 1, QUADS - 1)
            turn_out(SEQS - 1)
            project_out(SEQS - 1)

        @block.vector
        def _(dve):
            def statistics(b):
                for j in range(ST):
                    dve.bn_stats(stats[:, j, :], x_res[:, ds(ST * b + j, 1), :]).then_inc(stat_done, 1)
                wait_apart(dve, started, stat_done, ONE + ST * (b + 1))
                for j in range(ST):
                    dve.bn_aggr(mv[:, j, :], stats[:, j, :]).then_inc(aggr_done, 1)
                dve.wait_ge(aggr_done, ONE + ST * (b + 1))
                dve.wait_ge(rstd_done, ONE + b)
                dve.tensor_scalar(vare[:], mv[:, :, 1], EPS, None, ALU.add).then_inc(vare_done, 1)

            def normalise(b):
                dve.wait_ge(rstd_done, ONE + b + 1)
                dve.wait_ge(xt_done, ONE + b)
                for j in range(ST):
                    dve.tensor_scalar(xn[:, j, :], x_res[:, ds(ST * b + j, 1), :].rearrange("p o d -> p (o d)"),
                                      mv[:, j, 0:1], rstd[:, j:j + 1], ALU.subtract, ALU.mult).then_inc(xn_done, 1)

            def row_max(b, h):
                m = HEADS * b + h
                dve.wait_ge(s_done, ONE + m + 1)
                dve.tensor_reduce(nmax[h % 2][:], ps_s[h % 2][:].rearrange("p (i j) -> p i j", i=ST), AX.X, ALU.max,
                                  negate=True).then_inc(nmax_done, 1)

            def probs_out(b, h):
                dve.wait_ge(pt_done, ONE + HEADS * b + h + 1)
                dve.tensor_copy(probT[h % 2][:].rearrange("p j i -> p (j i)"), ps_pt[h % 2][:]).then_inc(pt_evac, 1)

            def divide(b, u):
                n = QUADS * b + u
                quad = ps_f[:, 0:T].rearrange("p (i h e) -> p i h e", i=ST, h=QUAD)
                dve.wait_ge(to_done, ONE + n + 1)
                dve.reciprocal(rsum[:].unsqueeze(3), quad[:, :, :, DH:DH + 1]).then_inc(rsum_done, 1)
                dve.wait_ge(rsum_done, ONE + n + 1)
                if u == 0:
                    dve.wait_ge(on_done, ONE + b)
                dve.tensor_tensor(o_norm[:, :, QUAD * DH * u:QUAD * DH * (u + 1)].rearrange("p i (h e) -> p i h e", h=QUAD),
                                  quad[:, :, :, 0:DH], rsum[:].unsqueeze(3).to_broadcast([P, ST, QUAD, DH]),
                                  ALU.mult).then_inc(norm_done, 1)

            def residual(b):
                dve.wait_ge(out_done, ONE + b + 1)
                pair = x_res[:, ds(ST * b, ST), :]
                dve.tensor_tensor(pair, ps_f[:].rearrange("p (j d) -> p j d", j=ST), pair, ALU.add)\
                   .then_inc(res_done, 1)

            def sequence(b, p, first, last):
                for h in range(HEADS):
                    probs_out(b, h)
                    if h + 2 < HEADS:
                        row_max(b, h + 2)
                    elif not last:
                        row_max(b + 1, h + 2 - HEADS)
                    if h % QUAD == 1 and h > QUAD:
                        divide(b, h // QUAD - 1)
                    if not first:
                        if h == 1:
                            divide(b - 1, QUADS - 1)
                        if h == 4:
                            residual(b - 1)
                    if not last:
                        if h == 0:
                            statistics(b + 1)
                        if h == 1:
                            normalise(b + 1)

            dve.wait_ge(mask_step, ONE + 3)
            for i in range(2):
                dve.tensor_reduce(q_mask[:, i:i + 1], blocks[:, i::2], AX.X, ALU.add).then_inc(mask_step, 1)
            statistics(0)
            normalise(0)
            row_max(0, 0)
            row_max(0, 1)
            over_sequences(dve, sequence)
            divide(SEQS - 1, QUADS - 1)
            residual(SEQS - 1)
            dve.wait_ge(res_done, ONE + SEQS)

        @block.scalar
        def _(act):
            def x_out(b):
                act.wait_ge(xt_done, ONE + b + 1)
                act.wait_ge(v_done, ONE + b)
                act.activation(xT[:].rearrange("p k t -> p (k t)"), ps_p[0][:], ACT.Copy).then_inc(xt_evac, 1)

            def q_out(b, p):
                act.wait_ge(q_done, ONE + b + 1)
                for i in range(2):
                    act.activation(q[p][i][:].rearrange("p c t -> p (c t)"), ps_p[1][:], ACT.Copy,
                                   scale=q_mask[:, i:i + 1]).then_inc(q_evac, 1)

            def k_out(b, p):
                act.wait_ge(k_done, ONE + b + 1)
                act.activation(kT[p][:].rearrange("p c t -> p (c t)"), ps_p[0][:], ACT.Copy).then_inc(k_evac, 1)

            def v_out(b, p):
                act.wait_ge(v_done, ONE + b + 1)
                act.activation(v[p][:, :, :, 0:DH], ps_p[1][:].rearrange("p (j h e) -> p j h e", j=ST, h=HEADS),
                               ACT.Copy).then_inc(v_evac, 1)

            def exponentials(b, h):
                act.wait_ge(nmax_done, ONE + HEADS * b + h + 1)
                for i in range(ST):
                    act.activation(prob[h % 2][:, i, :], ps_s[h % 2][:, T * i:T * i + T], ACT.Exp,
                                   bias=nmax[h % 2][:, i:i + 1]).then_inc(exp_done, 1)

            def quad_out(b, u):
                n = QUADS * b + u
                act.wait_ge(pv_done, ONE + n + 1)
                act.wait_ge(to_done, ONE + n)
                act.activation(oT[:], ps_o[:, 0:T], ACT.Copy).then_inc(ot_evac, 1)

            def out_out(b):
                act.wait_ge(on_done, ONE + b + 1)
                act.wait_ge(out_done, ONE + b)
                act.activation(onT[:].rearrange("p k t -> p (k t)"), ps_f[:], ACT.Copy).then_inc(on_evac, 1)

            def sequence(b, p, first, last):
                for h in range(HEADS):
                    if h + 2 < HEADS:
                        exponentials(b, h + 2)
                    elif not last:
                        exponentials(b + 1, h + 2 - HEADS)
                    if h % QUAD == 0 and h:
                        quad_out(b, h // QUAD - 1)
                    if not first:
                        if h == 0:
                            quad_out(b - 1, QUADS - 1)
                        if h == 3:
                            out_out(b - 1)
                    if not last:
                        if h == 2:
                            x_out(b + 1)
                        if h == 5:
                            q_out(b + 1, 1 - p)
                        if h == 7:
                            k_out(b + 1, 1 - p)
                        if h == 9:
                            v_out(b + 1, 1 - p)

            act.wait_ge(mask_step, ONE + 5)
            act.wait_ge(v_init, ONE + 4)
            x_out(0)
            q_out(0, 0)
            k_out(0, 0)
            v_out(0, 0)
            exponentials(0, 0)
            exponentials(0, 1)
            over_sequences(act, sequence)
            quad_out(SEQS - 1, QUADS - 1)
            out_out(SEQS - 1)


def route(nc, started, x_res, xn_dram, ident, neg_half, w, r):
    E, L = EXPERTS, LANGS
    with ExitStack() as ctx:
        def sb(name, shape, dt=F32):
            return ctx.enter_context(nc.sbuf_tensor(name, shape, dt))

        def psum(name, cols=512):
            return ctx.enter_context(nc.psum_tensor(name, [P, cols], F32))

        sems = []

        def sem(name):
            sems.append(ctx.enter_context(nc.semaphore(name)))
            return sems[-1]

        w_r = sb("w_r", [P, KD, E + L])
        bias = sb("r_bias", [P, E + L])
        stats, mv = sb("r_stats", [P, G, 6]), sb("r_mv", [P, G, 2])
        vare, rstd = sb("r_vare", [P, G]), sb("r_rstd", [P, G])
        xn = sb("r_xn", [P, G, D])
        xT = sb("r_xT", [P, KD, GT])
        logits = sb("logits", [P, TILES, E + L])
        col = [sb(f"r_col{i}", [P, TILES, 1]) for i in range(6)]
        lang = sb("lang", [P, TILES, L + 1])
        ew = sb("ew", [P, TILES, L])
        pr = [sb(f"r_pr{i}", [P, TILES, E]) for i in range(3)]
        hot = [sb(f"hot{i}", [P, TILES, E]) for i in range(2)]
        both = sb("both", [P, TILES, E])
        rev = sb("rev", [P, E])
        lane_i, lane_f = sb("lane_i", [P, P], I32), sb("lane_f", [P, P])
        token_i, token_f = sb("token_i", [P, TILES], I32), sb("token_f", [P, TILES])
        thresholds = sb("thresholds", [P, TILES])
        before = sb("before", [P, P])
        ones = sb("r_ones", [P, P])
        totals = sb("totals", [P, E, TILES])
        keep = sb("keep", [P, E, TILES])
        running = sb("running", [P, E, TILES])
        place = sb("place", [P, E, TILES])
        over = sb("over", [P, E, TILES])
        blocks_of, ends, starts = sb("blocks_of", [P, E]), sb("ends", [P, E]), sb("starts", [P, E])
        past = sb("past", [P, BLOCKS, E])
        block_f = sb("block_f", [P, BLOCKS, 1])
        slot_f = [sb(f"slot_f{i}", [P, TILES, 1]) for i in range(2)]
        slot_i = [sb(f"slot_i{i}", [P, TILES], I32) for i in range(2)]
        part_i = [sb(f"part_i{i}", [P, TILES], I32) for i in range(4)]
        part_f = [sb(f"part_f{i}", [P, TILES]) for i in range(4)]
        lane_hot = [sb(f"lane_hot{i}", [P, P]) for i in range(4)]
        block_hot = [sb(f"block_hot{i}", [P, BLOCKS]) for i in range(4)]
        ps_t = [psum(f"r_ps_t{i}") for i in range(2)]
        ps_l, ps_rank, ps_tot, ps_tab = psum("ps_l"), psum("ps_rank"), psum("ps_tot"), psum("ps_tab")

        w_in, const = sem("rw_in"), sem("r_const")
        stat_done, aggr_done, vare_done, rstd_done, xn_done, xn_stored = map(
            sem, ("r_stat", "r_aggr", "r_vare_done", "r_rstd_done", "r_xn_done", "xn_stored"))
        t_done, t_evac, l_done, l_evac = map(sem, ("r_t_done", "r_t_evac", "l_done", "l_evac"))
        chain, exp_go, exp_back, both_ready, rank_done, hot_ready, table_used = map(
            sem, ("r_chain", "exp_go", "exp_back", "both_ready", "rank_done", "hot_ready", "table_used"))
        CONSTS = 10

        start_at_one(nc, sems)
        block = ctx.enter_context(nc.Block())

        @block.sync
        def _(sp):
            sp.dma_start(w_r[:], w["routerT"].rearrange("(k p) e -> p k e", p=P)).then_inc(w_in, 16)
            sp.dma_start(bias[:, 0:E], w["router_b"].rearrange("(o e) -> o e", o=1).to_broadcast([P, E])).then_inc(w_in, 16)
            sp.dma_start(bias[:, E:E + L], w["lang_b"].rearrange("(o e) -> o e", o=1).to_broadcast([P, L])).then_inc(w_in, 16)
            with sp.Fori(0, GROUPS) as g:
                sp.wait_ge(xn_done, ONE + G * (g + 1))
                sp.dma_start(xn_dram[ds(GT * g, GT), :].rearrange("(j p) d -> p j d", p=P), xn[:]).then_inc(xn_stored, 16)
            sp.wait_ge(xn_stored, ONE + 16 * GROUPS)

        @block.gpsimd
        def _(pool):
            pool.iota(lane_i[:], pattern=[[1, P]], base=0, channel_multiplier=0).then_inc(const, 1)
            pool.iota(token_i[:], pattern=[[P, TILES]], base=0, channel_multiplier=1).then_inc(const, 1)
            pool.memset(ones[:], 1.0).then_inc(const, 1)
            pool.memset(keep[:], 1.0).then_inc(const, 1)
            pool.memset(lang[:], 0.0).then_inc(const, 1)
            pool.wait_ge(const, ONE + 5)
            pool.tensor_copy(lane_f[:], lane_i[:]).then_inc(const, 1)
            pool.tensor_copy(token_f[:], token_i[:]).then_inc(const, 1)
            pool.affine_select(out=before[:], in_=ones[:], compare_op=ALU.is_ge, fill=0.0, base=-1,
                               pattern=[[1, P]], channel_multiplier=-1).then_inc(const, 1)
            pool.memset(keep[:, :, 0:1], 0.0).then_inc(const, 1)
            pool.wait_ge(const, ONE + 9)
            pool.tensor_scalar(rev[:], lane_f[:, 0:E], -1.0, float(E), ALU.mult, ALU.add).then_inc(const, 1)
            with pool.Fori(0, GROUPS) as g:
                pool.wait_ge(vare_done, ONE + g + 1)
                pool.wait_ge(xn_done, ONE + G * g)
                pool.tensor_tensor(rstd[:], vare[:], neg_half[:, 0:G], ALU.pow).then_inc(rstd_done, 1)

        @block.tensor
        def _(pe):
            with pe.Fori(0, GROUPS) as g:
                pe.wait_ge(xn_done, ONE + G * (g + 1))
                pe.wait_ge(t_evac, ONE + KD * g)
                for k in range(KD):
                    for j in range(G):
                        last = pe.transpose(ps_t[k][:, P * j:P * j + P], xn[:, j, P * k:P * k + P], ident)
                last.then_inc(t_done, 1)
                pe.wait_ge(w_in, ONE + 48)
                pe.wait_ge(t_evac, ONE + KD * (g + 1))
                pe.wait_ge(l_evac, ONE + g)
                for j in range(G):
                    for k in range(KD):
                        last = pe.matmul(ps_l[:, (E + L) * j:(E + L) * (j + 1)], xT[:, k, P * j:P * j + P], w_r[:, k, :],
                                         start=(k == 0), stop=(k == KD - 1))
                last.then_inc(l_done, 1)
            pe.wait_ge(both_ready, ONE + 1)
            pe.wait_ge(const, ONE + CONSTS)
            flat = both[:].rearrange("p t e -> p (t e)")
            pe.matmul(ps_rank[:, 0:TILES * E], before[:], flat, start=True, stop=True)
            pe.matmul(ps_tot[:, 0:TILES * E], ones[:], flat, start=True, stop=True).then_inc(rank_done, 1)
            def table(n, i, first=False, last=False):
                pe.wait_ge(hot_ready, ONE + 2 * (n + 1))
                pe.matmul(ps_tab[:, 0:BLOCKS], lane_hot[i][:], block_hot[i][:], start=first, stop=last,
                          skip_group_check=True).then_inc(table_used, 1)

            for i in range(4):
                table(i, i, first=(i == 0))
            with pe.Fori(1, 2 * TILES // 4 - 1) as n:
                for i in range(4):
                    table(4 * n + i, i)
            for i in range(4):
                table(2 * TILES - 4 + i, i, last=(i == 3))

        @block.scalar
        def _(act):
            with act.Fori(0, GROUPS) as g:
                act.wait_ge(t_done, ONE + g + 1)
                act.wait_ge(l_done, ONE + g)
                for k in range(KD):
                    act.activation(xT[:, k, :], ps_t[k][:], ACT.Copy).then_inc(t_evac, 1)
            act.wait_ge(exp_go, ONE + 1)
            act.activation(lang[:, :, 0:L], logits[:, :, E:E + L], ACT.Exp).then_inc(exp_back, 1)
            act.wait_ge(exp_go, ONE + 2)
            act.activation(pr[1][:], pr[0][:], ACT.Exp).then_inc(exp_back, 1)

        @block.vector
        def _(dve):
            links = [0]

            def link(ins):
                links[0] += 1
                ins.then_inc(chain, 1)
                dve.wait_ge(chain, ONE + links[0])

            with dve.Fori(0, GROUPS) as g:
                for j in range(G):
                    dve.bn_stats(stats[:, j, :], x_res[:, ds(G * g + j, 1), :]).then_inc(stat_done, 1)
                wait_apart(dve, started, stat_done, ONE + G * (g + 1))
                for j in range(G):
                    dve.bn_aggr(mv[:, j, :], stats[:, j, :]).then_inc(aggr_done, 1)
                dve.wait_ge(aggr_done, ONE + G * (g + 1))
                dve.wait_ge(rstd_done, ONE + g)
                dve.tensor_scalar(vare[:], mv[:, :, 1], EPS, None, ALU.add).then_inc(vare_done, 1)
                dve.wait_ge(rstd_done, ONE + g + 1)
                dve.wait_ge(t_done, ONE + g)
                dve.wait_ge(xn_stored, ONE + 16 * g)
                for j in range(G):
                    dve.tensor_scalar(xn[:, j, :], x_res[:, ds(G * g + j, 1), :].rearrange("p o d -> p (o d)"),
                                      mv[:, j, 0:1], rstd[:, j:j + 1], ALU.subtract, ALU.mult).then_inc(xn_done, 1)
                dve.wait_ge(l_done, ONE + g + 1)
                dve.wait_ge(w_in, ONE + 48)
                dve.tensor_tensor(logits[:, ds(G * g, G), :], ps_l[:, 0:G * (E + L)].rearrange("p (j e) -> p j e", j=G),
                                  bias[:].unsqueeze(1).to_broadcast([P, G, E + L]), ALU.add).then_inc(l_evac, 1)
            dve.wait_ge(l_evac, ONE + GROUPS)
            dve.wait_ge(const, ONE + CONSTS)

            def wide(c, n):
                return c[:].to_broadcast([P, TILES, n])

            link(dve.tensor_reduce(col[0][:, :, 0], logits[:, :, E:E + L], AX.X, ALU.max))
            dve.tensor_tensor(logits[:, :, E:E + L], logits[:, :, E:E + L], wide(col[0], L), ALU.subtract)\
               .then_inc(exp_go, 1)
            dve.wait_ge(exp_back, ONE + 1)
            link(dve.tensor_reduce(col[1][:, :, 0], lang[:, :, 0:L], AX.X, ALU.add))
            link(dve.reciprocal(col[2][:], col[1][:]))
            link(dve.tensor_tensor(lang[:, :, 0:L], lang[:, :, 0:L], wide(col[2], L), ALU.mult))
            link(dve.tensor_tensor(ew[:], lang[:, :, 0:L], lang[:, :, 1:L + 1], ALU.add))
            for i in range(E // L):
                link(dve.scalar_tensor_tensor(out=pr[2][:, :, L * i:L * i + L], in0=ew[:], scalar=0.1,
                                              in1=logits[:, :, L * i:L * i + L], op0=ALU.mult, op1=ALU.add))
            link(dve.tensor_reduce(col[0][:, :, 0], pr[2][:], AX.X, ALU.max))
            dve.tensor_tensor(pr[0][:], pr[2][:], wide(col[0], E), ALU.subtract).then_inc(exp_go, 1)
            dve.wait_ge(exp_back, ONE + 2)
            link(dve.tensor_reduce(col[1][:, :, 0], pr[1][:], AX.X, ALU.add))
            link(dve.reciprocal(col[2][:], col[1][:]))
            link(dve.tensor_tensor(pr[0][:], pr[1][:], wide(col[2], E), ALU.mult))
            best = [col[3], col[4]]
            for i in range(2):
                link(dve.tensor_reduce(best[i][:, :, 0], pr[0][:], AX.X, ALU.max))
                link(dve.tensor_tensor(pr[1][:], pr[0][:], wide(best[i], E), ALU.is_equal))
                link(dve.tensor_tensor(pr[2][:], pr[1][:], rev[:].unsqueeze(1).to_broadcast([P, TILES, E]), ALU.mult))
                link(dve.tensor_reduce(col[5][:, :, 0], pr[2][:], AX.X, ALU.max))
                link(dve.tensor_tensor(hot[i][:], rev[:].unsqueeze(1).to_broadcast([P, TILES, E]), wide(col[5], E),
                                       ALU.is_equal))
                if i == 0:
                    link(dve.scalar_tensor_tensor(out=pr[0][:], in0=hot[0][:], scalar=-2.0, in1=pr[0][:],
                                                  op0=ALU.mult, op1=ALU.add))
            link(dve.tensor_tensor(col[0][:], best[0][:], best[1][:], ALU.add))
            link(dve.reciprocal(col[1][:], col[0][:]))
            for i in range(2):
                link(dve.tensor_tensor(r["weight"][i][:].unsqueeze(2), best[i][:], col[1][:], ALU.mult))
            dve.tensor_tensor(both[:], hot[0][:], hot[1][:], ALU.add).then_inc(both_ready, 1)
            dve.wait_ge(rank_done, ONE + 1)
            link(dve.tensor_copy(totals[:], ps_tot[:, 0:TILES * E].rearrange("p (t e) -> p e t", e=E)))
            link(dve.tensor_tensor_scan(running[:].rearrange("p e t -> p (e t)"), keep[:].rearrange("p e t -> p (e t)"),
                                        totals[:].rearrange("p e t -> p (e t)"), 0.0, ALU.mult, ALU.add))
            link(dve.tensor_scalar(thresholds[:], lane_f[:, 0:TILES], float(P), None, ALU.mult))
            link(dve.tensor_tensor(over[:], running[:, :, TILES - 1:TILES].to_broadcast([P, E, TILES]),
                                   thresholds[:].unsqueeze(1).to_broadcast([P, E, TILES]), ALU.is_gt))
            link(dve.tensor_reduce(blocks_of[:], over[:], AX.X, ALU.add))
            link(dve.tensor_tensor_scan(ends[:], ones[:, 0:E], blocks_of[:], 0.0, ALU.mult, ALU.add))
            link(dve.tensor_tensor(starts[:], ends[:], blocks_of[:], ALU.subtract))
            link(dve.tensor_tensor(past[:], lane_f[:, 0:BLOCKS].unsqueeze(2).to_broadcast([P, BLOCKS, E]),
                                   ends[:].unsqueeze(1).to_broadcast([P, BLOCKS, E]), ALU.is_ge))
            link(dve.tensor_reduce(block_f[:, :, 0], past[:], AX.X, ALU.add))
            link(dve.tensor_scalar(r["expert"][:], block_f[:, :, 0], float(E - 1), None, ALU.min))
            link(dve.tensor_tensor(place[:], running[:], totals[:], ALU.subtract))
            link(dve.tensor_tensor(running[:], place[:], ps_rank[:, 0:TILES * E].rearrange("p (t e) -> p e t", e=E), ALU.add))
            link(dve.scalar_tensor_tensor(out=place[:], in0=starts[:].unsqueeze(2).to_broadcast([P, E, TILES]),
                                          scalar=float(P), in1=running[:], op0=ALU.mult, op1=ALU.add))
            for i in range(2):
                link(dve.tensor_tensor(pr[i][:], hot[i][:], place[:].rearrange("p e t -> p t e"), ALU.mult))
                link(dve.tensor_reduce(slot_f[i][:, :, 0], pr[i][:], AX.X, ALU.add))
                link(dve.tensor_copy(r["slot"][i][:], slot_f[i][:, :, 0]))
                link(dve.tensor_copy(slot_i[i][:], slot_f[i][:, :, 0]))
                link(dve.tensor_scalar(part_i[2 * i][:], slot_i[i][:], P - 1, None, ALU.bitwise_and))
                link(dve.tensor_scalar(part_i[2 * i + 1][:], slot_i[i][:], P.bit_length() - 1, None,
                                       ALU.logical_shift_right))
                for j in (2 * i, 2 * i + 1):
                    link(dve.tensor_copy(part_f[j][:], part_i[j][:]))

            def one_hots(t, u, i):
                b = 2 * u + i
                dve.tensor_scalar(lane_hot[b][:], lane_f[:], part_f[2 * i][:, ds(t, 1)], None,
                                  ALU.is_equal).then_inc(hot_ready, 1)
                dve.tensor_scalar(block_hot[b][:], lane_f[:, 0:BLOCKS], part_f[2 * i + 1][:, ds(t, 1)],
                                  token_f[:, ds(t, 1)], ALU.is_equal, ALU.mult).then_inc(hot_ready, 1)

            for u in range(2):
                for i in range(2):
                    one_hots(u, u, i)
            with dve.Fori(1, TILES // 2) as n:
                for u in range(2):
                    for i in range(2):
                        dve.wait_ge(table_used, ONE + 4 * n + 2 * u + i - 3)
                        one_hots(2 * n + u, u, i)
            dve.wait_ge(table_used, ONE + 2 * TILES)
            link(dve.tensor_copy(r["token"][:], ps_tab[:, 0:BLOCKS]))


def experts(nc, started, xn_dram, y_dram, ident, w1, w2, w_in, r, w):
    with ExitStack() as ctx:
        def sb(name, shape, dt=F32):
            return ctx.enter_context(nc.sbuf_tensor(name, shape, dt))

        def psum(name):
            return ctx.enter_context(nc.psum_tensor(name, [P, 512], F32))

        sems = []

        def sem(name):
            sems.append(ctx.enter_context(nc.semaphore(name)))
            return sems[-1]

        b1 = sb("e_b1", [P, EXPERTS, FC])
        b2 = sb("e_b2", [P, EXPERTS, D])
        index = [sb(f"index{i}", [P, 1], U32) for i in range(2)]
        index_ready = sem("index_ready")
        xg = [sb(f"xg{i}", [P, D]) for i in range(2)]
        xgT = [sb(f"xgT{i}", [P, KD, P]) for i in range(2)]
        pre = sb("pre", [P, F])
        hT = [sb(f"e_hT{i}", [P, FC, P]) for i in range(2)]
        y = [sb(f"e_y{i}", [P, D]) for i in range(2)]
        ps_x = psum("e_ps_x")
        ps_h = [psum(f"e_ps_h{i}") for i in range(2)]
        ps_t = [psum(f"e_ps_t{i}") for i in range(2)]
        ps_y = psum("e_ps_y")
        gathered = [ctx.enter_context(nc.semaphore(f"e_gathered{i}")) for i in range(2)]
        y_stored = [sem(f"e_y_stored{i}") for i in range(2)]
        b_in, xt_done, xt_evac, h_done, h_evac, ht_done, gelu_done, y_done, y_evac = map(
            sem, ("eb_in", "e_xt_done", "e_xt_evac", "e_h_done", "e_h_evac", "e_ht_done",
                  "e_gelu_done", "e_y_done", "e_y_evac"))

        start_at_one(nc, sems)
        block = ctx.enter_context(nc.Block())

        def expert_of(eng, b):
            return eng.value_load(r["expert"][0:1, ds(b, 1)], min_val=0, max_val=EXPERTS - 1)

        @block.gpsimd
        def _(pool):
            def gather(b, i):
                pool.tensor_copy(index[i][:], r["token"][:, ds(b, 1)]).then_inc(index_ready, 1)
                wait_apart(pool, started, index_ready, ONE + b + 1)
                pool.indirect_dma_start(
                    out=xg[i][:], out_offset=None, in_=xn_dram,
                    in_offset=bass.IndirectOffsetOnAxis(ap=index[i][:], axis=0),
                ).then_inc(gathered[i], 16)

            gather(0, 0)
            gather(1, 1)
            with pool.Fori(0, BLOCKS // 2 - 1) as n:
                for i in range(2):
                    pool.wait_ge(xt_done, ONE + 2 * n + i + 1)
                    gather(2 * n + i + 2, i)

        @block.sync
        def _(sp):
            sp.dma_start(b1[:], w["e_b1"]).then_inc(b_in, 16)
            sp.dma_start(b2[:], w["e_b2"].rearrange("(o e) d -> o e d", o=1).to_broadcast([P, EXPERTS, D])).then_inc(b_in, 16)
            with sp.Fori(0, BLOCKS // 2) as n:
                for i in range(2):
                    b = 2 * n + i
                    sp.wait_ge(y_evac, ONE + b + 1)
                    sp.dma_start(y_dram[ds(P * b, P), :], y[i][:]).then_inc(y_stored[i], 16)
            for i in range(2):
                sp.wait_ge(y_stored[i], ONE + 16 * BLOCKS // 2)

        @block.tensor
        def _(pe):
            def turn_x(b, i, pair):
                pe.wait_ge(gathered[i], 16 * (pair + 1))
                pe.wait_ge(xt_evac, ONE + b)
                for k in range(KD):
                    last = pe.transpose(ps_x[:, P * k:P * k + P], xg[i][:, P * k:P * k + P], ident)
                last.then_inc(xt_done, 1)

            def hidden(b, i):
                e = expert_of(pe, b)
                pe.wait_ge(xt_evac, ONE + b + 1)
                pe.wait_ge(h_evac, ONE + 2 * b)
                for f in range(2):
                    for k in range(KD):
                        last = pe.matmul(ps_h[f][:], xgT[i][:, k, :],
                                         w1[:, ds(e, 1), k, 512 * f:512 * f + 512].rearrange("p o f -> p (o f)"),
                                         start=(k == 0), stop=(k == KD - 1))
                last.then_inc(h_done, 1)

            def turn_h(b):
                pe.wait_ge(h_evac, ONE + 2 * (b + 1))
                pe.wait_ge(gelu_done, ONE + FC * b)
                for c in range(FC):
                    last = pe.transpose(ps_t[c // 4][:, P * (c % 4):P * (c % 4) + P], pre[:, P * c:P * c + P], ident)
                last.then_inc(ht_done, 1)

            def output(b, i):
                e = expert_of(pe, b)
                pe.wait_ge(gelu_done, ONE + FC * (b + 1))
                pe.wait_ge(y_evac, ONE + b)
                for c in range(FC):
                    last = pe.matmul(ps_y[:, 0:D], hT[i][:, c, :], w2[:, ds(e, 1), c, :].rearrange("p o d -> p (o d)"),
                                     start=(c == 0), stop=(c == FC - 1))
                last.then_inc(y_done, 1)

            pe.wait_ge(w_in, 16 * 2 * EXPERTS)
            turn_x(0, 0, 0)
            hidden(0, 0)
            turn_x(1, 1, 0)
            hidden(1, 1)
            turn_h(0)
            turn_x(2, 0, 1)
            with pe.Fori(0, BLOCKS // 2 - 2) as n:
                for i in (1, 2):
                    b = 2 * n + i
                    hidden(b + 1, (i + 1) % 2)
                    turn_h(b)
                    turn_x(b + 2, i % 2, n + 1 + i // 2)
                    output(b - 1, (i + 1) % 2)
            b = BLOCKS - 3
            hidden(b + 1, 0)
            turn_h(b)
            turn_x(b + 2, 1, BLOCKS // 2 - 1)
            output(b - 1, 0)
            hidden(b + 2, 1)
            turn_h(b + 1)
            output(b, 1)
            turn_h(b + 2)
            output(b + 1, 0)
            output(b + 2, 1)

        @block.vector
        def _(dve):
            def hidden_out(b):
                dve.wait_ge(h_done, ONE + b + 1)
                dve.wait_ge(ht_done, ONE + b)
                for f in range(2):
                    dve.tensor_copy(pre[:, 512 * f:512 * f + 512], ps_h[f][:]).then_inc(h_evac, 1)

            def output_out(b, i):
                e = expert_of(dve, b)
                dve.wait_ge(y_done, ONE + b + 1)
                dve.tensor_tensor(y[i][:], ps_y[:, 0:D], b2[:, ds(e, 1), :].rearrange("p o d -> p (o d)"), ALU.add)\
                   .then_inc(y_evac, 1)

            dve.wait_ge(b_in, ONE + 32)
            hidden_out(0)
            hidden_out(1)
            hidden_out(2)
            output_out(0, 0)
            hidden_out(3)
            output_out(1, 1)
            with dve.Fori(1, BLOCKS // 2 - 1) as n:
                for i in range(2):
                    b = 2 * n + i
                    hidden_out(b + 2)
                    dve.wait_ge(y_stored[i], ONE + 16 * n)
                    output_out(b, i)
            for i in range(2):
                b = BLOCKS - 2 + i
                dve.wait_ge(y_stored[i], ONE + 16 * (BLOCKS // 2 - 1))
                output_out(b, i)

        @block.scalar
        def _(act):
            def x_out(b, i):
                act.wait_ge(xt_done, ONE + b + 1)
                act.activation(xgT[i][:].rearrange("p k t -> p (k t)"), ps_x[:, 0:KD * P], ACT.Copy).then_inc(xt_evac, 1)

            def gelu(b, i):
                e = expert_of(act, b)
                wait_apart(act, started, ht_done, ONE + b + 1)
                for c in range(FC):
                    act.activation(hT[i][:, c, :], ps_t[c // 4][:, P * (c % 4):P * (c % 4) + P], ACT.Gelu,
                                   bias=b1[:, ds(e, 1), c]).then_inc(gelu_done, 1)

            act.wait_ge(b_in, ONE + 32)
            x_out(0, 0)
            x_out(1, 1)
            gelu(0, 0)
            with act.Fori(0, BLOCKS // 2 - 1) as n:
                for i in range(2):
                    act.wait_ge(h_done, ONE + 2 * n + i + 1)
                    x_out(2 * n + i + 2, i)
                    gelu(2 * n + i + 1, (i + 1) % 2)
            gelu(BLOCKS - 1, 1)


def combine(nc, started, x_res, y_dram, out, r):
    with ExitStack() as ctx:
        SLOTS = 4
        rows = [[ctx.enter_context(nc.sbuf_tensor(f"rows{i}_{s}", [P, D], F32)) for s in range(SLOTS)] for i in range(2)]
        result = [ctx.enter_context(nc.sbuf_tensor(f"result{s}", [P, D], F32)) for s in range(SLOTS)]
        half = [ctx.enter_context(nc.sbuf_tensor(f"half{s}", [P, D], F32)) for s in range(SLOTS)]
        index = [[ctx.enter_context(nc.sbuf_tensor(f"slot{i}_{s}", [P, 1], U32)) for s in range(SLOTS)] for i in range(2)]
        fetched = [ctx.enter_context(nc.semaphore(f"rows_in{s}")) for s in range(SLOTS)]
        stored = [ctx.enter_context(nc.semaphore(f"out_stored{s}")) for s in range(SLOTS)]
        index_ready, first_done, done = [ctx.enter_context(nc.semaphore(n)) for n in
                                         ("slots_ready", "first_added", "result_done")]
        sems = [*stored, index_ready, first_done, done]
        start_at_one(nc, sems)
        block = ctx.enter_context(nc.Block())

        @block.gpsimd
        def _(pool):
            def fetch(t, s):
                for i in range(2):
                    pool.tensor_copy(index[i][s][:], r["slot"][i][:, ds(t, 1)]).then_inc(index_ready, 1)
                wait_apart(pool, started, index_ready, ONE + 2 * (t + 1))
                for i in range(2):
                    pool.indirect_dma_start(
                        out=rows[i][s][:], out_offset=None, in_=y_dram,
                        in_offset=bass.IndirectOffsetOnAxis(ap=index[i][s][:], axis=0),
                    ).then_inc(fetched[s], 16)

            for s in range(SLOTS):
                fetch(s, s)
            with pool.Fori(1, TILES // SLOTS) as n:
                for s in range(SLOTS):
                    pool.wait_ge(done, ONE + SLOTS * n + s - SLOTS + 1)
                    fetch(SLOTS * n + s, s)

        @block.vector
        def _(dve):
            def add(t, s, turn):
                dve.wait_ge(fetched[s], 32 * (turn + 1))
                x = x_res[:, ds(t, 1), :].rearrange("p o d -> p (o d)")
                dve.scalar_tensor_tensor(out=half[s][:], in0=rows[0][s][:], scalar=r["weight"][0][:, ds(t, 1)],
                                         in1=x, op0=ALU.mult, op1=ALU.add).then_inc(first_done, 1)
                dve.wait_ge(first_done, ONE + t + 1)
                dve.scalar_tensor_tensor(out=result[s][:], in0=rows[1][s][:], scalar=r["weight"][1][:, ds(t, 1)],
                                         in1=half[s][:], op0=ALU.mult, op1=ALU.add).then_inc(done, 1)

            for s in range(SLOTS):
                add(s, s, 0)
            with dve.Fori(1, TILES // SLOTS) as n:
                for s in range(SLOTS):
                    dve.wait_ge(stored[s], ONE + 16 * n)
                    add(SLOTS * n + s, s, n)

        @block.sync
        def _(sp):
            with sp.Fori(0, TILES // SLOTS) as n:
                for s in range(SLOTS):
                    sp.wait_ge(done, ONE + SLOTS * n + s + 1)
                    sp.dma_start(out[ds(P * (SLOTS * n + s), P), :], result[s][:]).then_inc(stored[s], 16)
            for s in range(SLOTS):
                sp.wait_ge(stored[s], ONE + 16 * TILES // SLOTS)


def build(nc, w, out):
    with ExitStack() as ctx:
        def sb(name, shape, dt=F32):
            return ctx.enter_context(nc.sbuf_tensor(name, shape, dt))

        x_res = sb("x_res", [P, TILES, D])
        ident = sb("ident", [P, P])
        neg_half = sb("neg_half", [P, 8])
        r = {"token": sb("slot_token", [P, BLOCKS], U32), "expert": sb("block_expert", [P, BLOCKS], I32),
             "slot": [sb(f"token_slot{i}", [P, TILES], U32) for i in range(2)],
             "weight": [sb(f"token_weight{i}", [P, TILES]) for i in range(2)]}
        xn_dram = nc.dram_tensor("xn_dram", [N, D], F32, kind="Internal").ap()
        y_dram = nc.dram_tensor("y_dram", [P * BLOCKS, D], F32, kind="Internal").ap()
        const = ctx.enter_context(nc.semaphore("const"))
        started = ctx.enter_context(nc.semaphore("started"))
        experts_in = ctx.enter_context(nc.semaphore("experts_in"))
        w_qkv, w_out = sb("w_qkv", [P, KD, 3 * D]), sb("w_out", [P, KD, D])
        attn_w_in = ctx.enter_context(nc.semaphore("attn_w_in"))
        with nc.Block() as block:
            @block.gpsimd
            def _(pool):
                pool.memset(neg_half[:], -0.5).then_inc(const, 1)
                pool.memset(ident[:], 0.0).then_inc(const, 1)
                pool.wait_ge(const, 2)
                pool.affine_select(out=ident[:], in_=ident[:], compare_op=ALU.not_equal, fill=1.0, base=0,
                                   pattern=[[-1, P]], channel_multiplier=1).then_inc(const, 1)
                pool.wait_ge(const, 3)
                pool.memset(neg_half[:], -0.5).then_inc(started, 1)
                pool.wait_ge(started, 1)
        tower(nc, started, x_res, ident[:], neg_half, w_qkv, w_out, attn_w_in, w)
        e_w1 = sb("e_w1", [P, EXPERTS, KD, F])
        e_w2 = sb("e_w2", [P, EXPERTS, FC, D])
        with nc.Block() as block:
            @block.sync
            def _(sp):
                for e in range(EXPERTS):
                    sp.dma_start(e_w1[:, e], w["e_w1"][e].rearrange("(k p) f -> p k f", p=P)).then_inc(experts_in, 16)
                    sp.dma_start(e_w2[:, e], w["e_w2"][e].rearrange("(c p) d -> p c d", p=P)).then_inc(experts_in, 16)
        attention(nc, started, x_res, ident[:], neg_half, w_qkv, w_out, attn_w_in)
        route(nc, started, x_res, xn_dram, ident[:], neg_half, w, r)
        experts(nc, started, xn_dram, y_dram, ident[:], e_w1, e_w2, experts_in, r, w)
        combine(nc, started, x_res, y_dram, out, r)


def lay_out(inputs):
    import numpy as np

    a = {k.removeprefix("L0_tok_"): v for k, v in inputs.items() if k.startswith("L0_tok_")}
    a["tokens"] = np.asarray(inputs["x"]).reshape(TILES, P).T
    f = {k.removeprefix("L0_ffn_"): np.asarray(v) for k, v in inputs.items() if k.startswith("L0_ffn_")}
    a["routerT"] = np.concatenate([f["router_w"], f["lang_w"]]).T
    a["router_b"], a["lang_b"] = f["router_b"], f["lang_b"]
    a["e_w1"], a["e_w2"], a["e_b2"] = f["w1"], f["w2"], f["b2"]
    a["e_b1"] = f["b1"].reshape(EXPERTS, FC, P).transpose(2, 0, 1)
    a["w_qkvT"] = np.asarray(inputs["L0_attn_w_qkv"]).T
    a["w_outT"] = np.asarray(inputs["L0_attn_w_out"]).T
    a["A_diag"] = np.concatenate([a["A_diag"].T] * 2)
    a["b1"] = np.asarray(a["b1"]).reshape(LAYERS, FC, P).transpose(2, 0, 1)
    a["ln_par"] = np.stack([np.asarray(a.pop(n)).reshape(LAYERS, KD, P).transpose(2, 0, 1)
                            for n in ("ln1_s", "ln1_b", "ln2_s", "ln2_b")], axis=1)
    return {k: np.ascontiguousarray(v) for k, v in a.items()}


def kernel(**inputs):
    import concourse.bacc as bacc
    from concourse.bass_utils import run_bass_kernel_spmd

    nc = bacc.Bacc("TRN2", target_bir_lowering=False, num_devices=1)
    arrays = {f"in_{k}": v for k, v in lay_out(inputs).items()}
    w = {k.removeprefix("in_"): nc.dram_tensor(k, v.shape, mybir.dt.from_np(v.dtype), kind="ExternalInput").ap()
         for k, v in arrays.items()}
    out = nc.dram_tensor("out", (N, D), F32, kind="ExternalOutput").ap()
    build(nc, w, out)
    r = run_bass_kernel_spmd(nc, [arrays], core_ids=[0])
    return r.results[0]["out"].reshape(SEQS, T, D)
```

```python
from contextlib import ExitStack

import concourse.bass as bass
from concourse import mybir

P = 128
ALU = mybir.AluOpType
ACT = mybir.ActivationFunctionType
AX = mybir.AxisListType
F32 = mybir.dt.float32
F32R = mybir.dt.float32r
I32 = mybir.dt.int32
U32 = mybir.dt.uint32

SEQS, T = 16, 256
N = SEQS * T
TILES = N // P
D = 256
KD = D // P
LAYERS, S, F = 4, 64, 1024
FC = F // P
G = 4
GROUPS = TILES // G
GT = G * P
HEADS, DH = 16, 16
EXPERTS, LANGS = 8, 4
EPS = 1e-5
BLOCKS = 2 * N // P + EXPERTS
RING = 3
ds = bass.ds


ONE = 1


def start_at_one(nc, sems):
    with nc.Block() as block:
        @block.sync
        def _(sp):
            for s in sems:
                sp.sem_inc(s, ONE)


def wait_apart(eng, started, sem, value):
    value = value if isinstance(value, int) else eng.compute_val(value)
    eng.wait_ge(started, 1)
    eng.wait_ge(sem, value)


def tower(nc, started, x_res, ident, neg_half, w_qkv, w_out, attn_w_in, w):
    vocab = w["emb"].shape[0]
    with ExitStack() as ctx:
        def sb(name, shape, dt=F32):
            return ctx.enter_context(nc.sbuf_tensor(name, shape, dt))

        def psum(name):
            return ctx.enter_context(nc.psum_tensor(name, [P, 512], F32))

        sems = []

        def sem(name):
            sems.append(ctx.enter_context(nc.semaphore(name)))
            return sems[-1]

        AHEAD = 4
        tok_i = sb("tok_i", [P, TILES], I32)
        tok_f = sb("tok_f", [P, TILES])
        wrap = sb("wrap", [P, TILES])
        wrapped = sb("wrapped", [P, TILES])
        row = sb("row", [P, TILES], U32)
        pos_sb = sb("pos_sb", [P, T // P, D])
        b_all = sb("b_all", [P, LAYERS, KD, S])
        b_now = [sb(f"b_{n}", [P, KD, 3 * S], F32R) for n in ("hi", "lo")]
        c_now = [sb(f"c_{n}", [P, D], F32R) for n in ("hi", "lo")]
        d_now = [sb(f"d_{n}", [P, KD, D], F32R) for n in ("hi", "lo")]
        c_all = sb("c_all", [P, LAYERS, D])
        d_all = sb("d_all", [P, LAYERS, KD, D])
        a_raw = sb("a_raw", [P, LAYERS])
        decay = sb("decay", [P, LAYERS])
        decay_row = sb("decay_row", [P, LAYERS, T])
        b1_all = sb("b1_all", [P, LAYERS, FC])
        b2_all = sb("b2_all", [P, LAYERS, D])
        ln_par = sb("ln_par", [P, 4, LAYERS, KD])
        w1_raw = sb("w1_raw", [P, KD, F])
        w2_raw = sb("w2_raw", [P, FC, D])
        w1_hi, w1_lo = sb("w1_hi", [P, KD, F], F32R), sb("w1_lo", [P, KD, F], F32R)
        w2_hi, w2_lo = sb("w2_hi", [P, FC, D], F32R), sb("w2_lo", [P, FC, D], F32R)
        lnf_s, lnf_b = sb("lnf_s", [P, D]), sb("lnf_b", [P, D])
        NORMS = 3
        stats = [sb(f"stats{i}", [P, G, 6]) for i in range(NORMS)]
        mv = [sb(f"mean_var{i}", [P, G, 2]) for i in range(NORMS)]
        vare = [sb(f"var_eps{i}", [P, G]) for i in range(NORMS)]
        rstd = [sb(f"rstd{i}", [P, G]) for i in range(NORMS)]
        xn = [sb(f"xn{i}", [P, G, D]) for i in range(NORMS)]
        x1T = sb("x1T", [P, KD, GT])
        x1_hi, x1_lo = sb("x1_hi", [P, KD, GT], F32R), sb("x1_lo", [P, KD, GT], F32R)
        states = sb("states", [P, T])
        states_hi, states_lo = sb("states_hi", [P, T], F32R), sb("states_lo", [P, T], F32R)
        x2T = sb("x2T", [P, KD, GT])
        x2T_hi = [sb(f"x2T_hi{i}", [P, KD, GT], F32R) for i in range(2)]
        x2T_lo = [sb(f"x2T_lo{i}", [P, KD, GT], F32R) for i in range(2)]
        HB = 4
        hT = sb("hT", [P, HB, GT])
        hT_hi, hT_lo = sb("hT_hi", [P, HB, GT], F32R), sb("hT_lo", [P, HB, GT], F32R)
        ps_t = [psum(f"ps_t{i}") for i in range(2)]
        ps_y = [psum(f"ps_y{i}") for i in range(2)]
        ps_h = [psum(f"ps_h{i}") for i in range(HB)]

        gathered = [ctx.enter_context(nc.semaphore(f"gathered{g}")) for g in range(AHEAD)]
        tokens_in, pos_in, idx_step, pos_added = map(sem, ("tokens_in", "pos_in", "idx_step", "pos_added"))
        small_in, a_in, w1_in, w2_in = map(sem, ("small_in", "a_in", "w1_in", "w2_in"))
        decay_done, decay_ready = sem("decay_done"), sem("decay_ready")
        hi_done, w1_split, w2_split, ssm_w_ready = map(sem, ("w_hi_done", "w1_split", "w2_split", "ssm_w_ready"))
        w2_hi_done = sem("w2_hi_done")
        stat_done = [sem(f"stat_done{i}") for i in range(NORMS)]
        aggr_done = [sem(f"aggr_done{i}") for i in range(NORMS)]
        vare_done = [sem(f"vare_done{i}") for i in range(NORMS)]
        rstd_done = [sem(f"rstd_done{i}") for i in range(NORMS)]
        xn_done = [sem(f"xn_done{i}") for i in range(NORMS)]
        t_done = [sem(f"t_done{i}") for i in range(2)]
        x1_evac, x1_lo_done, u_done, scan_done, y_done, res1_done = map(
            sem, ("x1_evac", "x1_lo_done", "u_done", "scan_done", "y_done", "res1_done"))
        states_hi_done, states_lo_done, ssm_hi_done = map(sem, ("states_hi_done", "states_lo_done", "ssm_hi_done"))
        b2_added, x2_evac, x2_lo_done = map(sem, ("b2_added", "x2_evac", "x2_lo_done"))
        h_done, gelu_done, h_lo_done, f_done, res2_done = map(
            sem, ("h_done", "gelu_done", "h_lo_done", "f_done", "res2_done"))
        lnf_in, scaled, fin = sem("lnf_in"), sem("final_scaled"), sem("final_ln")

        start_at_one(nc, sems)
        block = ctx.enter_context(nc.Block())

        def layer_of_bodies(eng, l, last, body):
            with eng.Fori(0, GROUPS // 2 - 1) as i:
                for p in range(2):
                    body(GROUPS * l + 2 * i + p, 2 * i + p, p, l, last)
            for p in range(2):
                g = GROUPS - 2 + p
                body(GROUPS * l + g, g, p, l, last)

        def all_bodies(eng, body, first_layer=0):
            with eng.Fori(first_layer, LAYERS - 1) as l:
                layer_of_bodies(eng, l, False, body)
            layer_of_bodies(eng, LAYERS - 1, True, body)

        def after(g, steps, last):
            if isinstance(g, int) and g + steps >= GROUPS:
                return None if last else g + steps - GROUPS
            return g + steps

        def next_layer(g, l):
            return l + 1 if isinstance(g, int) and g == GROUPS - 1 else l

        @block.sync
        def _(sp):
            sp.dma_start(tok_i[:], w["tokens"]).then_inc(tokens_in, 16)
            sp.dma_start(pos_sb[:], w["pos_emb"][0:T, :].rearrange("(j p) d -> p j d", p=P)).then_inc(pos_in, 16)
            sp.dma_start(a_raw[:], w["A_diag"]).then_inc(a_in, 16)
            small = [(b_all[:, l], w["B"][l].rearrange("(k p) s -> p k s", p=P)) for l in range(LAYERS)]
            small += [(c_all[64 * h:64 * h + 64, :, :], w["C"].rearrange("l s d -> s l d")) for h in range(2)]
            small += [(d_all[:, l], w["D"][l].rearrange("(k p) e -> p k e", p=P)) for l in range(LAYERS)]
            small += [(b1_all[:], w["b1"]), (ln_par[:], w["ln_par"]),
                      (b2_all[:], w["b2"].rearrange("(o l) d -> o l d", o=1).to_broadcast([P, LAYERS, D]))]
            for dst, src in small:
                sp.dma_start(dst, src).then_inc(small_in, 16)
            with sp.Fori(0, LAYERS) as l:
                sp.wait_ge(w1_split, ONE + l)
                sp.dma_start(w1_raw[:], w["w1"][ds(l, 1)].rearrange("o (k p) f -> p (o k) f", p=P)).then_inc(w1_in, 16)
                sp.wait_ge(w2_split, ONE + l)
                sp.dma_start(w2_raw[:], w["w2"][ds(l, 1)].rearrange("o (c p) d -> p (o c) d", p=P)).then_inc(w2_in, 16)
            sp.dma_start(w_qkv[:], w["w_qkvT"].rearrange("(k p) f -> p k f", p=P)).then_inc(attn_w_in, 16)
            sp.dma_start(w_out[:], w["w_outT"].rearrange("(k p) f -> p k f", p=P)).then_inc(attn_w_in, 16)
            for dst, name in ((lnf_s, "lnf_s"), (lnf_b, "lnf_b")):
                sp.dma_start(dst[:], w[name].rearrange("(o d) -> o d", o=1).to_broadcast([P, D])).then_inc(lnf_in, 16)

        SMALL = 16 * (LAYERS * 2 + 2 + 3)

        @block.tensor
        def _(pe):
            def turn(i, n):
                pe.wait_ge(xn_done[i], ONE + G * (n + 1))
                for k in range(KD):
                    for j in range(G):
                        last = pe.transpose(ps_t[k][:, P * j:P * j + P], xn[i][:, j, P * k:P * k + P], ident)
                last.then_inc(t_done[i], 1)

            def turn1(n):
                pe.wait_ge(x2_evac, ONE + 2 * KD * n)
                turn(0, n)

            def drive(n):
                pe.wait_ge(x1_lo_done, ONE + KD * (n + 1))
                for q in range(2):
                    for k in range(KD):
                        for i, (b, x) in enumerate([(0, x1_hi), (0, x1_lo), (1, x1_hi)]):
                            last = pe.matmul(ps_t[0][:, 0:T], b_now[b][:, k, S * (1 - q):S * (3 - q)],
                                             x[:, k, T * q:T * q + T], start=(q == 0 and k == 0 and i == 0),
                                             stop=(q == 1 and k == KD - 1 and i == 2))
                last.then_inc(u_done, 1)

            def ssm_out(n):
                def out(j):
                    return ps_t[j // 2][:, D * (j % 2):D * (j % 2) + D]

                for h in (1, 0):
                    if h == 0:
                        pe.wait_ge(scan_done, ONE + n + 1)
                    for j in (2 * h, 2 * h + 1):
                        for k in range(KD):
                            for i, (x, d) in enumerate([(x1_hi, 0), (x1_hi, 1), (x1_lo, 0)]):
                                pe.matmul(out(j), x[:, k, P * j:P * j + P], d_now[d][:, k, :],
                                          start=(k == 0 and i == 0 and j % 2 == 0), stop=False, skip_group_check=True)
                pe.wait_ge(states_lo_done, ONE + n + 1)
                for j in range(G):
                    rows, i0 = slice(S * (j // 2), S * (j // 2) + S), P * (j % 2)
                    for i, (x, c) in enumerate([(states_hi, 0), (states_hi, 1), (states_lo, 0)]):
                        last = pe.matmul(out(j), x[rows, i0:i0 + P], c_now[c][rows, :], start=False, stop=(i == 2),
                                         skip_group_check=True)
                last.then_inc(y_done, 1)

            def turn2(n):
                pe.wait_ge(res1_done, ONE + 2 * (n + 1))
                turn(1, n)

            def up(n, p, c):
                if c == 0:
                    pe.wait_ge(x2_lo_done, ONE + KD * (n + 1))
                passes = [(w1_hi, x2T_hi[p]), (w1_hi, x2T_lo[p]), (w1_lo, x2T_hi[p])]
                for k in range(KD):
                    for i, (a, b) in enumerate(passes):
                        last = pe.matmul(ps_h[c % HB][:], a[:, k, P * c:P * c + P], b[:, k, :],
                                         start=(k == 0 and i == 0), stop=(k == KD - 1 and i == 2))
                last.then_inc(h_done, 1)

            def down(n, l, c):
                if c == 0:
                    pe.wait_ge(res2_done, ONE + 2 * n)
                    wait_apart(pe, started, w2_split, ONE + l + 1)
                pe.wait_ge(h_lo_done, ONE + FC * n + c + 1)
                for j in range(G):
                    out = ps_y[j // 2][:, D * (j % 2):D * (j % 2) + D]
                    tok = slice(P * j, P * j + P)
                    for i, (a, b) in enumerate([(hT_hi, w2_hi), (hT_hi, w2_lo), (hT_lo, w2_hi)]):
                        last = pe.matmul(out, a[:, c % HB, tok], b[:, c, :],
                                         start=(c == 0 and i == 0 and j % 2 == 0), stop=(c == FC - 1 and i == 2),
                                         skip_group_check=True)
                if c == FC - 1:
                    last.then_inc(f_done, 1)

            def body(n, g, p, l, last):
                more = after(g, 1, last) is not None
                if more:
                    turn1(n + 1)
                up(n, p, 2)
                down(n, l, 0)
                up(n, p, 3)
                if more:
                    if next_layer(g, l) is not l:
                        pe.wait_ge(ssm_w_ready, ONE + 3 * (l + 2))
                    drive(n + 1)
                down(n, l, 1)
                if more:
                    ssm_out(n + 1)
                up(n, p, 4)
                down(n, l, 2)
                up(n, p, 5)
                down(n, l, 3)
                up(n, p, 6)
                if more:
                    turn2(n + 1)
                down(n, l, 4)
                up(n, p, 7)
                down(n, l, 5)
                if more:
                    if next_layer(g, l) is not l:
                        pe.wait_ge(w1_split, ONE + l + 2)
                    up(n + 1, 1 - p, 0)
                down(n, l, 6)
                if more:
                    up(n + 1, 1 - p, 1)
                down(n, l, 7)

            pe.wait_ge(small_in, ONE + SMALL)
            turn1(0)
            pe.wait_ge(ssm_w_ready, ONE + 3)
            drive(0)
            ssm_out(0)
            turn2(0)
            pe.wait_ge(w1_split, ONE + 1)
            up(0, 0, 0)
            up(0, 0, 1)
            all_bodies(pe, body)

        @block.vector
        def _(dve):
            def statistics(i, n, g):
                for j in range(G):
                    dve.bn_stats(stats[i][:, j, :], x_res[:, ds(G * g + j, 1), :]).then_inc(stat_done[i], 1)
                wait_apart(dve, started, stat_done[i], ONE + G * (n + 1))
                for j in range(G):
                    dve.bn_aggr(mv[i][:, j, :], stats[i][:, j, :]).then_inc(aggr_done[i], 1)
                dve.wait_ge(aggr_done[i], ONE + G * (n + 1))
                dve.wait_ge(rstd_done[i], ONE + n)
                dve.tensor_scalar(vare[i][:], mv[i][:, :, 1], EPS, None, ALU.add).then_inc(vare_done[i], 1)

            def normalise(i, n, g):
                dve.wait_ge(rstd_done[i], ONE + n + 1)
                if i < 2:
                    dve.wait_ge(t_done[i], ONE + n)
                else:
                    dve.wait_ge(fin, ONE + n)
                for j in range(G):
                    dve.tensor_scalar(xn[i][:, j, :], x_res[:, ds(G * g + j, 1), :].rearrange("p o d -> p (o d)"),
                                      mv[i][:, j, 0:1], rstd[i][:, j:j + 1], ALU.subtract, ALU.mult)\
                       .then_inc(xn_done[i], 1)

            def statistics1(n, g):
                wait_apart(dve, started, pos_added, ONE + g + 1)
                statistics(0, n, g)

            def scan(n, l):
                dve.wait_ge(u_done, ONE + n + 1)
                dve.wait_ge(y_done, ONE + n)
                dve.tensor_tensor_scan(states[:], decay_row[:, ds(l, 1), :].rearrange("p o t -> p (o t)"),
                                       ps_t[0][:, 0:T], 0.0, ALU.mult, ALU.add).then_inc(scan_done, 1)
                wait_apart(dve, started, scan_done, ONE + n + 1)
                dve.tensor_copy(states_hi[:], states[:]).then_inc(states_hi_done, 1)
                dve.wait_ge(states_hi_done, ONE + n + 1)
                dve.tensor_tensor(states_lo[:], states[:], states_hi[:].bitcast(F32), ALU.subtract)\
                   .then_inc(states_lo_done, 1)

            def x1_rest(n):
                for k in range(KD):
                    dve.wait_ge(x1_evac, ONE + 2 * KD * n + 2 * (k + 1))
                    dve.tensor_tensor(x1_lo[:, k, :], x1T[:, k, :], x1_hi[:, k, :].bitcast(F32), ALU.subtract)\
                       .then_inc(x1_lo_done, 1)

            def add_pair(ps, done, g):
                for h in range(2):
                    pair = x_res[:, ds(G * g + 2 * h, 2), :]
                    dve.tensor_tensor(pair, ps[h][:].rearrange("p (j d) -> p j d", j=2), pair, ALU.add)\
                       .then_inc(done, 1)

            def residual1(n, g):
                dve.wait_ge(y_done, ONE + n + 1)
                add_pair(ps_t, res1_done, g)
                wait_apart(dve, started, res1_done, ONE + 2 * (n + 1))
                statistics(1, n, g)

            def x2_rest(n, p):
                for k in range(KD):
                    dve.wait_ge(x2_evac, ONE + 2 * KD * n + 2 * (k + 1))
                    dve.tensor_tensor(x2T_lo[p][:, k, :], x2T[:, k, :], x2T_hi[p][:, k, :].bitcast(F32), ALU.subtract)\
                       .then_inc(x2_lo_done, 1)

            def h_rest(n, c):
                b = c % HB
                dve.wait_ge(gelu_done, ONE + 2 * (FC * n + c + 1))
                dve.tensor_tensor(hT_lo[:, b, :], hT[:, b, :], hT_hi[:, b, :].bitcast(F32), ALU.subtract)\
                   .then_inc(h_lo_done, 1)

            def residual2(n, g):
                dve.wait_ge(f_done, ONE + n + 1)
                dve.wait_ge(b2_added, ONE + n + 1)
                add_pair(ps_y, res2_done, g)

            def body(n, g, p, l, last):
                g1, g2 = after(g, 1, last), after(g, 2, last)
                if g1 is not None:
                    x1_rest(n + 1)
                h_rest(n, 2)
                if g1 is not None:
                    scan(n + 1, next_layer(g, l))
                h_rest(n, 3)
                if g1 is not None:
                    residual1(n + 1, g1)
                h_rest(n, 4)
                if g1 is not None:
                    normalise(1, n + 1, g1)
                h_rest(n, 5)
                if g2 is not None:
                    wait_apart(dve, started, res2_done, ONE + 2 * n)
                    statistics1(n + 2, g2)
                h_rest(n, 6)
                if g1 is not None:
                    x2_rest(n + 1, 1 - p)
                h_rest(n, 7)
                if g2 is not None:
                    normalise(0, n + 2, g2)
                if g1 is not None:
                    h_rest(n + 1, 0)
                residual2(n, g)
                if last:
                    wait_apart(dve, started, res2_done, ONE + 2 * (n + 1))
                    statistics(2, g, g)
                if g1 is not None:
                    h_rest(n + 1, 1)
                if last:
                    normalise(2, g, g)

            dve.wait_ge(tokens_in, ONE + 16)
            dve.tensor_copy(tok_f[:], tok_i[:]).then_inc(idx_step, 1)
            dve.wait_ge(idx_step, ONE + 1)
            dve.tensor_scalar(wrap[:], tok_f[:], 0.0, float(vocab), ALU.is_lt, ALU.mult).then_inc(idx_step, 1)
            dve.wait_ge(idx_step, ONE + 2)
            dve.tensor_tensor(wrapped[:], tok_f[:], wrap[:], ALU.add).then_inc(idx_step, 1)
            dve.wait_ge(idx_step, ONE + 3)
            dve.tensor_scalar(row[:], wrapped[:], 0.0, float(vocab - 1), ALU.max, ALU.min).then_inc(idx_step, 1)
            dve.memset(decay_row[:], 1.0).then_inc(decay_ready, 1)
            dve.wait_ge(decay_done, ONE + 1)
            dve.wait_ge(decay_ready, ONE + 1)
            for l in range(LAYERS):
                dve.tensor_scalar(decay_row[:, l, :], decay_row[:, l, :], decay[:, l:l + 1], None, ALU.mult)\
                   .then_inc(decay_ready, 1)
            dve.wait_ge(decay_ready, ONE + 1 + LAYERS)
            statistics1(0, 0)
            normalise(0, 0, 0)
            dve.wait_ge(w1_in, ONE + 16)
            dve.tensor_copy(w1_hi[:], w1_raw[:]).then_inc(hi_done, 1)
            dve.wait_ge(hi_done, ONE + 1)
            dve.tensor_tensor(w1_lo[:], w1_raw[:], w1_hi[:].bitcast(F32), ALU.subtract).then_inc(w1_split, 1)
            x1_rest(0)
            scan(0, 0)
            residual1(0, 0)
            normalise(1, 0, 0)
            x2_rest(0, 0)
            statistics1(1, 1)
            normalise(0, 1, 1)
            dve.wait_ge(w2_hi_done, ONE + 1)
            dve.tensor_tensor(w2_lo[:], w2_raw[:], w2_hi[:].bitcast(F32), ALU.subtract).then_inc(w2_split, 1)
            h_rest(0, 0)
            h_rest(0, 1)
            all_bodies(dve, body)

        @block.scalar
        def _(act):
            def turned1(n, l):
                wait_apart(act, started, t_done[0], ONE + n + 1)
                wait_apart(act, started, y_done, ONE + n)
                for k in range(KD):
                    for dst in (x1T, x1_hi):
                        act.activation(dst[:, k, :], ps_t[k][:], ACT.Identity, scale=ln_par[:, 0, ds(l, 1), k],
                                       bias=ln_par[:, 1, ds(l, 1), k]).then_inc(x1_evac, 1)

            def turned2(n, p, l):
                wait_apart(act, started, t_done[1], ONE + n + 1)
                wait_apart(act, started, x2_lo_done, ONE + KD * n)
                for k in range(KD):
                    for dst in (x2T, x2T_hi[p]):
                        act.activation(dst[:, k, :], ps_t[k][:], ACT.Identity, scale=ln_par[:, 2, ds(l, 1), k],
                                       bias=ln_par[:, 3, ds(l, 1), k]).then_inc(x2_evac, 1)

            def gelu(n, l, c):
                wait_apart(act, started, h_done, ONE + FC * n + c + 1)
                for dst in (hT, hT_hi):
                    act.activation(dst[:, c % HB, :], ps_h[c % HB][:], ACT.Gelu, bias=b1_all[:, ds(l, 1), c])\
                       .then_inc(gelu_done, 1)

            def body(n, g, p, l, last):
                more = after(g, 1, last) is not None
                if more:
                    turned1(n + 1, next_layer(g, l))
                for c in range(2, FC - 1):
                    gelu(n, l, c)
                if more:
                    turned2(n + 1, 1 - p, next_layer(g, l))
                gelu(n, l, FC - 1)
                if more:
                    for c in range(2):
                        gelu(n + 1, next_layer(g, l), c)

            act.wait_ge(a_in, ONE + 16)
            act.activation(decay[:], a_raw[:], ACT.Sigmoid).then_inc(decay_done, 1)
            act.wait_ge(small_in, ONE + SMALL)
            turned1(0, 0)
            act.wait_ge(w2_in, ONE + 16)
            act.activation(w2_hi[:], w2_raw[:], ACT.Copy).then_inc(w2_hi_done, 1)
            turned2(0, 0, 0)
            for c in range(2):
                gelu(0, 0, c)
            all_bodies(act, body)

        @block.gpsimd
        def _(pool):
            def gather(g):
                for t in range(G * g, G * g + G):
                    pool.indirect_dma_start(
                        out=x_res[:, t, :], out_offset=None, in_=w["emb"],
                        in_offset=bass.IndirectOffsetOnAxis(ap=row[:, t:t + 1], axis=0),
                    ).then_inc(gathered[g % AHEAD], 16)

            def add_pos(g):
                pool.wait_ge(gathered[g % AHEAD], 16 * G * (g // AHEAD + 1))
                group = x_res[:, G * g:G * g + G, :].rearrange("p (s j) d -> p s j d", j=T // P)
                pool.tensor_tensor(group, group, pos_sb[:].unsqueeze(1).to_broadcast([P, GT // T, T // P, D]), ALU.add)\
                    .then_inc(pos_added, 1)

            def root(i, n):
                pool.wait_ge(vare_done[i], ONE + n + 1)
                pool.wait_ge(xn_done[i], ONE + G * n)
                pool.tensor_tensor(rstd[i][:], vare[i][:], neg_half[:, 0:G], ALU.pow).then_inc(rstd_done[i], 1)

            def add_b2(n, l, g):
                pool.wait_ge(xn_done[1], ONE + G * (n + 1))
                part = x_res[:, ds(G * g, G), :]
                pool.tensor_tensor(part, part, b2_all[:, ds(l, 1), :].to_broadcast([P, G, D]), ALU.add)\
                    .then_inc(b2_added, 1)

            def ssm_weights(n, l):
                wait_apart(pool, started, y_done, ONE + n)
                weights = ((b_all, [b[:, :, S:2 * S] for b in b_now]), (c_all, [c[:] for c in c_now]),
                           (d_all, [d[:] for d in d_now]))
                for raw, now in weights:
                    pool.tensor_copy(now[0].unsqueeze(1), raw[:, ds(l, 1)]).then_inc(ssm_hi_done, 1)
                wait_apart(pool, started, ssm_hi_done, ONE + 2 + 3 * (l + 1))
                for raw, now in weights:
                    pool.tensor_tensor(now[1].unsqueeze(1), raw[:, ds(l, 1)], now[0].unsqueeze(1).bitcast(F32),
                                       ALU.subtract).then_inc(ssm_w_ready, 1)

            LAG = 3

            def split(n, l, c):
                parts = []
                if c < FC:
                    chunk = slice(P * c, P * c + P)
                    parts.append((w1_raw[:, :, chunk], w1_hi[:, :, chunk], w1_lo[:, :, chunk], c == FC - 1, w1_split))
                if c >= LAG:
                    d = c - LAG
                    parts.append((w2_raw[:, d, :], w2_hi[:, d, :], w2_lo[:, d, :], d == FC - 1, w2_split))
                if c <= FC + 1:
                    wait_apart(pool, started, h_done, ONE + FC * n + c + 1)
                else:
                    wait_apart(pool, started, f_done, ONE + n + 1)
                for raw, hi, _, _, _ in parts:
                    pool.tensor_copy(hi, raw).then_inc(hi_done, 1)
                wait_apart(pool, started, hi_done, ONE + 1 + 2 * FC * (l - 1) + min(c + 1, FC) + max(0, c + 1 - LAG))
                for raw, hi, lo, final, done in parts:
                    ins = pool.tensor_tensor(lo, raw, hi.bitcast(F32), ALU.subtract)
                    if final:
                        ins.then_inc(done, 1)

            def body(n, g, p, l, last):
                g1, g2 = after(g, 1, last), after(g, 2, last)
                turning = g1 is not None and next_layer(g, l) is not l
                if isinstance(l, int) and l == 0:
                    if g + 2 < GROUPS:
                        add_pos(g + 2)
                    if g + AHEAD < GROUPS:
                        gather(g + AHEAD)
                if turning:
                    ssm_weights(n + 1, l + 1)
                    pool.wait_ge(w1_in, ONE + 16 * (l + 2))
                    pool.wait_ge(w2_in, ONE + 16 * (l + 2))
                    for c in range(5):
                        split(n, l + 1, c)
                if g1 is not None:
                    root(1, n + 1)
                if turning:
                    split(n, l + 1, 5)
                elif g1 is not None:
                    add_b2(n + 1, l, g1)
                if g2 is not None:
                    root(0, n + 2)
                if turning:
                    for c in range(6, FC):
                        split(n, l + 1, c)
                    add_b2(n + 1, l + 1, g1)
                    for c in range(FC, FC + LAG):
                        split(n, l + 1, c)
                if last:
                    root(2, g)
                    pool.wait_ge(xn_done[2], ONE + G * (g + 1))
                    pool.tensor_tensor(xn[2][:], xn[2][:], lnf_s[:].unsqueeze(1).to_broadcast([P, G, D]), ALU.mult)\
                        .then_inc(scaled, 1)
                    wait_apart(pool, started, scaled, ONE + g + 1)
                    pool.tensor_tensor(x_res[:, ds(G * g, G), :], xn[2][:],
                                       lnf_b[:].unsqueeze(1).to_broadcast([P, G, D]), ALU.add).then_inc(fin, 1)

            for b in b_now:
                pool.memset(b[:].bitcast(F32), 0.0).then_inc(ssm_hi_done, 1)
            pool.wait_ge(ssm_hi_done, ONE + 2)
            pool.wait_ge(idx_step, ONE + 4)
            gather(0)
            gather(1)
            pool.wait_ge(pos_in, ONE + 16)
            add_pos(0)
            pool.wait_ge(small_in, ONE + SMALL)
            root(0, 0)
            ssm_weights(0, 0)
            add_pos(1)
            gather(2)
            root(1, 0)
            add_b2(0, 0, 0)
            root(0, 1)
            gather(3)
            for g in range(GROUPS):
                body(g, g, g % 2, 0, False)
            with pool.Fori(1, LAYERS - 1) as l:
                layer_of_bodies(pool, l, False, body)
            pool.wait_ge(lnf_in, ONE + 32)
            layer_of_bodies(pool, LAYERS - 1, True, body)
            pool.wait_ge(fin, ONE + GROUPS)


def attention(nc, started, x_res, ident, neg_half, w_qkv, w_out, w_in, parts_dram, w):
    ST = T // P
    QUAD = 4
    DV = 32
    QUADS = HEADS // QUAD
    PER = P // (2 * DH)
    HC = HEADS // PER
    BANKS = 2
    PER_BANK = HC // BANKS
    with ExitStack() as ctx:
        def sb(name, shape, dt=F32):
            return ctx.enter_context(nc.sbuf_tensor(name, shape, dt))

        def psum(name):
            return ctx.enter_context(nc.psum_tensor(name, [P, 512], F32))

        sems = []

        def sem(name):
            sems.append(ctx.enter_context(nc.semaphore(name)))
            return sems[-1]

        w_qk = [sb(f"w_qk_{n}", [P, KD, 2, HEADS, 2, DH], F32R) for n in ("hi", "lo")]
        w_v = [sb(f"w_v_{n}", [P, KD, D], F32R) for n in ("hi", "lo")]
        w_o = [sb(f"w_o_{n}", [P, KD, D], F32R) for n in ("hi", "lo")]
        minus_low = sb("minus_low", [P, 1])
        lane_i, lane_f = sb("a_lane_i", [P, 1], I32), sb("a_lane_f", [P, 1])
        stats, mv = sb("a_stats", [P, ST, 6]), sb("a_mv", [P, ST, 2])
        vare, rstd = sb("a_vare", [P, ST]), sb("a_rstd", [P, ST])
        xn = sb("a_xn", [P, ST, D])
        x_hi, x_lo = sb("a_x_hi", [P, KD, T], F32R), sb("a_x_lo", [P, KD, T], F32R)
        q_hi = sb("q_hi", [P, HC, T], F32R)
        q = [sb(f"q{p}", [P, HC, T], F32R) for p in range(2)]
        k_hi = [sb(f"k_hi{p}", [P, HC, T], F32R) for p in range(2)]
        k_lo = [sb(f"k_lo{p}", [P, HC, T], F32R) for p in range(2)]
        v = [sb(f"v{p}", [P, ST, HEADS, DV]) for p in range(2)]
        nmax = [sb(f"nmax{i}", [P, ST]) for i in range(2)]
        prob = [sb(f"prob{i}", [P, ST, T]) for i in range(2)]
        probT = [sb(f"probT{i}", [P, ST, T]) for i in range(2 * QUAD)]
        raw = [sb(f"expert_raw{i}", [P, KD * F]) for i in range(2)]
        parts = [sb(f"expert_parts{i}", [P, 2, KD * F], F32R) for i in range(2)]
        oT = sb("oT", [P, T])
        rsum = sb("rsum", [P, ST, QUAD])
        o_norm = sb("o_norm", [P, ST, D])
        on_hi, on_lo = sb("on_hi", [P, KD, T], F32R), sb("on_lo", [P, KD, T], F32R)
        ps_s = [psum(f"ps_s{i}") for i in range(2)]
        ps_pt = [psum(f"ps_pt{i}") for i in range(2)]
        ps_p = [psum(f"ps_p{i}") for i in range(2)]
        ps_o, ps_f = psum("ps_o"), psum("ps_f")

        mask_step, v_init = sem("mask_step"), sem("v_init")
        raw_in = [sem(f"raw_in{i}") for i in range(2)]
        hi_done, split_done = [sem(f"e_hi_done{i}") for i in range(2)], [sem(f"e_split_done{i}") for i in range(2)]
        split_stored = [sem(f"split_stored{i}") for i in range(2)]
        stat_done, aggr_done, vare_done, rstd_done, xn_done = map(
            sem, ("a_stat_done", "a_aggr_done", "a_vare_done", "a_rstd_done", "a_xn_done"))
        w_hi_done, w_split = sem("aw_hi_done"), sem("aw_split")
        xt_done, x_hi_done, x_split, v_done, v_evac = map(sem, ("xt_done", "ax_hi_done", "ax_split", "v_done", "v_evac"))
        q_done, q_hi_done, q_split, k_done, k_hi_done, k_split = map(
            sem, ("q_done", "q_hi_done", "q_split", "k_done", "k_hi_done", "k_split"))
        s_done, nmax_done, exp_done, pt_done, pv_done = map(
            sem, ("s_done", "nmax_done", "exp_done", "pt_done", "pv_done"))
        pt_evac = [sem(f"pt_evac{i}") for i in range(2)]
        ot_evac, to_done, rsum_done, norm_done = map(sem, ("ot_evac", "to_done", "rsum_done", "norm_done"))
        on_done, on_hi_done, on_split, out_done, res_done = map(
            sem, ("on_done", "on_hi_done", "on_split", "out_done", "a_res_done"))

        start_at_one(nc, sems)
        block = ctx.enter_context(nc.Block())

        def heads_of(i):
            return w_qkv[:, :, D * i:D * i + D].rearrange("p k (h e) -> p k h e", h=HEADS)

        def scale_of(i):
            return 1.0 / DH ** 0.5 if i == 0 else 1.0

        def wait_probs(eng, b, h):
            eng.wait_ge(pt_done, ONE + HEADS * b + h + 1)
            if h % QUAD < 2 and (h >= 2 * QUAD or not isinstance(b, int) or b):
                eng.wait_ge(pv_done, ONE + QUADS * b + h // QUAD - 1)

        def over_sequences(eng, run):
            run(0, 0, True, False)
            with eng.Fori(0, SEQS // 2 - 1) as i:
                run(2 * i + 1, 1, False, False)
                run(2 * i + 2, 0, False, False)
            run(SEQS - 1, 1, False, True)

        @block.sync
        def _(sp):
            def load(e, i):
                if i == 0:
                    src = w["e_w1"][ds(e, 1)].rearrange("o (k p) f -> p (o k) f", p=P)
                    dst = raw[0][:].rearrange("p (k f) -> p k f", k=KD)
                else:
                    src = w["e_w2"][ds(e, 1)].rearrange("o (c p) d -> p (o c) d", p=P)
                    dst = raw[1][:].rearrange("p (c d) -> p c d", c=FC)
                sp.dma_start(dst, src).then_inc(raw_in[i], 16)

            def store(e, i):
                sp.wait_ge(split_done[i], ONE + e + 1)
                sp.dma_start(parts_dram[ds(e, 1), i].rearrange("o p h x -> p (o h) x"), parts[i][:].bitcast(F32))\
                    .then_inc(split_stored[i], 16)

            load(0, 0)
            load(0, 1)
            with sp.Fori(0, EXPERTS - 1) as e:
                for i in range(2):
                    store(e, i)
                    load(e + 1, i)
            for i in range(2):
                store(EXPERTS - 1, i)
            for i in range(2):
                sp.wait_ge(split_stored[i], ONE + 16 * EXPERTS)

        @block.gpsimd
        def _(pool):
            pool.iota(lane_i[:], pattern=[[1, 1]], base=0, channel_multiplier=1).then_inc(mask_step, 1)
            for p in range(2):
                pool.memset(v[p][:], 0.0).then_inc(v_init, 1)
            pool.wait_ge(v_init, ONE + 2)
            for p in range(2):
                pool.memset(v[p][:, :, :, DH:DH + 1], 1.0).then_inc(v_init, 1)

            def root(b):
                pool.wait_ge(vare_done, ONE + b + 1)
                pool.wait_ge(xn_done, ONE + ST * b)
                pool.tensor_tensor(rstd[:], vare[:], neg_half[:, 0:ST], ALU.pow).then_inc(rstd_done, 1)

            def split(e, i):
                wait_apart(pool, started, raw_in[i], ONE + 16 * (e + 1))
                wait_apart(pool, started, split_stored[i], ONE + 16 * e)
                pool.tensor_copy(parts[i][:, 0], raw[i][:]).then_inc(hi_done[i], 1)
                wait_apart(pool, started, hi_done[i], ONE + e + 1)
                pool.tensor_tensor(parts[i][:, 1], raw[i][:], parts[i][:, 0].bitcast(F32), ALU.subtract)\
                    .then_inc(split_done[i], 1)

            root(0)
            root(1)
            split(0, 0)
            with pool.Fori(0, SEQS // 2 - 1) as e:
                root(2 * e + 2)
                split(e, 1)
                root(2 * e + 3)
                split(e + 1, 0)
            split(EXPERTS - 1, 1)

        @block.tensor
        def _(pe):
            def turn_x(b):
                pe.wait_ge(xn_done, ONE + ST * (b + 1))
                pe.wait_ge(v_evac, ONE + b)
                for k in range(KD):
                    for j in range(ST):
                        last = pe.transpose(ps_p[0][:, T * k + P * j:T * k + P * j + P],
                                            xn[:, j, P * k:P * k + P], ident)
                last.then_inc(xt_done, 1)

            def project(i, c):
                out = ps_p[c // PER_BANK][:, T * (c % PER_BANK):T * (c % PER_BANK) + T]
                for k in range(KD):
                    for n, (part, x) in enumerate([(0, x_hi), (0, x_lo), (1, x_hi)]):
                        last = pe.matmul(out, w_qk[part][:, k, i, PER * c:PER * c + PER].rearrange("p h r e -> p (h r e)"),
                                         x[:, k, :], start=(k == 0 and n == 0), stop=(k == KD - 1 and n == 2))
                if c % PER_BANK == PER_BANK - 1:
                    last.then_inc((q_done, k_done)[i], 1)

            def project_q(b, c):
                if c == 0:
                    pe.wait_ge(x_split, ONE + b + 1)
                    pe.wait_ge(k_split, ONE + BANKS * b)
                project(0, c)

            def project_k(b, c):
                if c % PER_BANK == 0:
                    pe.wait_ge(q_split, ONE + BANKS * b + c // PER_BANK + 1)
                project(1, c)

            def project_v(b, j):
                pe.wait_ge(k_split, ONE + BANKS * b + 1)
                for k in range(KD):
                    for n, (x, part) in enumerate([(x_hi, 0), (x_hi, 1), (x_lo, 0)]):
                        last = pe.matmul(ps_p[0][:, D * j:D * j + D], x[:, k, P * j:P * j + P], w_v[part][:, k, :],
                                         start=(k == 0 and n == 0), stop=(k == KD - 1 and n == 2))
                if j == ST - 1:
                    last.then_inc(v_done, 1)

            def scores(b, p, h):
                if h % (HEADS // BANKS) == 0:
                    pe.wait_ge(q_split, ONE + BANKS * b + h // (HEADS // BANKS) + 1)
                    pe.wait_ge(k_split, ONE + BANKS * b + h // (HEADS // BANKS) + 1)
                c, rows = h // PER, slice(2 * DH * (h % PER), 2 * DH * (h % PER) + 2 * DH)
                for i in range(ST):
                    for n, key in enumerate((k_hi[p], k_lo[p])):
                        last = pe.matmul(ps_s[h % 2][:, T * i:T * i + T], q[p][rows, c, P * i:P * i + P],
                                         key[rows, c, :], start=(n == 0), stop=(n == 1))
                last.then_inc(s_done, 1)

            def turn_probs(b, h):
                pe.wait_ge(exp_done, ONE + ST * (HEADS * b + h + 1))
                pe.wait_ge(pt_evac[h % 2], ONE + HEADS // 2 * b + h // 2)
                for j in range(ST):
                    for i in range(ST):
                        last = pe.transpose(ps_pt[h % 2][:, T * j + P * i:T * j + P * i + P],
                                            prob[h % 2][:, i, P * j:P * j + P], ident)
                last.then_inc(pt_done, 1)

            def weigh(b, p, u):
                for i in range(2):
                    pe.wait_ge(pt_evac[i], ONE + HEADS // 2 * b + QUAD // 2 * (u + 1))
                if u == 0:
                    pe.wait_ge(v_evac, ONE + b + 1)
                pe.wait_ge(ot_evac, ONE + QUADS * b + u)
                for j in range(ST):
                    for i in range(QUAD):
                        h = QUAD * u + i
                        last = pe.matmul(ps_o[DV * i:DV * i + DV, 0:T], v[p][:, j, h, :],
                                         probT[h % (2 * QUAD)][:, j, :], start=(j == 0), stop=(j == ST - 1))
                last.then_inc(pv_done, 1)

            def turn_quad(b, u):
                pe.wait_ge(ot_evac, ONE + QUADS * b + u + 1)
                if u == 0:
                    pe.wait_ge(res_done, ONE + b)
                else:
                    pe.wait_ge(norm_done, ONE + QUADS * b + u)
                for i in range(ST):
                    last = pe.transpose(ps_f[:, P * i:P * i + P], oT[:, P * i:P * i + P], ident)
                last.then_inc(to_done, 1)

            def turn_out(b):
                pe.wait_ge(norm_done, ONE + QUADS * (b + 1))
                for k in range(KD):
                    for i in range(ST):
                        last = pe.transpose(ps_f[:, T * k + P * i:T * k + P * i + P],
                                            o_norm[:, i, P * k:P * k + P], ident)
                last.then_inc(on_done, 1)

            def project_out(b, i):
                pe.wait_ge(on_split, ONE + b + 1)
                for k in range(KD):
                    for n, (o, part) in enumerate([(on_hi, 0), (on_hi, 1), (on_lo, 0)]):
                        last = pe.matmul(ps_f[:, D * i:D * i + D], o[:, k, P * i:P * i + P], w_o[part][:, k, :],
                                         start=(k == 0 and n == 0), stop=(k == KD - 1 and n == 2))
                if i == ST - 1:
                    last.then_inc(out_done, 1)

            def sequence(b, p, first, last):
                for h in range(HEADS):
                    turn_probs(b, h)
                    if h + 2 < HEADS:
                        scores(b, p, h + 2)
                    elif not last:
                        scores(b + 1, 1 - p, h + 2 - HEADS)
                    if not first:
                        if h == 0:
                            turn_quad(b - 1, QUADS - 2)
                        if h == 1:
                            weigh(b - 1, 1 - p, QUADS - 1)
                        if h == 3:
                            turn_quad(b - 1, QUADS - 1)
                        if h == 4:
                            turn_out(b - 1)
                        if h in (6, 7):
                            project_out(b - 1, h - 6)
                    if h in (5, 9, 13):
                        weigh(b, p, h // QUAD - 1)
                    if h in (8, 12):
                        turn_quad(b, h // QUAD - 2)
                    if not last:
                        if h == 3:
                            turn_x(b + 1)
                        if 6 <= h < 10:
                            project_q(b + 1, h - 6)
                        if 10 <= h < 14:
                            project_k(b + 1, h - 10)
                        if 14 <= h < 16:
                            project_v(b + 1, h - 14)

            turn_x(0)
            pe.wait_ge(w_split, ONE + 4)
            for c in range(HC):
                project_q(0, c)
            for c in range(HC):
                project_k(0, c)
            for j in range(ST):
                project_v(0, j)
            scores(0, 0, 0)
            scores(0, 0, 1)
            pe.wait_ge(v_init, ONE + 4)
            over_sequences(pe, sequence)
            turn_quad(SEQS - 1, QUADS - 2)
            weigh(SEQS - 1, 1, QUADS - 1)
            turn_quad(SEQS - 1, QUADS - 1)
            turn_out(SEQS - 1)
            for i in range(ST):
                project_out(SEQS - 1, i)

        @block.vector
        def _(dve):
            def statistics(b):
                for j in range(ST):
                    dve.bn_stats(stats[:, j, :], x_res[:, ds(ST * b + j, 1), :]).then_inc(stat_done, 1)
                wait_apart(dve, started, stat_done, ONE + ST * (b + 1))
                for j in range(ST):
                    dve.bn_aggr(mv[:, j, :], stats[:, j, :]).then_inc(aggr_done, 1)
                dve.wait_ge(aggr_done, ONE + ST * (b + 1))
                dve.wait_ge(rstd_done, ONE + b)
                dve.tensor_scalar(vare[:], mv[:, :, 1], EPS, None, ALU.add).then_inc(vare_done, 1)

            def normalise(b):
                dve.wait_ge(rstd_done, ONE + b + 1)
                dve.wait_ge(xt_done, ONE + b)
                for j in range(ST):
                    dve.tensor_scalar(xn[:, j, :], x_res[:, ds(ST * b + j, 1), :].rearrange("p o d -> p (o d)"),
                                      mv[:, j, 0:1], rstd[:, j:j + 1], ALU.subtract, ALU.mult).then_inc(xn_done, 1)

            def row_max(b, h):
                m = HEADS * b + h
                dve.wait_ge(s_done, ONE + m + 1)
                dve.tensor_reduce(nmax[h % 2][:], ps_s[h % 2][:].rearrange("p (i j) -> p i j", i=ST), AX.X, ALU.max,
                                  negate=True).then_inc(nmax_done, 1)

            def x_rest(b):
                dve.wait_ge(x_hi_done, ONE + b + 1)
                dve.tensor_tensor(x_lo[:].rearrange("p k t -> p (k t)"), ps_p[0][:],
                                  x_hi[:].rearrange("p k t -> p (k t)").bitcast(F32), ALU.subtract).then_inc(x_split, 1)

            def bank_of(x, i):
                return x[:, PER_BANK * i:PER_BANK * (i + 1), :].rearrange("p c t -> p (c t)")

            def q_rest(b, p, i):
                dve.wait_ge(q_hi_done, ONE + BANKS * b + i + 1)
                dve.scalar_tensor_tensor(out=bank_of(q[p], i), in0=bank_of(q_hi, i).bitcast(F32),
                                         scalar=minus_low[:], in1=ps_p[i][:], op0=ALU.mult, op1=ALU.add)\
                   .then_inc(q_split, 1)

            def k_rest(b, p, i):
                dve.wait_ge(k_hi_done, ONE + BANKS * b + i + 1)
                dve.tensor_tensor(bank_of(k_lo[p], i), ps_p[i][:], bank_of(k_hi[p], i).bitcast(F32), ALU.subtract)\
                   .then_inc(k_split, 1)

            def out_rest(b):
                dve.wait_ge(on_hi_done, ONE + b + 1)
                dve.tensor_tensor(on_lo[:].rearrange("p k t -> p (k t)"), ps_f[:],
                                  on_hi[:].rearrange("p k t -> p (k t)").bitcast(F32), ALU.subtract).then_inc(on_split, 1)

            def divide(b, u):
                n = QUADS * b + u
                quad = ps_f[:, 0:T].rearrange("p (i h e) -> p i h e", i=ST, h=QUAD)
                dve.wait_ge(to_done, ONE + n + 1)
                dve.reciprocal(rsum[:].unsqueeze(3), quad[:, :, :, DH:DH + 1]).then_inc(rsum_done, 1)
                dve.wait_ge(rsum_done, ONE + n + 1)
                if u == 0:
                    dve.wait_ge(on_done, ONE + b)
                dve.tensor_tensor(o_norm[:, :, QUAD * DH * u:QUAD * DH * (u + 1)].rearrange("p i (h e) -> p i h e", h=QUAD),
                                  quad[:, :, :, 0:DH], rsum[:].unsqueeze(3).to_broadcast([P, ST, QUAD, DH]),
                                  ALU.mult).then_inc(norm_done, 1)

            def residual(b):
                dve.wait_ge(out_done, ONE + b + 1)
                pair = x_res[:, ds(ST * b, ST), :]
                dve.tensor_tensor(pair, ps_f[:].rearrange("p (j d) -> p j d", j=ST), pair, ALU.add)\
                   .then_inc(res_done, 1)

            def sequence(b, p, first, last):
                for h in range(HEADS):
                    if h % 2 == 0:
                        wait_probs(dve, b, h)
                        dve.tensor_copy(probT[h % (2 * QUAD)][:].rearrange("p j i -> p (j i)"), ps_pt[0][:])\
                            .then_inc(pt_evac[0], 1)
                    if h + 2 < HEADS:
                        row_max(b, h + 2)
                    elif not last:
                        row_max(b + 1, h + 2 - HEADS)
                    if not first:
                        if h == 1:
                            divide(b - 1, QUADS - 2)
                        if h == 3:
                            divide(b - 1, QUADS - 1)
                        if h == 5:
                            out_rest(b - 1)
                        if h == 7:
                            residual(b - 1)
                    if h in (9, 13):
                        divide(b, h // QUAD - 2)
                    if not last:
                        if h == 0:
                            statistics(b + 1)
                        if h == 1:
                            normalise(b + 1)
                        if h == 5:
                            x_rest(b + 1)
                        if h in (9, 11):
                            q_rest(b + 1, 1 - p, h // 2 - 4)
                        if h in (13, 15):
                            k_rest(b + 1, 1 - p, h // 2 - 6)

            statistics(0)
            normalise(0)
            dve.wait_ge(mask_step, ONE + 1)
            dve.tensor_scalar(lane_i[:], lane_i[:], DH, None, ALU.bitwise_and).then_inc(mask_step, 1)
            dve.wait_ge(mask_step, ONE + 2)
            dve.tensor_copy(lane_f[:], lane_i[:]).then_inc(mask_step, 1)
            dve.wait_ge(mask_step, ONE + 3)
            dve.tensor_scalar(minus_low[:], lane_f[:], -1.0 / DH, None, ALU.mult).then_inc(mask_step, 1)
            dve.wait_ge(w_hi_done, ONE + 4)
            for i in range(2):
                for k in range(KD):
                    for rep in range(2):
                        last = dve.scalar_tensor_tensor(
                            out=w_qk[1][:, k, i, :, rep], in0=heads_of(i)[:, k], scalar=scale_of(i),
                            in1=w_qk[0][:, k, i, :, rep].bitcast(F32), op0=ALU.mult, op1=ALU.subtract)
                last.then_inc(w_split, 1)
            dve.tensor_tensor(w_v[1][:], w_qkv[:, :, 2 * D:3 * D], w_v[0][:].bitcast(F32), ALU.subtract).then_inc(w_split, 1)
            dve.tensor_tensor(w_o[1][:], w_out[:], w_o[0][:].bitcast(F32), ALU.subtract).then_inc(w_split, 1)
            dve.wait_ge(mask_step, ONE + 4)
            x_rest(0)
            for i in range(BANKS):
                q_rest(0, 0, i)
            for i in range(BANKS):
                k_rest(0, 0, i)
            row_max(0, 0)
            row_max(0, 1)
            over_sequences(dve, sequence)
            divide(SEQS - 1, QUADS - 2)
            divide(SEQS - 1, QUADS - 1)
            out_rest(SEQS - 1)
            residual(SEQS - 1)
            dve.wait_ge(res_done, ONE + SEQS)

        @block.scalar
        def _(act):
            def x_out(b):
                act.wait_ge(xt_done, ONE + b + 1)
                act.wait_ge(v_done, ONE + b)
                act.activation(x_hi[:].rearrange("p k t -> p (k t)"), ps_p[0][:], ACT.Copy).then_inc(x_hi_done, 1)

            def high(x, i, done):
                act.activation(x[:, PER_BANK * i:PER_BANK * (i + 1), :].rearrange("p c t -> p (c t)"), ps_p[i][:],
                               ACT.Copy).then_inc(done, 1)

            def q_out(b, i):
                act.wait_ge(q_done, ONE + BANKS * b + i + 1)
                high(q_hi, i, q_hi_done)

            def k_out(b, p, i):
                act.wait_ge(k_done, ONE + BANKS * b + i + 1)
                high(k_hi[p], i, k_hi_done)

            def v_out(b, p):
                act.wait_ge(v_done, ONE + b + 1)
                act.activation(v[p][:, :, :, 0:DH], ps_p[0][:].rearrange("p (j h e) -> p j h e", j=ST, h=HEADS),
                               ACT.Copy).then_inc(v_evac, 1)

            def exponentials(b, h):
                act.wait_ge(nmax_done, ONE + HEADS * b + h + 1)
                for i in range(ST):
                    act.activation(prob[h % 2][:, i, :], ps_s[h % 2][:, T * i:T * i + T], ACT.Exp,
                                   bias=nmax[h % 2][:, i:i + 1]).then_inc(exp_done, 1)

            def quad_out(b, u):
                n = QUADS * b + u
                act.wait_ge(pv_done, ONE + n + 1)
                act.wait_ge(to_done, ONE + n)
                act.activation(oT[:], ps_o[:, 0:T], ACT.Copy).then_inc(ot_evac, 1)

            def out_out(b):
                act.wait_ge(on_done, ONE + b + 1)
                act.wait_ge(out_done, ONE + b)
                act.activation(on_hi[:].rearrange("p k t -> p (k t)"), ps_f[:], ACT.Copy).then_inc(on_hi_done, 1)

            def sequence(b, p, first, last):
                for h in range(HEADS):
                    if h % 2 == 1:
                        wait_probs(act, b, h)
                        act.activation(probT[h % (2 * QUAD)][:].rearrange("p j i -> p (j i)"), ps_pt[1][:], ACT.Copy)\
                            .then_inc(pt_evac[1], 1)
                    if h + 2 < HEADS:
                        exponentials(b, h + 2)
                    elif not last:
                        exponentials(b + 1, h + 2 - HEADS)
                    if not first:
                        if h == 0:
                            v_out(b, p)
                        if h == 1:
                            quad_out(b - 1, QUADS - 1)
                        if h == 4:
                            out_out(b - 1)
                    if h in (5, 9, 13):
                        quad_out(b, h // QUAD - 1)
                    if not last:
                        if h == 4:
                            x_out(b + 1)
                        if h in (8, 10):
                            q_out(b + 1, h // 2 - 4)
                        if h in (12, 14):
                            k_out(b + 1, 1 - p, h // 2 - 6)

            act.wait_ge(w_in, 32)
            for i in range(2):
                for rep in range(2):
                    last = act.activation(w_qk[0][:, :, i, :, rep], heads_of(i), ACT.Copy, scale=scale_of(i))
                last.then_inc(w_hi_done, 1)
            act.activation(w_v[0][:], w_qkv[:, :, 2 * D:3 * D], ACT.Copy).then_inc(w_hi_done, 1)
            act.activation(w_o[0][:], w_out[:], ACT.Copy).then_inc(w_hi_done, 1)
            x_out(0)
            for i in range(BANKS):
                q_out(0, i)
            for i in range(BANKS):
                k_out(0, 0, i)
            act.wait_ge(v_init, ONE + 4)
            v_out(0, 0)
            exponentials(0, 0)
            exponentials(0, 1)
            over_sequences(act, sequence)
            quad_out(SEQS - 1, QUADS - 1)
            out_out(SEQS - 1)


def load_expert(eng, ring, ring_in, parts_dram, e):
    for i in range(2):
        eng.dma_start(ring[:, e % RING, i].bitcast(F32), parts_dram[e, i].rearrange("p h x -> p (h x)"))\
            .then_inc(ring_in[e % RING], 16)


def route(nc, started, x_res, xn_dram, ident, neg_half, ring, ring_in, parts_dram, w, r):
    E, L = EXPERTS, LANGS
    with ExitStack() as ctx:
        def sb(name, shape, dt=F32):
            return ctx.enter_context(nc.sbuf_tensor(name, shape, dt))

        def psum(name, cols=512):
            return ctx.enter_context(nc.psum_tensor(name, [P, cols], F32))

        sems = []

        def sem(name):
            sems.append(ctx.enter_context(nc.semaphore(name)))
            return sems[-1]

        w_r = sb("w_r", [P, KD, E + L])
        bias = sb("r_bias", [P, E + L])
        stats, mv = [sb(f"r_stats{i}", [P, G, 6]) for i in range(2)], [sb(f"r_mv{i}", [P, G, 2]) for i in range(2)]
        vare, rstd = [sb(f"r_vare{i}", [P, G]) for i in range(2)], [sb(f"r_rstd{i}", [P, G]) for i in range(2)]
        xn = [sb(f"r_xn{i}", [P, G, D]) for i in range(2)]
        xT = sb("r_xT", [P, KD, GT])
        logits = sb("logits", [P, TILES, E + L])
        col = [sb(f"r_col{i}", [P, TILES, 1]) for i in range(6)]
        lang = sb("lang", [P, TILES, L + 1])
        ew = sb("ew", [P, TILES, L])
        pr = [sb(f"r_pr{i}", [P, TILES, E]) for i in range(3)]
        hot = [sb(f"hot{i}", [P, TILES, E]) for i in range(2)]
        both = sb("both", [P, TILES, E])
        rev = sb("rev", [P, E])
        lane_i, lane_f = sb("lane_i", [P, P], I32), sb("lane_f", [P, P])
        token_i, token_f = sb("token_i", [P, TILES], I32), sb("token_f", [P, TILES])
        thresholds = sb("thresholds", [P, TILES])
        before = sb("before", [P, P])
        ones = sb("r_ones", [P, P])
        totals = sb("totals", [P, E, TILES])
        keep = sb("keep", [P, E, TILES])
        running = sb("running", [P, E, TILES])
        place = sb("place", [P, E, TILES])
        over = sb("over", [P, E, TILES])
        part_blocks = sb("part_blocks", [P, E])
        turns = [sb(f"ring_turns{i}", [P, BLOCKS]) for i in range(2)]
        blocks_of, ends, starts = sb("blocks_of", [P, E]), sb("ends", [P, E]), sb("starts", [P, E])
        past = sb("past", [P, BLOCKS, E])
        block_f = sb("block_f", [P, BLOCKS, 1])
        slot_f = [sb(f"slot_f{i}", [P, TILES, 1]) for i in range(2)]
        slot_i = [sb(f"slot_i{i}", [P, TILES], I32) for i in range(2)]
        part_i = [sb(f"part_i{i}", [P, TILES], I32) for i in range(4)]
        part_f = [sb(f"part_f{i}", [P, TILES]) for i in range(4)]
        lane_hot = [sb(f"lane_hot{i}", [P, P]) for i in range(4)]
        block_hot = [sb(f"block_hot{i}", [P, BLOCKS]) for i in range(4)]
        ps_t = [psum(f"r_ps_t{i}") for i in range(2)]
        ps_l = [psum(f"ps_l{i}") for i in range(2)]
        ps_rank, ps_tot, ps_tab = psum("ps_rank"), psum("ps_tot"), psum("ps_tab")

        w_in, const = sem("rw_in"), sem("r_const")
        stat_done, aggr_done, vare_done, rstd_done, xn_done = map(
            sem, ("r_stat", "r_aggr", "r_vare_done", "r_rstd_done", "r_xn_done"))
        xn_stored = [sem(f"xn_stored{i}") for i in range(2)]
        t_done, t_evac, l_done, l_evac = map(sem, ("r_t_done", "r_t_evac", "l_done", "l_evac"))
        chain, exp_go, exp_back, both_ready, rank_done, hot_ready, table_used = map(
            sem, ("r_chain", "exp_go", "exp_back", "both_ready", "rank_done", "hot_ready", "table_used"))
        CONSTS = 10

        start_at_one(nc, sems)
        block = ctx.enter_context(nc.Block())

        @block.sync
        def _(sp):
            sp.dma_start(w_r[:], w["routerT"].rearrange("(k p) e -> p k e", p=P)).then_inc(w_in, 16)
            sp.dma_start(bias[:, 0:E], w["router_b"].rearrange("(o e) -> o e", o=1).to_broadcast([P, E])).then_inc(w_in, 16)
            sp.dma_start(bias[:, E:E + L], w["lang_b"].rearrange("(o e) -> o e", o=1).to_broadcast([P, L])).then_inc(w_in, 16)
            with sp.Fori(0, GROUPS // 2) as n:
                for p in range(2):
                    g = 2 * n + p
                    sp.wait_ge(xn_done, ONE + G * (g + 1))
                    sp.dma_start(xn_dram[ds(GT * g, GT), :].rearrange("(j p) d -> p j d", p=P), xn[p][:])\
                        .then_inc(xn_stored[p], 16)
            for e in range(RING):
                load_expert(sp, ring, ring_in, parts_dram, e)
            for p in range(2):
                sp.wait_ge(xn_stored[p], ONE + 16 * GROUPS // 2)

        @block.gpsimd
        def _(pool):
            pool.iota(lane_i[:], pattern=[[1, P]], base=0, channel_multiplier=0).then_inc(const, 1)
            pool.iota(token_i[:], pattern=[[P, TILES]], base=0, channel_multiplier=1).then_inc(const, 1)
            pool.memset(ones[:], 1.0).then_inc(const, 1)
            pool.memset(keep[:], 1.0).then_inc(const, 1)
            pool.memset(lang[:], 0.0).then_inc(const, 1)
            pool.wait_ge(const, ONE + 5)
            pool.tensor_copy(lane_f[:], lane_i[:]).then_inc(const, 1)
            pool.tensor_copy(token_f[:], token_i[:]).then_inc(const, 1)
            pool.affine_select(out=before[:], in_=ones[:], compare_op=ALU.is_ge, fill=0.0, base=-1,
                               pattern=[[1, P]], channel_multiplier=-1).then_inc(const, 1)
            pool.memset(keep[:, :, 0:1], 0.0).then_inc(const, 1)
            pool.wait_ge(const, ONE + 9)
            pool.tensor_scalar(rev[:], lane_f[:, 0:E], -1.0, float(E), ALU.mult, ALU.add).then_inc(const, 1)

            def root(g, p):
                pool.wait_ge(vare_done, ONE + g + 1)
                if not isinstance(g, int) or g > 1:
                    pool.wait_ge(xn_done, ONE + G * (g - 1))
                pool.tensor_tensor(rstd[p][:], vare[p][:], neg_half[:, 0:G], ALU.pow).then_inc(rstd_done, 1)

            root(0, 0)
            root(1, 1)
            with pool.Fori(1, GROUPS // 2) as n:
                for p in range(2):
                    root(2 * n + p, p)

        @block.tensor
        def _(pe):
            def logits_of(g, p):
                pe.wait_ge(xn_done, ONE + G * (g + 1))
                pe.wait_ge(t_evac, ONE + KD * g)
                for k in range(KD):
                    for j in range(G):
                        last = pe.transpose(ps_t[k][:, P * j:P * j + P], xn[p][:, j, P * k:P * k + P], ident)
                last.then_inc(t_done, 1)
                pe.wait_ge(t_evac, ONE + KD * (g + 1))
                if not isinstance(g, int) or g > 1:
                    pe.wait_ge(l_evac, ONE + g - 1)
                for j in range(G):
                    for k in range(KD):
                        last = pe.matmul(ps_l[p][:, (E + L) * j:(E + L) * (j + 1)], xT[:, k, P * j:P * j + P],
                                         w_r[:, k, :], start=(k == 0), stop=(k == KD - 1))
                last.then_inc(l_done, 1)

            pe.wait_ge(w_in, ONE + 48)
            logits_of(0, 0)
            logits_of(1, 1)
            with pe.Fori(1, GROUPS // 2) as n:
                for p in range(2):
                    logits_of(2 * n + p, p)
            pe.wait_ge(both_ready, ONE + 1)
            pe.wait_ge(const, ONE + CONSTS)
            flat = both[:].rearrange("p t e -> p (t e)")
            pe.matmul(ps_rank[:, 0:TILES * E], before[:], flat, start=True, stop=True)
            pe.matmul(ps_tot[:, 0:TILES * E], ones[:], flat, start=True, stop=True).then_inc(rank_done, 1)
            def table(n, i, first=False, last=False):
                pe.wait_ge(hot_ready, ONE + 2 * (n + 1))
                pe.matmul(ps_tab[:, 0:BLOCKS], lane_hot[i][:], block_hot[i][:], start=first, stop=last,
                          skip_group_check=True).then_inc(table_used, 1)

            for i in range(4):
                table(i, i, first=(i == 0))
            with pe.Fori(1, 2 * TILES // 4 - 1) as n:
                for i in range(4):
                    table(4 * n + i, i)
            for i in range(4):
                table(2 * TILES - 4 + i, i, last=(i == 3))

        @block.scalar
        def _(act):
            with act.Fori(0, GROUPS) as g:
                act.wait_ge(t_done, ONE + g + 1)
                act.wait_ge(l_done, ONE + g)
                for k in range(KD):
                    act.activation(xT[:, k, :], ps_t[k][:], ACT.Copy).then_inc(t_evac, 1)
            act.wait_ge(exp_go, ONE + 1)
            act.activation(lang[:, :, 0:L], logits[:, :, E:E + L], ACT.Exp).then_inc(exp_back, 1)
            act.wait_ge(exp_go, ONE + 2)
            act.activation(pr[1][:], pr[0][:], ACT.Exp).then_inc(exp_back, 1)

        @block.vector
        def _(dve):
            links = [0]

            def link(ins):
                links[0] += 1
                ins.then_inc(chain, 1)
                dve.wait_ge(chain, ONE + links[0])

            def statistics(g, p):
                for j in range(G):
                    dve.bn_stats(stats[p][:, j, :], x_res[:, ds(G * g + j, 1), :]).then_inc(stat_done, 1)
                wait_apart(dve, started, stat_done, ONE + G * (g + 1))
                for j in range(G):
                    dve.bn_aggr(mv[p][:, j, :], stats[p][:, j, :]).then_inc(aggr_done, 1)
                dve.wait_ge(aggr_done, ONE + G * (g + 1))
                dve.tensor_scalar(vare[p][:], mv[p][:, :, 1], EPS, None, ALU.add).then_inc(vare_done, 1)

            def normalise(g, p, pair):
                dve.wait_ge(rstd_done, ONE + g + 1)
                if not isinstance(g, int) or g > 1:
                    dve.wait_ge(t_done, ONE + g - 1)
                dve.wait_ge(xn_stored[p], ONE + 16 * pair)
                for j in range(G):
                    dve.tensor_scalar(xn[p][:, j, :], x_res[:, ds(G * g + j, 1), :].rearrange("p o d -> p (o d)"),
                                      mv[p][:, j, 0:1], rstd[p][:, j:j + 1], ALU.subtract, ALU.mult).then_inc(xn_done, 1)

            def logits_out(g, p):
                dve.wait_ge(l_done, ONE + g + 1)
                dve.tensor_tensor(logits[:, ds(G * g, G), :], ps_l[p][:, 0:G * (E + L)].rearrange("p (j e) -> p j e", j=G),
                                  bias[:].unsqueeze(1).to_broadcast([P, G, E + L]), ALU.add).then_inc(l_evac, 1)

            dve.wait_ge(w_in, ONE + 48)
            statistics(0, 0)
            normalise(0, 0, 0)
            statistics(1, 1)
            with dve.Fori(0, GROUPS // 2 - 1) as n:
                for p in range(2):
                    g = 2 * n + p
                    normalise(g + 1, 1 - p, n + p)
                    statistics(g + 2, p)
                    logits_out(g, p)
            normalise(GROUPS - 1, 1, GROUPS // 2 - 1)
            logits_out(GROUPS - 2, 0)
            logits_out(GROUPS - 1, 1)
            dve.wait_ge(l_evac, ONE + GROUPS)
            dve.wait_ge(const, ONE + CONSTS)

            def wide(c, n):
                return c[:].to_broadcast([P, TILES, n])

            link(dve.tensor_reduce(col[0][:, :, 0], logits[:, :, E:E + L], AX.X, ALU.max))
            dve.tensor_tensor(logits[:, :, E:E + L], logits[:, :, E:E + L], wide(col[0], L), ALU.subtract)\
               .then_inc(exp_go, 1)
            dve.wait_ge(exp_back, ONE + 1)
            link(dve.tensor_reduce(col[1][:, :, 0], lang[:, :, 0:L], AX.X, ALU.add))
            link(dve.reciprocal(col[2][:], col[1][:]))
            link(dve.tensor_tensor(lang[:, :, 0:L], lang[:, :, 0:L], wide(col[2], L), ALU.mult))
            link(dve.tensor_tensor(ew[:], lang[:, :, 0:L], lang[:, :, 1:L + 1], ALU.add))
            for i in range(E // L):
                link(dve.scalar_tensor_tensor(out=pr[2][:, :, L * i:L * i + L], in0=ew[:], scalar=0.1,
                                              in1=logits[:, :, L * i:L * i + L], op0=ALU.mult, op1=ALU.add))
            link(dve.tensor_reduce(col[0][:, :, 0], pr[2][:], AX.X, ALU.max))
            dve.tensor_tensor(pr[0][:], pr[2][:], wide(col[0], E), ALU.subtract).then_inc(exp_go, 1)
            dve.wait_ge(exp_back, ONE + 2)
            link(dve.tensor_reduce(col[1][:, :, 0], pr[1][:], AX.X, ALU.add))
            link(dve.reciprocal(col[2][:], col[1][:]))
            link(dve.tensor_tensor(pr[0][:], pr[1][:], wide(col[2], E), ALU.mult))
            best = [col[3], col[4]]
            for i in range(2):
                link(dve.tensor_reduce(best[i][:, :, 0], pr[0][:], AX.X, ALU.max))
                link(dve.tensor_tensor(pr[1][:], pr[0][:], wide(best[i], E), ALU.is_equal))
                link(dve.tensor_tensor(pr[2][:], pr[1][:], rev[:].unsqueeze(1).to_broadcast([P, TILES, E]), ALU.mult))
                link(dve.tensor_reduce(col[5][:, :, 0], pr[2][:], AX.X, ALU.max))
                link(dve.tensor_tensor(hot[i][:], rev[:].unsqueeze(1).to_broadcast([P, TILES, E]), wide(col[5], E),
                                       ALU.is_equal))
                if i == 0:
                    link(dve.scalar_tensor_tensor(out=pr[0][:], in0=hot[0][:], scalar=-2.0, in1=pr[0][:],
                                                  op0=ALU.mult, op1=ALU.add))
            link(dve.tensor_tensor(col[0][:], best[0][:], best[1][:], ALU.add))
            link(dve.reciprocal(col[1][:], col[0][:]))
            for i in range(2):
                link(dve.tensor_tensor(r["weight"][i][:].unsqueeze(2), best[i][:], col[1][:], ALU.mult))
            dve.tensor_tensor(both[:], hot[0][:], hot[1][:], ALU.add).then_inc(both_ready, 1)
            dve.wait_ge(rank_done, ONE + 1)
            link(dve.tensor_copy(totals[:], ps_tot[:, 0:TILES * E].rearrange("p (t e) -> p e t", e=E)))
            link(dve.tensor_tensor_scan(running[:].rearrange("p e t -> p (e t)"), keep[:].rearrange("p e t -> p (e t)"),
                                        totals[:].rearrange("p e t -> p (e t)"), 0.0, ALU.mult, ALU.add))
            link(dve.tensor_scalar(thresholds[:], lane_f[:, 0:TILES], float(P), None, ALU.mult))
            link(dve.tensor_tensor(over[:], running[:, :, TILES - 1:TILES].to_broadcast([P, E, TILES]),
                                   thresholds[:].unsqueeze(1).to_broadcast([P, E, TILES]), ALU.is_gt))
            link(dve.tensor_reduce(part_blocks[:], over[:], AX.X, ALU.add))
            link(dve.tensor_scalar(blocks_of[:], part_blocks[:], 1.0, None, ALU.max))
            link(dve.tensor_tensor_scan(ends[:], ones[:, 0:E], blocks_of[:], 0.0, ALU.mult, ALU.add))
            link(dve.tensor_tensor(starts[:], ends[:], blocks_of[:], ALU.subtract))
            link(dve.tensor_tensor(past[:], lane_f[:, 0:BLOCKS].unsqueeze(2).to_broadcast([P, BLOCKS, E]),
                                   ends[:].unsqueeze(1).to_broadcast([P, BLOCKS, E]), ALU.is_ge))
            link(dve.tensor_reduce(block_f[:, :, 0], past[:], AX.X, ALU.add))
            link(dve.tensor_scalar(r["expert"][:], block_f[:, :, 0], float(E - 1), None, ALU.min))
            link(dve.tensor_copy(r["end"][:], ends[:]))
            link(dve.tensor_scalar(turns[0][:], block_f[:, :, 0], float(E - 1), None, ALU.min))
            for e in range(RING, E, RING):
                link(dve.tensor_scalar(turns[1][:], block_f[:, :, 0], float(e), float(-RING), ALU.is_ge, ALU.mult))
                link(dve.tensor_tensor(turns[0][:], turns[0][:], turns[1][:], ALU.add))
            link(dve.tensor_copy(r["ring"][:], turns[0][:]))
            link(dve.tensor_tensor(place[:], running[:], totals[:], ALU.subtract))
            link(dve.tensor_tensor(running[:], place[:], ps_rank[:, 0:TILES * E].rearrange("p (t e) -> p e t", e=E), ALU.add))
            link(dve.scalar_tensor_tensor(out=place[:], in0=starts[:].unsqueeze(2).to_broadcast([P, E, TILES]),
                                          scalar=float(P), in1=running[:], op0=ALU.mult, op1=ALU.add))
            for i in range(2):
                link(dve.tensor_tensor(pr[i][:], hot[i][:], place[:].rearrange("p e t -> p t e"), ALU.mult))
                link(dve.tensor_reduce(slot_f[i][:, :, 0], pr[i][:], AX.X, ALU.add))
                link(dve.tensor_copy(r["slot"][i][:], slot_f[i][:, :, 0]))
                link(dve.tensor_copy(slot_i[i][:], slot_f[i][:, :, 0]))
                link(dve.tensor_scalar(part_i[2 * i][:], slot_i[i][:], P - 1, None, ALU.bitwise_and))
                link(dve.tensor_scalar(part_i[2 * i + 1][:], slot_i[i][:], P.bit_length() - 1, None,
                                       ALU.logical_shift_right))
                for j in (2 * i, 2 * i + 1):
                    link(dve.tensor_copy(part_f[j][:], part_i[j][:]))

            def one_hots(t, u, i):
                b = 2 * u + i
                dve.tensor_scalar(lane_hot[b][:], lane_f[:], part_f[2 * i][:, ds(t, 1)], None,
                                  ALU.is_equal).then_inc(hot_ready, 1)
                dve.tensor_scalar(block_hot[b][:], lane_f[:, 0:BLOCKS], part_f[2 * i + 1][:, ds(t, 1)],
                                  token_f[:, ds(t, 1)], ALU.is_equal, ALU.mult).then_inc(hot_ready, 1)

            for u in range(2):
                for i in range(2):
                    one_hots(u, u, i)
            with dve.Fori(1, TILES // 2) as n:
                for u in range(2):
                    for i in range(2):
                        dve.wait_ge(table_used, ONE + 4 * n + 2 * u + i - 3)
                        one_hots(2 * n + u, u, i)
            dve.wait_ge(table_used, ONE + 2 * TILES)
            link(dve.tensor_copy(r["token"][:], ps_tab[:, 0:BLOCKS]))


def experts(nc, started, xn_dram, y_dram, ident, ring, ring_in, parts_dram, r, w):
    with ExitStack() as ctx:
        def sb(name, shape, dt=F32):
            return ctx.enter_context(nc.sbuf_tensor(name, shape, dt))

        def psum(name):
            return ctx.enter_context(nc.psum_tensor(name, [P, 512], F32))

        sems = []

        def sem(name):
            sems.append(ctx.enter_context(nc.semaphore(name)))
            return sems[-1]

        b1 = sb("e_b1", [P, EXPERTS, FC])
        b2 = sb("e_b2", [P, EXPERTS, D])
        index = [sb(f"index{i}", [P, 1], U32) for i in range(2)]
        xg = [sb(f"xg{i}", [P, D]) for i in range(2)]
        x_hi = [sb(f"x_hi{i}", [P, KD, P], F32R) for i in range(2)]
        x_lo = [sb(f"x_lo{i}", [P, KD, P], F32R) for i in range(2)]
        pre = sb("pre", [P, F])
        hT = sb("e_hT", [P, FC, P])
        h_hi = [sb(f"e_h_hi{i}", [P, FC, P], F32R) for i in range(2)]
        h_lo = [sb(f"e_h_lo{i}", [P, FC, P], F32R) for i in range(2)]
        y = [sb(f"e_y{i}", [P, D]) for i in range(2)]
        ps_x = psum("e_ps_x")
        ps_h = [psum(f"e_ps_h{i}") for i in range(2)]
        ps_t = [psum(f"e_ps_t{i}") for i in range(2)]
        ps_y = psum("e_ps_y")
        gathered = [ctx.enter_context(nc.semaphore(f"e_gathered{i}")) for i in range(2)]
        y_stored = [ctx.enter_context(nc.semaphore(f"e_y_stored{i}")) for i in range(2)]
        index_ready, expert_ready = sem("index_ready"), sem("expert_ready")
        b_in, xt_done, x_hi_done, x_split, h_done, h_evac, ht_done, gelu_done, h_hi_done, h_split, y_done, y_evac = map(
            sem, ("eb_in", "e_xt_done", "e_x_hi_done", "e_x_split", "e_h_done", "e_h_evac", "e_ht_done",
                  "e_gelu_done", "e_h_hi_done", "e_h_split", "e_y_done", "e_y_evac"))

        start_at_one(nc, sems)
        block = ctx.enter_context(nc.Block())

        def expert_of(eng, b):
            return eng.value_load(r["expert"][0:1, ds(b, 1)], min_val=0, max_val=EXPERTS - 1)

        @block.gpsimd
        def _(pool):
            def gather(b, i):
                pool.tensor_copy(index[i][:], r["token"][:, ds(b, 1)]).then_inc(index_ready, 1)
                wait_apart(pool, started, index_ready, ONE + b + 1)
                pool.indirect_dma_start(
                    out=xg[i][:], out_offset=None, in_=xn_dram,
                    in_offset=bass.IndirectOffsetOnAxis(ap=index[i][:], axis=0),
                ).then_inc(gathered[i], 16)

            def store(b, i):
                pool.wait_ge(y_evac, ONE + b + 1)
                pool.dma_start(y_dram[ds(P * b, P), :], y[i][:]).then_inc(y_stored[i], 16)

            def gather_next(b, i):
                pool.wait_ge(xt_done, ONE + b - 1)
                gather(b, i)

            gather(0, 0)
            gather(1, 1)
            gather_next(2, 0)
            gather_next(3, 1)
            gather_next(4, 0)
            with pool.Fori(0, BLOCKS // 2 - 3) as n:
                for i in (1, 2):
                    gather_next(2 * n + i + 4, i % 2)
                    store(2 * n + i - 1, (i + 1) % 2)
            gather_next(BLOCKS - 1, 1)
            for b in range(BLOCKS - 6, BLOCKS):
                store(b, b % 2)
            for i in range(2):
                pool.wait_ge(y_stored[i], 16 * BLOCKS // 2)

        @block.sync
        def _(sp):
            sp.dma_start(b1[:], w["e_b1"]).then_inc(b_in, 16)
            sp.dma_start(b2[:], w["e_b2"].rearrange("(o e) d -> o e d", o=1).to_broadcast([P, EXPERTS, D])).then_inc(b_in, 16)
            for e in range(EXPERTS):
                if e >= RING:
                    end = sp.value_load(r["end"][0:1, e - RING:e - RING + 1], min_val=1, max_val=BLOCKS)
                    wait_apart(sp, started, y_done, ONE + end)
                    load_expert(sp, ring, ring_in, parts_dram, e)
                sp.wait_ge(ring_in[e % RING], 32 * (e // RING + 1))
                sp.sem_inc(expert_ready, 1)

        @block.tensor
        def _(pe):
            def place_of(b):
                return pe.value_load(r["ring"][0:1, ds(b, 1)], min_val=0, max_val=RING - 1)

            def weights(place, i, part, f0, cols):
                at = part * KD * F + f0
                return ring[:, ds(place, 1), i, at:at + cols].rearrange("p o f -> p (o f)")

            def turn_x(b, i, pair):
                pe.wait_ge(gathered[i], 16 * (pair + 1))
                pe.wait_ge(x_split, ONE + b)
                for k in range(KD):
                    last = pe.transpose(ps_x[:, P * k:P * k + P], xg[i][:, P * k:P * k + P], ident)
                last.then_inc(xt_done, 1)

            def hidden(b, i):
                place = place_of(b)
                pe.wait_ge(x_split, ONE + b + 1)
                pe.wait_ge(h_evac, ONE + 2 * b)
                for f in range(2):
                    for k in range(KD):
                        for n, (x, part) in enumerate([(x_hi, 0), (x_lo, 0), (x_hi, 1)]):
                            last = pe.matmul(ps_h[f][:], x[i][:, k, :], weights(place, 0, part, F * k + 512 * f, 512),
                                             start=(k == 0 and n == 0), stop=(k == KD - 1 and n == 2))
                last.then_inc(h_done, 1)

            def turn_h(b):
                pe.wait_ge(h_evac, ONE + 2 * (b + 1))
                pe.wait_ge(gelu_done, ONE + FC * b)
                for c in range(FC):
                    last = pe.transpose(ps_t[c // 4][:, P * (c % 4):P * (c % 4) + P], pre[:, P * c:P * c + P], ident)
                last.then_inc(ht_done, 1)

            def output(b, i):
                place = place_of(b)
                pe.wait_ge(h_split, ONE + b + 1)
                pe.wait_ge(y_evac, ONE + b)
                for c in range(FC):
                    for n, (h, part) in enumerate([(h_hi, 0), (h_lo, 0), (h_hi, 1)]):
                        last = pe.matmul(ps_y[:, 0:D], h[i][:, c, :], weights(place, 1, part, D * c, D),
                                         start=(c == 0 and n == 0), stop=(c == FC - 1 and n == 2))
                last.then_inc(y_done, 1)

            turn_x(0, 0, 0)
            hidden(0, 0)
            turn_x(1, 1, 0)
            hidden(1, 1)
            turn_x(2, 0, 1)
            turn_h(0)
            with pe.Fori(0, BLOCKS // 2 - 2) as n:
                for i in (1, 2):
                    b = 2 * n + i
                    hidden(b + 1, (i + 1) % 2)
                    turn_x(b + 2, i % 2, n + 1 + i // 2)
                    turn_h(b)
                    output(b - 1, (i + 1) % 2)
            b = BLOCKS - 3
            hidden(b + 1, 0)
            turn_x(b + 2, 1, BLOCKS // 2 - 1)
            turn_h(b)
            output(b - 1, 0)
            hidden(b + 2, 1)
            turn_h(b + 1)
            output(b, 1)
            turn_h(b + 2)
            output(b + 1, 0)
            output(b + 2, 1)

        @block.vector
        def _(dve):
            def x_rest(b, i):
                dve.wait_ge(x_hi_done, ONE + b + 1)
                dve.tensor_tensor(x_lo[i][:].rearrange("p k t -> p (k t)"), ps_x[:, 0:KD * P],
                                  x_hi[i][:].rearrange("p k t -> p (k t)").bitcast(F32), ALU.subtract).then_inc(x_split, 1)

            def hidden_out(b):
                dve.wait_ge(h_done, ONE + b + 1)
                dve.wait_ge(ht_done, ONE + b)
                for f in range(2):
                    dve.tensor_copy(pre[:, 512 * f:512 * f + 512], ps_h[f][:]).then_inc(h_evac, 1)

            def h_rest(b, i):
                dve.wait_ge(h_hi_done, ONE + b + 1)
                dve.tensor_tensor(h_lo[i][:], hT[:], h_hi[i][:].bitcast(F32), ALU.subtract).then_inc(h_split, 1)

            def output_out(b, i, pair):
                e = expert_of(dve, b)
                dve.wait_ge(y_done, ONE + b + 1)
                if not isinstance(pair, int) or pair:
                    wait_apart(dve, started, y_stored[i], 16 * pair)
                dve.tensor_tensor(y[i][:], ps_y[:, 0:D], b2[:, ds(e, 1), :].rearrange("p o d -> p (o d)"), ALU.add)\
                   .then_inc(y_evac, 1)

            dve.wait_ge(b_in, ONE + 32)
            x_rest(0, 0)
            hidden_out(0)
            x_rest(1, 1)
            x_rest(2, 0)
            hidden_out(1)
            h_rest(0, 0)

            def slots(n):
                for i in (1, 2):
                    b = 2 * n + i
                    x_rest(b + 2, i % 2)
                    hidden_out(b + 1)
                    h_rest(b, i % 2)
                    output_out(b - 1, (i + 1) % 2, n)

            slots(0)
            with dve.Fori(1, BLOCKS // 2 - 2) as n:
                slots(n)
            b = BLOCKS - 3
            x_rest(b + 2, 1)
            hidden_out(b + 1)
            h_rest(b, 1)
            output_out(b - 1, 0, BLOCKS // 2 - 2)
            hidden_out(b + 2)
            h_rest(b + 1, 0)
            output_out(b, 1, BLOCKS // 2 - 2)
            h_rest(b + 2, 1)
            output_out(b + 1, 0, BLOCKS // 2 - 1)
            output_out(b + 2, 1, BLOCKS // 2 - 1)

        @block.scalar
        def _(act):
            def x_out(b, i):
                e = expert_of(act, b)
                wait_apart(act, started, expert_ready, ONE + e + 1)
                act.wait_ge(xt_done, ONE + b + 1)
                act.activation(x_hi[i][:].rearrange("p k t -> p (k t)"), ps_x[:, 0:KD * P], ACT.Copy).then_inc(x_hi_done, 1)

            def gelu(b, i):
                e = expert_of(act, b)
                wait_apart(act, started, ht_done, ONE + b + 1)
                wait_apart(act, started, h_split, ONE + b)
                for c in range(FC):
                    act.activation(hT[:, c, :], ps_t[c // 4][:, P * (c % 4):P * (c % 4) + P], ACT.Gelu,
                                   bias=b1[:, ds(e, 1), c]).then_inc(gelu_done, 1)
                act.wait_ge(gelu_done, ONE + FC * (b + 1))
                act.activation(h_hi[i][:], hT[:], ACT.Copy).then_inc(h_hi_done, 1)

            act.wait_ge(b_in, ONE + 32)
            x_out(0, 0)
            x_out(1, 1)
            act.wait_ge(h_done, ONE + 1)
            x_out(2, 0)
            gelu(0, 0)
            with act.Fori(0, BLOCKS // 2 - 2) as n:
                for i in (1, 2):
                    b = 2 * n + i
                    act.wait_ge(h_done, ONE + b + 1)
                    x_out(b + 2, i % 2)
                    gelu(b, i % 2)
            b = BLOCKS - 3
            act.wait_ge(h_done, ONE + b + 1)
            x_out(b + 2, 1)
            gelu(b, 1)
            gelu(b + 1, 0)
            gelu(b + 2, 1)


def combine(nc, started, x_res, y_dram, out, r):
    with ExitStack() as ctx:
        SLOTS = 4
        rows = [[ctx.enter_context(nc.sbuf_tensor(f"rows{i}_{s}", [P, D], F32)) for s in range(SLOTS)] for i in range(2)]
        result = [ctx.enter_context(nc.sbuf_tensor(f"result{s}", [P, D], F32)) for s in range(SLOTS)]
        half = [ctx.enter_context(nc.sbuf_tensor(f"half{s}", [P, D], F32)) for s in range(SLOTS)]
        index = [[ctx.enter_context(nc.sbuf_tensor(f"slot{i}_{s}", [P, 1], U32)) for s in range(SLOTS)] for i in range(2)]
        fetched = [ctx.enter_context(nc.semaphore(f"rows_in{s}")) for s in range(SLOTS)]
        stored = [ctx.enter_context(nc.semaphore(f"out_stored{s}")) for s in range(SLOTS)]
        index_ready, first_done, done = [ctx.enter_context(nc.semaphore(n)) for n in
                                         ("slots_ready", "first_added", "result_done")]
        sems = [*stored, index_ready, first_done, done]
        start_at_one(nc, sems)
        block = ctx.enter_context(nc.Block())

        @block.gpsimd
        def _(pool):
            def fetch(t, s):
                wait_apart(pool, started, index_ready, ONE + 2 * (t + 1))
                for i in range(2):
                    pool.indirect_dma_start(
                        out=rows[i][s][:], out_offset=None, in_=y_dram,
                        in_offset=bass.IndirectOffsetOnAxis(ap=index[i][s][:], axis=0),
                    ).then_inc(fetched[s], 16)

            for s in range(SLOTS):
                fetch(s, s)
            with pool.Fori(1, TILES // SLOTS) as n:
                for s in range(SLOTS):
                    wait_apart(pool, started, done, ONE + SLOTS * n + s - SLOTS + 1)
                    fetch(SLOTS * n + s, s)

        @block.vector
        def _(dve):
            def indices(t, s):
                for i in range(2):
                    dve.tensor_copy(index[i][s][:], r["slot"][i][:, ds(t, 1)]).then_inc(index_ready, 1)

            def add(t, s, turn):
                dve.wait_ge(fetched[s], 32 * (turn + 1))
                x = x_res[:, ds(t, 1), :].rearrange("p o d -> p (o d)")
                dve.scalar_tensor_tensor(out=half[s][:], in0=rows[0][s][:], scalar=r["weight"][0][:, ds(t, 1)],
                                         in1=x, op0=ALU.mult, op1=ALU.add).then_inc(first_done, 1)
                dve.wait_ge(first_done, ONE + t + 1)
                dve.scalar_tensor_tensor(out=result[s][:], in0=rows[1][s][:], scalar=r["weight"][1][:, ds(t, 1)],
                                         in1=half[s][:], op0=ALU.mult, op1=ALU.add).then_inc(done, 1)

            for s in range(SLOTS):
                indices(s, s)
            for s in range(SLOTS):
                add(s, s, 0)
                indices(SLOTS + s, s)
            with dve.Fori(1, TILES // SLOTS - 1) as n:
                for s in range(SLOTS):
                    dve.wait_ge(stored[s], ONE + 16 * n)
                    add(SLOTS * n + s, s, n)
                    indices(SLOTS * (n + 1) + s, s)
            for s in range(SLOTS):
                n = TILES // SLOTS - 1
                dve.wait_ge(stored[s], ONE + 16 * n)
                add(SLOTS * n + s, s, n)

        @block.sync
        def _(sp):
            with sp.Fori(0, TILES // SLOTS) as n:
                for s in range(SLOTS):
                    sp.wait_ge(done, ONE + SLOTS * n + s + 1)
                    sp.dma_start(out[ds(P * (SLOTS * n + s), P), :], result[s][:]).then_inc(stored[s], 16)
            for s in range(SLOTS):
                sp.wait_ge(stored[s], ONE + 16 * TILES // SLOTS)


def build(nc, w, out):
    with ExitStack() as ctx:
        def sb(name, shape, dt=F32):
            return ctx.enter_context(nc.sbuf_tensor(name, shape, dt))

        x_res = sb("x_res", [P, TILES, D])
        ident = sb("ident", [P, P])
        neg_half = sb("neg_half", [P, 8])
        r = {"token": sb("slot_token", [P, BLOCKS], U32), "expert": sb("block_expert", [P, BLOCKS], I32),
             "ring": sb("block_ring", [P, BLOCKS], I32), "end": sb("expert_end", [P, EXPERTS], I32),
             "slot": [sb(f"token_slot{i}", [P, TILES], U32) for i in range(2)],
             "weight": [sb(f"token_weight{i}", [P, TILES]) for i in range(2)]}
        xn_dram = nc.dram_tensor("xn_dram", [N, D], F32, kind="Internal").ap()
        parts_dram = nc.dram_tensor("parts_dram", [EXPERTS, 2, P, 2, KD * F], F32, kind="Internal").ap()
        y_dram = nc.dram_tensor("y_dram", [P * BLOCKS, D], F32, kind="Internal").ap()
        const = ctx.enter_context(nc.semaphore("const"))
        started = ctx.enter_context(nc.semaphore("started"))
        ring_in = [ctx.enter_context(nc.semaphore(f"ring_in{i}")) for i in range(RING)]
        w_qkv, w_out = sb("w_qkv", [P, KD, 3 * D]), sb("w_out", [P, KD, D])
        attn_w_in = ctx.enter_context(nc.semaphore("attn_w_in"))
        with nc.Block() as block:
            @block.gpsimd
            def _(pool):
                pool.memset(neg_half[:], -0.5).then_inc(const, 1)
                pool.memset(ident[:], 0.0).then_inc(const, 1)
                pool.wait_ge(const, 2)
                pool.affine_select(out=ident[:], in_=ident[:], compare_op=ALU.not_equal, fill=1.0, base=0,
                                   pattern=[[-1, P]], channel_multiplier=1).then_inc(const, 1)
                pool.wait_ge(const, 3)
                pool.memset(neg_half[:], -0.5).then_inc(started, 1)
                pool.wait_ge(started, 1)
        tower(nc, started, x_res, ident[:], neg_half, w_qkv, w_out, attn_w_in, w)
        attention(nc, started, x_res, ident[:], neg_half, w_qkv, w_out, attn_w_in, parts_dram, w)
        ring = sb("ring", [P, RING, 2, 2 * KD * F], F32R)
        route(nc, started, x_res, xn_dram, ident[:], neg_half, ring, ring_in, parts_dram, w, r)
        experts(nc, started, xn_dram, y_dram, ident[:], ring, ring_in, parts_dram, r, w)
        combine(nc, started, x_res, y_dram, out, r)


def lay_out(inputs):
    import numpy as np

    a = {k.removeprefix("L0_tok_"): v for k, v in inputs.items() if k.startswith("L0_tok_")}
    a["tokens"] = np.asarray(inputs["x"]).reshape(TILES, P).T
    f = {k.removeprefix("L0_ffn_"): np.asarray(v) for k, v in inputs.items() if k.startswith("L0_ffn_")}
    a["routerT"] = np.concatenate([f["router_w"], f["lang_w"]]).T
    a["router_b"], a["lang_b"] = f["router_b"], f["lang_b"]
    a["e_w1"], a["e_w2"], a["e_b2"] = f["w1"], f["w2"], f["b2"]
    a["e_b1"] = f["b1"].reshape(EXPERTS, FC, P).transpose(2, 0, 1)
    a["w_qkvT"] = np.asarray(inputs["L0_attn_w_qkv"]).T
    a["w_outT"] = np.asarray(inputs["L0_attn_w_out"]).T
    a["A_diag"] = np.concatenate([a["A_diag"].T] * 2)
    a["b1"] = np.asarray(a["b1"]).reshape(LAYERS, FC, P).transpose(2, 0, 1)
    a["ln_par"] = np.stack([np.asarray(a.pop(n)).reshape(LAYERS, KD, P).transpose(2, 0, 1)
                            for n in ("ln1_s", "ln1_b", "ln2_s", "ln2_b")], axis=1)
    return {k: np.ascontiguousarray(v) for k, v in a.items()}


def kernel(**inputs):
    import concourse.bacc as bacc
    from concourse.bass_utils import run_bass_kernel_spmd

    nc = bacc.Bacc("TRN2", target_bir_lowering=False, num_devices=1)
    arrays = {f"in_{k}": v for k, v in lay_out(inputs).items()}
    w = {k.removeprefix("in_"): nc.dram_tensor(k, v.shape, mybir.dt.from_np(v.dtype), kind="ExternalInput").ap()
         for k, v in arrays.items()}
    out = nc.dram_tensor("out", (N, D), F32, kind="ExternalOutput").ap()
    build(nc, w, out)
    r = run_bass_kernel_spmd(nc, [arrays], core_ids=[0])
    return r.results[0]["out"].reshape(SEQS, T, D)
```
